# Optimizing a Trainium2 kernel written in Bass

```python
import numpy as np
import jax
import jax.numpy as jnp

def _softmax(x, axis=-1):
    return jax.nn.softmax(x, axis=axis)

def _gelu(x):
    return jax.nn.gelu(x, approximate=True)

def _silu(x):
    return jax.nn.silu(x)

def _sigmoid(x):
    return jax.nn.sigmoid(x)

def _layernorm(x, axis=-1, eps=1e-05):
    m = jnp.mean(x, axis=axis, keepdims=True)
    v = jnp.var(x, axis=axis, keepdims=True)
    return (x - m) / jnp.sqrt(v + eps)

def _scatter_add(tgt, idx, src, axis=0):
    return tgt.at[idx].add(src)

def _segment_sum(src, seg, n):
    return jax.ops.segment_sum(src, seg, n)
kernel_name = 'mk_hybrid_d1_jaxref_r4_18c4ee'

def setup_inputs(seed: int=0):
    np.random.seed(seed)
    _w = jnp.asarray

    def _L0_attn_a_setup():
        import jax, jax.numpy as jnp
        import numpy as np
        D_MODEL = 256
        NUM_HEADS = 16
        D_K = D_MODEL // NUM_HEADS
        ROPE_BASE = 10000.0

        def _rope_cos_sin(seq_len, d_k):
            inv_freq = 1.0 / ROPE_BASE ** (jnp.arange(0, d_k, 2, dtype=jnp.float32) / d_k)
            t = jnp.arange(seq_len, dtype=jnp.float32)
            freqs = t[:, None] * inv_freq[None, :]
            emb = jnp.concatenate([freqs, freqs], axis=-1)
            return (jnp.cos(emb)[None, None], jnp.sin(emb)[None, None])

        def _apply_rope(q, k, cos, sin):
            q1, q2 = (q[..., ::2], q[..., 1::2])
            k1, k2 = (k[..., ::2], k[..., 1::2])
            q_rot = jnp.concatenate([-q2, q1], axis=-1)
            k_rot = jnp.concatenate([-k2, k1], axis=-1)
            return (q * cos + q_rot * sin, k * cos + k_rot * sin)
        key = jax.random.key(seed)
        ks = jax.random.split(key, 5)
        B, S = (2, 512)
        x = jax.random.normal(ks[0], (B, S, D_MODEL), dtype=jnp.float32)
        scale = 1.0 / np.sqrt(D_MODEL)
        Wq = jax.random.normal(ks[1], (D_MODEL, D_MODEL), dtype=jnp.float32) * scale
        Wk = jax.random.normal(ks[2], (D_MODEL, D_MODEL), dtype=jnp.float32) * scale
        Wv = jax.random.normal(ks[3], (D_MODEL, D_MODEL), dtype=jnp.float32) * scale
        Wo = jax.random.normal(ks[4], (D_MODEL, D_MODEL), dtype=jnp.float32) * scale
        return {'x': x, 'Wq': Wq, 'Wk': Wk, 'Wv': Wv, 'Wo': Wo}
    _L0_attn_a_in = _L0_attn_a_setup()

    def _L0_attn_b_setup():
        import jax, jax.numpy as jnp
        import numpy as np
        S_LEN, BATCH, HID, HEADS = (512, 4, 256, 16)
        HD = HID // HEADS

        def _forget_attention(hidden_states, Wq, bq, Wk, bk, Wv, bv, Wf, bf, Wo, bo):
            S, B, H = hidden_states.shape
            nh, hd = (HEADS, HD)

            def shape(x):
                return x.reshape(S, B, nh, hd)
            q = shape(hidden_states @ Wq.T + bq)
            k = shape(hidden_states @ Wk.T + bk)
            v = shape(hidden_states @ Wv.T + bv)
            phi_q = jax.nn.elu(q) + 1.0
            phi_k = jax.nn.elu(k) + 1.0
            f = jax.nn.sigmoid(hidden_states @ Wf.T + bf)

            def step(carry, xs):
                Sm, z = carry
                ft, pk, pq, vt = xs
                fte = ft[..., None]
                Sm = fte[..., None] * Sm + pk[..., :, None] * vt[..., None, :]
                z = fte * z + pk
                num = jnp.einsum('bhd,bhde->bhe', pq, Sm)
                den = jnp.einsum('bhd,bhd->bh', pq, z)[..., None]
                return ((Sm, z), num / (den + 1e-06))
            init = (jnp.zeros((B, nh, hd, hd), hidden_states.dtype), jnp.zeros((B, nh, hd), hidden_states.dtype))
            _, out = jax.lax.scan(step, init, (f, phi_k, phi_q, v))
            out = out.reshape(S, B, H) @ Wo.T + bo
            return (out, f)

        def _reference_tuple_inner(hidden_states, Wq, bq, Wk, bk, Wv, bv, Wf, bf, Wo, bo):
            out, f = _forget_attention(hidden_states, Wq, bq, Wk, bk, Wv, bv, Wf, bf, Wo, bo)
            return (out, jnp.zeros_like(out), f)
        key = jax.random.key(seed)
        ks = jax.random.split(key, 6)

        def lin_w(k, out_dim, in_dim):
            return jax.random.normal(k, (out_dim, in_dim), jnp.float32) * (1.0 / np.sqrt(in_dim))
        return {'hidden_states': jax.random.normal(ks[0], (S_LEN, BATCH, HID), jnp.float32), 'Wq': lin_w(ks[1], HID, HID), 'bq': jnp.zeros((HID,), jnp.float32), 'Wk': lin_w(ks[2], HID, HID), 'bk': jnp.zeros((HID,), jnp.float32), 'Wv': lin_w(ks[3], HID, HID), 'bv': jnp.zeros((HID,), jnp.float32), 'Wf': lin_w(ks[4], HEADS, HID), 'bf': jnp.zeros((HEADS,), jnp.float32), 'Wo': lin_w(ks[5], HID, HID), 'bo': jnp.zeros((HID,), jnp.float32)}
    _L0_attn_b_in = _L0_attn_b_setup()

    def _L0_ffn_setup():
        import jax, jax.numpy as jnp
        import numpy as np
        B, S, D = (1, 512, 256)
        E, K, F = (64, 8, 192)
        SF = 192
        C = 128
        ROUTED_SCALE = 1.0

        def _moe_forward(x, router_w, w_gate, w_up, w_down, ws_gate_up, ws_down):
            T = x.shape[0]
            logits = x.astype(jnp.float32) @ router_w.T
            probs = jax.nn.softmax(logits, axis=-1)
            topk_w, topk_ids = jax.lax.top_k(probs, K)
            topk_w = topk_w / jnp.sum(topk_w, axis=-1, keepdims=True)
            topk_w = topk_w.astype(x.dtype)
            N = T * K
            flat_e = topk_ids.reshape(-1)
            flat_w = topk_w.reshape(-1)
            tok = jnp.arange(N) // K
            onehot = flat_e[:, None] == jnp.arange(E)[None, :]
            pos = jnp.cumsum(onehot, axis=0)[jnp.arange(N), flat_e] - 1
            valid = pos < C
            idx = jnp.where(valid, flat_e * C + pos, E * C)
            x_buf = jnp.zeros((E * C + 1, x.shape[1]), x.dtype).at[idx].set(x[tok])
            xb = x_buf[:E * C].reshape(E, C, -1)
            g = jnp.einsum('ecd,edf->ecf', xb, w_gate)
            u = jnp.einsum('ecd,edf->ecf', xb, w_up)
            h = jax.nn.silu(g) * u
            y = jnp.einsum('ecf,efd->ecd', h, w_down).reshape(E * C, -1)
            safe = jnp.where(valid, idx, 0)
            contrib = y[safe] * (flat_w * valid.astype(flat_w.dtype))[:, None]
            routed = jax.ops.segment_sum(contrib, tok, num_segments=T)
            routed = routed * ROUTED_SCALE
            gu = x @ ws_gate_up
            sg, su = (gu[:, :SF], gu[:, SF:])
            shared = jax.nn.silu(sg) * su @ ws_down
            return routed + shared
        key = jax.random.key(seed)
        ks = jax.random.split(key, 7)
        w = 0.02
        return {'hidden_states': jax.random.normal(ks[0], (B, S, D), jnp.float32), 'router_w': jax.random.normal(ks[1], (E, D), jnp.float32) * w, 'w_gate': jax.random.normal(ks[2], (E, D, F), jnp.float32) * w, 'w_up': jax.random.normal(ks[3], (E, D, F), jnp.float32) * w, 'w_down': jax.random.normal(ks[4], (E, F, D), jnp.float32) * w, 'ws_gate_up': jax.random.normal(ks[5], (D, 2 * SF), jnp.float32) * w, 'ws_down': jax.random.normal(ks[6], (SF, D), jnp.float32) * w}
    _L0_ffn_in = _L0_ffn_setup()
    _d = {'L0_attn_a_x': _L0_attn_a_in['x'], 'L0_attn_a_Wq': _L0_attn_a_in['Wq'], 'L0_attn_a_Wk': _L0_attn_a_in['Wk'], 'L0_attn_a_Wv': _L0_attn_a_in['Wv'], 'L0_attn_a_Wo': _L0_attn_a_in['Wo'], 'L0_attn_b_Wq': _L0_attn_b_in['Wq'], 'L0_attn_b_bq': _L0_attn_b_in['bq'], 'L0_attn_b_Wk': _L0_attn_b_in['Wk'], 'L0_attn_b_bk': _L0_attn_b_in['bk'], 'L0_attn_b_Wv': _L0_attn_b_in['Wv'], 'L0_attn_b_bv': _L0_attn_b_in['bv'], 'L0_attn_b_Wf': _L0_attn_b_in['Wf'], 'L0_attn_b_bf': _L0_attn_b_in['bf'], 'L0_attn_b_Wo': _L0_attn_b_in['Wo'], 'L0_attn_b_bo': _L0_attn_b_in['bo'], 'L0_ffn_router_w': _L0_ffn_in['router_w'], 'L0_ffn_w_gate': _L0_ffn_in['w_gate'], 'L0_ffn_w_up': _L0_ffn_in['w_up'], 'L0_ffn_w_down': _L0_ffn_in['w_down'], 'L0_ffn_ws_gate_up': _L0_ffn_in['ws_gate_up'], 'L0_ffn_ws_down': _L0_ffn_in['ws_down']}
    _x0 = _d['L0_attn_a_x']
    _d['L0_attn_a_x'] = jax.random.normal(jax.random.fold_in(jax.random.key(seed), 1), (16, 512, 256), dtype=_x0.dtype)
    del _x0
    return _d

def reference(L0_attn_a_x, L0_attn_a_Wq, L0_attn_a_Wk, L0_attn_a_Wv, L0_attn_a_Wo, L0_attn_b_Wq, L0_attn_b_bq, L0_attn_b_Wk, L0_attn_b_bk, L0_attn_b_Wv, L0_attn_b_bv, L0_attn_b_Wf, L0_attn_b_bf, L0_attn_b_Wo, L0_attn_b_bo, L0_ffn_router_w, L0_ffn_w_gate, L0_ffn_w_up, L0_ffn_w_down, L0_ffn_ws_gate_up, L0_ffn_ws_down):

    def _L0_attn_a_ref(x, Wq, Wk, Wv, Wo):
        import jax, jax.numpy as jnp
        import numpy as np
        D_MODEL = 256
        NUM_HEADS = 16
        D_K = D_MODEL // NUM_HEADS
        ROPE_BASE = 10000.0

        def _rope_cos_sin(seq_len, d_k):
            inv_freq = 1.0 / ROPE_BASE ** (jnp.arange(0, d_k, 2, dtype=jnp.float32) / d_k)
            t = jnp.arange(seq_len, dtype=jnp.float32)
            freqs = t[:, None] * inv_freq[None, :]
            emb = jnp.concatenate([freqs, freqs], axis=-1)
            return (jnp.cos(emb)[None, None], jnp.sin(emb)[None, None])

        def _apply_rope(q, k, cos, sin):
            q1, q2 = (q[..., ::2], q[..., 1::2])
            k1, k2 = (k[..., ::2], k[..., 1::2])
            q_rot = jnp.concatenate([-q2, q1], axis=-1)
            k_rot = jnp.concatenate([-k2, k1], axis=-1)
            return (q * cos + q_rot * sin, k * cos + k_rot * sin)
        B, S, D = x.shape
        H, dk = (NUM_HEADS, D_K)

        def proj(W):
            return (x @ W.T).reshape(B, S, H, dk).transpose(0, 2, 1, 3)
        q, k, v = (proj(Wq), proj(Wk), proj(Wv))
        cos, sin = _rope_cos_sin(S, dk)
        q, k = _apply_rope(q, k, cos, sin)
        scores = jnp.einsum('bhqd,bhkd->bhqk', q, k) / jnp.sqrt(jnp.float32(dk))
        attn = jax.nn.softmax(scores, axis=-1)
        out = jnp.einsum('bhqk,bhkd->bhqd', attn, v)
        out = out.transpose(0, 2, 1, 3).reshape(B, S, D)
        return out @ Wo.T

    def _L0_attn_b_ref(hidden_states, Wq, bq, Wk, bk, Wv, bv, Wf, bf, Wo, bo):
        import jax, jax.numpy as jnp
        import numpy as np
        S_LEN, BATCH, HID, HEADS = (512, 4, 256, 16)
        HD = HID // HEADS

        def _forget_attention(hidden_states, Wq, bq, Wk, bk, Wv, bv, Wf, bf, Wo, bo):
            S, B, H = hidden_states.shape
            nh, hd = (HEADS, HD)

            def shape(x):
                return x.reshape(S, B, nh, hd)
            q = shape(hidden_states @ Wq.T + bq)
            k = shape(hidden_states @ Wk.T + bk)
            v = shape(hidden_states @ Wv.T + bv)
            phi_q = jax.nn.elu(q) + 1.0
            phi_k = jax.nn.elu(k) + 1.0
            f = jax.nn.sigmoid(hidden_states @ Wf.T + bf)

            def step(carry, xs):
                Sm, z = carry
                ft, pk, pq, vt = xs
                fte = ft[..., None]
                Sm = fte[..., None] * Sm + pk[..., :, None] * vt[..., None, :]
                z = fte * z + pk
                num = jnp.einsum('bhd,bhde->bhe', pq, Sm)
                den = jnp.einsum('bhd,bhd->bh', pq, z)[..., None]
                return ((Sm, z), num / (den + 1e-06))
            init = (jnp.zeros((B, nh, hd, hd), hidden_states.dtype), jnp.zeros((B, nh, hd), hidden_states.dtype))
            _, out = jax.lax.scan(step, init, (f, phi_k, phi_q, v))
            out = out.reshape(S, B, H) @ Wo.T + bo
            return (out, f)

        def _reference_tuple_inner(hidden_states, Wq, bq, Wk, bk, Wv, bv, Wf, bf, Wo, bo):
            out, f = _forget_attention(hidden_states, Wq, bq, Wk, bk, Wv, bv, Wf, bf, Wo, bo)
            return (out, jnp.zeros_like(out), f)
        return _reference_tuple_inner(hidden_states, Wq, bq, Wk, bk, Wv, bv, Wf, bf, Wo, bo)[0]

    def _L0_ffn_ref(hidden_states, router_w, w_gate, w_up, w_down, ws_gate_up, ws_down):
        import jax, jax.numpy as jnp
        import numpy as np
        B, S, D = (1, 512, 256)
        E, K, F = (64, 8, 192)
        SF = 192
        C = 128
        ROUTED_SCALE = 1.0

        def _moe_forward(x, router_w, w_gate, w_up, w_down, ws_gate_up, ws_down):
            T = x.shape[0]
            logits = x.astype(jnp.float32) @ router_w.T
            probs = jax.nn.softmax(logits, axis=-1)
            topk_w, topk_ids = jax.lax.top_k(probs, K)
            topk_w = topk_w / jnp.sum(topk_w, axis=-1, keepdims=True)
            topk_w = topk_w.astype(x.dtype)
            N = T * K
            flat_e = topk_ids.reshape(-1)
            flat_w = topk_w.reshape(-1)
            tok = jnp.arange(N) // K
            onehot = flat_e[:, None] == jnp.arange(E)[None, :]
            pos = jnp.cumsum(onehot, axis=0)[jnp.arange(N), flat_e] - 1
            valid = pos < C
            idx = jnp.where(valid, flat_e * C + pos, E * C)
            x_buf = jnp.zeros((E * C + 1, x.shape[1]), x.dtype).at[idx].set(x[tok])
            xb = x_buf[:E * C].reshape(E, C, -1)
            g = jnp.einsum('ecd,edf->ecf', xb, w_gate)
            u = jnp.einsum('ecd,edf->ecf', xb, w_up)
            h = jax.nn.silu(g) * u
            y = jnp.einsum('ecf,efd->ecd', h, w_down).reshape(E * C, -1)
            safe = jnp.where(valid, idx, 0)
            contrib = y[safe] * (flat_w * valid.astype(flat_w.dtype))[:, None]
            routed = jax.ops.segment_sum(contrib, tok, num_segments=T)
            routed = routed * ROUTED_SCALE
            gu = x @ ws_gate_up
            sg, su = (gu[:, :SF], gu[:, SF:])
            shared = jax.nn.silu(sg) * su @ ws_down
            return routed + shared
        b, s, d = hidden_states.shape
        x = hidden_states.reshape(-1, d)
        out = _moe_forward(x, router_w, w_gate, w_up, w_down, ws_gate_up, ws_down)
        return out.reshape(b, s, d)
    x = L0_attn_a_x
    x = x + _L0_attn_a_ref(_layernorm(x, axis=-1), L0_attn_a_Wq, L0_attn_a_Wk, L0_attn_a_Wv, L0_attn_a_Wo)
    x = x + _L0_ffn_ref(_layernorm(x, axis=-1), L0_ffn_router_w, L0_ffn_w_gate, L0_ffn_w_up, L0_ffn_w_down, L0_ffn_ws_gate_up, L0_ffn_ws_down)
    x = x + _L0_attn_b_ref(_layernorm(x, axis=-1), L0_attn_b_Wq, L0_attn_b_bq, L0_attn_b_Wk, L0_attn_b_bk, L0_attn_b_Wv, L0_attn_b_bv, L0_attn_b_Wf, L0_attn_b_bf, L0_attn_b_Wo, L0_attn_b_bo)
    x = x + _L0_ffn_ref(_layernorm(x, axis=-1), L0_ffn_router_w, L0_ffn_w_gate, L0_ffn_w_up, L0_ffn_w_down, L0_ffn_ws_gate_up, L0_ffn_ws_down)
    return x

_drawn_inputs = setup_inputs


def setup_inputs(seed=0):
    import zlib

    import numpy as np

    out = dict(_drawn_inputs(seed))
    spreads = {'L0_attn_b_bq': (0.0, 2.0),
     'L0_attn_b_bk': (0.0, 2.0),
     'L0_attn_b_bv': (0.0, 0.1),
     'L0_attn_b_bf': (0.0, 0.472),
     'L0_attn_b_bo': (0.0, 0.1)}
    factors = {'L0_ffn_router_w': 8.0, 'L0_ffn_w_gate': 8.0, 'L0_ffn_w_up': 8.0, 'L0_ffn_w_down': 8.0}
    for name, (base, spread) in spreads.items():
        noise = np.random.default_rng([zlib.crc32(name.encode()), seed]).standard_normal(out[name].shape)
        drawn = base * np.exp(spread * noise) if base else spread * noise
        out[name] = jnp.asarray(drawn.astype(out[name].dtype))
    for name, factor in factors.items():
        out[name] = (out[name] * factor).astype(out[name].dtype)
    return out
```

```python
import numpy as np


def wait(eng, sem, value):
    if not isinstance(value, int) or value > 0:
        eng.wait_ge(sem, value)


def passed_by(eng, passed):
    eng.sem_inc(passed, 1)


def walk(eng, total, trip, look_back, stages):
    deepest = max(lag for lag, _ in stages)
    lead = trip * -(-(deepest + look_back) // trip)

    def step(s, k, peeled):
        for lag, stage in stages:
            if not peeled or 0 <= s - lag < total:
                stage(s - lag, (k - lag) % trip)

    for s in range(lead):
        step(s, s % trip, True)
    with eng.Fori(lead // trip, total // trip) as i:
        for k in range(trip):
            step(i * trip + k, k, False)
    for s in range(total, total + deepest):
        step(s, s % trip, True)


def turns(n, k, trip):
    return n // trip if isinstance(n, int) else (n - k) // trip


def attention_project(nc, dram, x_in, wq, wk, wv, const):
    import concourse.bass as bass
    from concourse import mybir
    from contextlib import ExitStack
    fp32, bf16 = mybir.dt.float32, mybir.dt.bfloat16
    ALU, ACT = mybir.AluOpType, mybir.ActivationFunctionType
    P, D, H, DK = 128, 256, 16, 16
    TPB = 4
    SEQS = 16
    TILES = SEQS * TPB
    HALF = DK // 2

    with ExitStack() as ctx:
        def sb(name, shape, dt=fp32):
            return ctx.enter_context(nc.sbuf_tensor("a1_" + name, shape, dt))

        def pb(name, shape, dt=fp32):
            return ctx.enter_context(nc.psum_tensor("a1_" + name, shape, dt))

        def sem(name):
            return nc.alloc_semaphore("a1_" + name)

        w_rows = sb("w_rows", [P, 6, D])
        w_qk = sb("w_qk", [P, 2, 2 * D])
        w_v = sb("w_v", [P, 2, D])
        ident = sb("ident", [P, P])
        cos = sb("cos", [P, TPB, DK])
        sin = sb("sin", [P, TPB, DK])
        minus_half = sb("minus_half", [P, 1])
        eps = sb("eps", [P, 1])
        xt = sb("xt", [P, TPB, D])
        stats = sb("stats", [P, 2, 6])
        mean_var = sb("mean_var", [P, TPB, 2])
        var_eps = sb("var_eps", [P, 2, 1])
        rstd = sb("rstd", [P, TPB, 1])
        xn = sb("xn", [P, TPB, D])
        xnT = sb("xnT", [P, 2, 2, P])
        rot_cos = sb("rot_cos", [P, 2, 2 * D])
        rot_sin = sb("rot_sin", [P, 2, 2 * D])
        qk = sb("qk", [P, 2, 2 * D])
        v_aug = sb("v_aug", [P, 2, H, 2 * DK])
        rest = sb("rest", [P, 2, 2 * D])
        parts = sb("parts", [P, TPB, 3, 4, P], bf16)
        ps_x = pb("ps_x", [P, 2, P])
        ps_qk = [pb(f"ps_qk{u}", [P, 2 * D]) for u in range(2)]
        ps_v = [pb(f"ps_v{u}", [P, D]) for u in range(2)]
        ps_t = [pb(f"ps_t{u}", [P, 4, P]) for u in range(2)]

        const_in, w_turned, w_copied, setup = sem("const_in"), sem("w_turned"), sem("w_copied"), sem("setup")
        x_loaded = [sem(f"x_loaded{u}") for u in range(TPB)]
        stats_done, mv_done, ve_done, rstd_done, xn_done = (sem(n) for n in ("stats_done", "mv_done", "ve_done", "rstd_done", "xn_done"))
        x_turned, xnT_done, qk_projected, v_projected, v_copied = (sem(n) for n in ("x_turned", "xnT_done", "qk_projected", "v_projected", "v_copied"))
        rot_done, qk_done, qk_turned, high_done, rest_done, mid_done, low_done = (sem(n) for n in (
            "rot_done", "qk_done", "qk_turned", "high_done", "rest_done", "mid_done", "low_done"))
        v_stored = [sem(f"v_stored{u}") for u in range(2)]
        parts_stored = [sem(f"parts_stored{u}") for u in range(TPB)]
        dve_passed = sem("dve_passed")
        block = ctx.enter_context(nc.Block())

        @block.sync
        def _(sp):
            for i, w in enumerate((wq, wk, wv)):
                sp.dma_start(w_rows[:, 2 * i:2 * i + 2, :], w.rearrange("(c p) d -> p c d", p=P)).then_inc(const_in, 16)
            sp.dma_start(ident[:], const["ident"]).then_inc(const_in, 16)
            sp.dma_start(cos[:], const["cos"]).then_inc(const_in, 16)
            sp.dma_start(sin[:], const["sin"]).then_inc(const_in, 16)

            def load(n, j):
                u = j % 2
                wait(sp, xn_done, n - 3)
                sp.dma_start(xt[:, j, :], x_in[bass.ds(n * P, P), :]).then_inc(x_loaded[j], 16)

            def store_parts(n, j):
                u = j % 2
                sp.wait_ge(low_done, n + 1)
                sp.wait_ge(mid_done, n + 1)
                sp.wait_ge(high_done, n + 1)
                sp.dma_start(dram["parts"][turns(n, j, TPB)].rearrange("(k g) p t -> p k g t", k=3)[:, :, :, j * P:(j + 1) * P],
                             parts[:, j]).then_inc(parts_stored[j], 16)

            walk(sp, TILES, TPB, TPB, [(0, load), (8, store_parts)])
            for j in range(TPB):
                sp.wait_ge(parts_stored[j], 16 * SEQS)

        @block.gpsimd
        def _(pool):
            nc.gpsimd.memset(minus_half[:], -0.5).then_inc(setup, 1)
            nc.gpsimd.memset(eps[:], 1e-5).then_inc(setup, 1)
            nc.gpsimd.memset(v_aug[:], 0.0).then_inc(setup, 1)
            pool.wait_ge(setup, 3)
            nc.gpsimd.memset(v_aug[:, :, :, DK:DK + 1], 1.0).then_inc(setup, 1)

            def inverse_deviation(n, j):
                u = j % 2
                pool.wait_ge(mv_done, n + 1)
                nc.gpsimd.tensor_tensor(var_eps[:, u], mean_var[:, j, 1:2], eps[:], ALU.add).then_inc(ve_done, 1)
                pool.wait_ge(ve_done, n + 1)
                nc.gpsimd.tensor_tensor(rstd[:, j], var_eps[:, u], minus_half[:], ALU.pow).then_inc(rstd_done, 1)

            def split(n, j):
                u = j % 2
                pool.wait_ge(mid_done, n + 1)
                nc.gpsimd.tensor_tensor(parts[:, j, 2], rest[:, u, :].rearrange("p (g t) -> p g t", g=4), parts[:, j, 1],
                                        ALU.subtract).then_inc(low_done, 1)

            walk(pool, TILES, TPB, TPB, [(0, inverse_deviation), (7, split)])

        @block.vector
        def _(dve):
            for i in range(6):
                dve.wait_ge(w_turned, i + 1)
                for c in range(2):
                    dst = w_qk[:, c, i * P:(i + 1) * P] if i < 4 else w_v[:, c, (i - 4) * P:(i - 3) * P]
                    last = nc.vector.tensor_copy(dst, ps_t[i % 2][:, c, :])
                last.then_inc(w_copied, 1)

            def statistics(n, j):
                u = j % 2
                dve.wait_ge(x_loaded[j], 16 * (turns(n, j, TPB) + 1))
                nc.vector.bn_stats(stats[:, u, :], xt[:, j, :]).then_inc(stats_done, 1)
                dve.wait_ge(stats_done, n + 1)
                wait(dve, xn_done, n - 3)
                passed_by(dve, dve_passed)
                nc.vector.bn_aggr(mean_var[:, j, :], stats[:, u, :]).then_inc(mv_done, 1)

            def normalise(n, j):
                u = j % 2
                dve.wait_ge(rstd_done, n + 1)
                wait(dve, x_turned, n - 3)
                nc.vector.tensor_scalar(xn[:, j, :], xt[:, j, :], mean_var[:, j, 0:1], rstd[:, j],
                                        ALU.subtract, ALU.mult).then_inc(xn_done, 1)

            def rotate(n, j):
                u = j % 2
                if j == 0 and isinstance(n, int) and n == 0:
                    dve.wait_ge(const_in, 16 * 6)
                dve.wait_ge(qk_projected, n + 1)
                heads = ps_qk[u][:].rearrange("p (h d) -> p h d", d=DK)
                turned = rot_sin[:, u, :].rearrange("p (h d) -> p h d", d=DK)
                cos_b = cos[:, j, :].rearrange("p (o d) -> p o d", o=1).to_broadcast([P, 2 * H, DK])
                nc.vector.tensor_tensor(rot_cos[:, u, :].rearrange("p (h d) -> p h d", d=DK), heads, cos_b, ALU.mult)
                for part in range(2):
                    dims = slice(part * HALF, (part + 1) * HALF)
                    sin_b = sin[:, j, dims].rearrange("p (o d) -> p o d", o=1).to_broadcast([P, 2 * H, HALF])
                    last = nc.vector.tensor_tensor(turned[:, :, dims], heads[:, :, 1 - part::2], sin_b, ALU.mult)
                last.then_inc(rot_done, 1)
                dve.wait_ge(rot_done, n + 1)
                wait(dve, qk_turned, n - 1)
                nc.vector.tensor_tensor(qk[:, u, :], rot_cos[:, u, :], rot_sin[:, u, :], ALU.add).then_inc(qk_done, 1)

            def remainder(n, j):
                u = j % 2
                dve.wait_ge(high_done, n + 1)
                wait(dve, low_done, n - 1)
                nc.vector.tensor_tensor(rest[:, u, :].rearrange("p (g t) -> p g t", g=4), ps_t[u][:], parts[:, j, 0],
                                        ALU.subtract).then_inc(rest_done, 1)

            walk(dve, TILES, TPB, TPB, [(0, statistics), (4, rotate), (6, remainder), (1, normalise)])

        @block.scalar
        def _(act):
            def evacuate_x(n, j):
                u = j % 2
                act.wait_ge(x_turned, n + 1)
                wait(act, v_projected, n - 1)
                nc.scalar.activation(xnT[:, u], ps_x[:], ACT.Copy).then_inc(xnT_done, 1)

            def evacuate_v(n, j):
                u = j % 2
                act.wait_ge(v_projected, n + 1)
                if isinstance(n, int) and n == 0:
                    act.wait_ge(setup, 4)
                wait(act, v_stored[u], 16 * turns(n, u, 2))
                nc.scalar.activation(v_aug[:, u, :, 0:DK], ps_v[u][:].rearrange("p (h d) -> p h d", d=DK), ACT.Copy).then_inc(v_copied, 1)
                act.wait_ge(v_copied, n + 1)
                act.dma_start(dram["v_aug"][bass.ds(n * P, P), :], v_aug[:, u].rearrange("p h d -> p (h d)")).then_inc(v_stored[u], 16)

            def high(n, j):
                u = j % 2
                act.wait_ge(qk_turned, n + 1)
                wait(act, parts_stored[j], 16 * turns(n, j, TPB))
                nc.scalar.activation(parts[:, j, 0], ps_t[u][:], ACT.Copy).then_inc(high_done, 1)

            def middle(n, j):
                u = j % 2
                act.wait_ge(rest_done, n + 1)
                nc.scalar.activation(parts[:, j, 1], rest[:, u, :].rearrange("p (g t) -> p g t", g=4), ACT.Copy).then_inc(mid_done, 1)

            walk(act, TILES, TPB, TPB, [(7, middle), (2, evacuate_x), (3, evacuate_v), (5, high)])
            for u in range(2):
                act.wait_ge(v_stored[u], 16 * TILES // 2)

        @block.tensor
        def _(pe):
            pe.wait_ge(const_in, 16 * 6)
            for i in range(6):
                wait(pe, w_copied, i - 1)
                for c in range(2):
                    last = nc.tensor.transpose(ps_t[i % 2][:, c, :], w_rows[:, i, c * P:(c + 1) * P], ident[:])
                last.then_inc(w_turned, 1)
            pe.wait_ge(w_copied, 6)

            def turn_x(n, j):
                u = j % 2
                pe.wait_ge(xn_done, n + 1)
                wait(pe, xnT_done, n)
                for c in range(2):
                    last = nc.tensor.transpose(ps_x[:, c, :], xn[:, j, c * P:(c + 1) * P], ident[:])
                last.then_inc(x_turned, 1)

            def project(n, j):
                u = j % 2
                pe.wait_ge(xnT_done, n + 1)
                wait(pe, rot_done, n - 1)
                for c in range(2):
                    last = nc.tensor.matmul(ps_qk[u][:], xnT[:, u, c, :], w_qk[:, c, :], start=c == 0, stop=c == 1)
                last.then_inc(qk_projected, 1)
                wait(pe, v_copied, n - 1)
                for c in range(2):
                    last = nc.tensor.matmul(ps_v[u][:], xnT[:, u, c, :], w_v[:, c, :], start=c == 0, stop=c == 1)
                last.then_inc(v_projected, 1)

            def turn_qk(n, j):
                u = j % 2
                pe.wait_ge(qk_done, n + 1)
                wait(pe, rest_done, n - 1)
                for g in range(4):
                    last = nc.tensor.transpose(ps_t[u][:, g, :], qk[:, u, g * P:(g + 1) * P], ident[:])
                last.then_inc(qk_turned, 1)

            walk(pe, TILES, TPB, TPB, [(2, turn_x), (3, project), (5, turn_qk)])


def attention_mix(nc, dram, x_in, x_out, wo, const):
    import concourse.bass as bass
    from concourse import mybir
    from contextlib import ExitStack
    fp32, bf16 = mybir.dt.float32, mybir.dt.bfloat16
    ALU, ACT, AX = mybir.AluOpType, mybir.ActivationFunctionType, mybir.AxisListType
    P, D, H, DK, S = 128, 256, 16, 16, 512
    SEQS, QT = 16, S // P
    PERIOD = 2 * H
    Q_PARTS = (0, 0, 1, 1, 0, 2)
    K_PARTS = (0, 1, 0, 1, 2, 0)
    SLOTS = len(Q_PARTS)
    K_MAX = SLOTS * DK
    K_ALL = K_MAX + 2
    HALF = H // 2
    VW = 2 * DK
    L_TURN, L_MSPLIT, L_S, L_PV, L_OCOPY, L_OTURN, L_ONORM = 1, 2, 12, 17, 18, 19, 20
    L_ATT = L_ONORM + 1

    with ExitStack() as ctx:
        def sb(name, shape, dt=fp32):
            return ctx.enter_context(nc.sbuf_tensor("a2_" + name, shape, dt))

        def pb(name, shape, dt=fp32):
            return ctx.enter_context(nc.psum_tensor("a2_" + name, shape, dt))

        def sem(name):
            return nc.alloc_semaphore("a2_" + name)

        wo_rows = sb("wo_rows", [P, 2, D])
        woT = sb("woT", [P, 2, D])
        ident = sb("ident", [P, P])
        qs = [sb(f"qs{u}", [P, H, S], bf16) for u in range(2)]
        ks = [sb(f"ks{u}", [P, H, S], bf16) for u in range(2)]
        va = [sb(f"va{u}", [P, QT, H * VW]) for u in range(2)]
        xr = [sb(f"xr{u}", [P, QT, D]) for u in range(2)]
        row_max = sb("row_max", [P, 2, QT, H])
        m_parts = sb("m_parts", [HALF, 2, 2, S], bf16)
        probs = sb("probs", [P, 2, 4, QT, S])
        o_sb = sb("o_sb", [P, 2, S])
        rden = sb("rden", [P, 2, QT, 4])
        att = sb("att", [P, 2, QT, D])
        attT = sb("attT", [P, 2, 4, P])
        xo = sb("xo", [P, 2, 2, D])
        ps_m = [pb(f"ps_m{u}", [P, S]) for u in range(2)]
        ps_s = [pb(f"ps_s{u}", [P, 2, S]) for u in range(2)]
        ps_o = pb("ps_o", [P, S])
        ps_w = pb("ps_w", [P, 4, P])

        const_in, w_turned, w_copied, ones_set = sem("const_in"), sem("w_turned"), sem("w_copied"), sem("ones_set")
        qk_loaded = [[sem(f"qk_loaded{u}{f}") for f in range(2)] for u in range(2)]
        va_loaded = [sem(f"va_loaded{u}") for u in range(2)]
        xr_loaded = [sem(f"xr_loaded{u}") for u in range(2)]
        m_loaded = [sem(f"m_loaded{f}") for f in range(2)]
        max_ready, max_done, m_turned, m_high, m_low = (sem(n) for n in ("max_ready", "max_done", "m_turned", "m_high", "m_low"))
        s_ready, exp_done, pv_done, o_copied, o_turned, rden_done, o_normed = (sem(n) for n in (
            "s_ready", "exp_done", "pv_done", "o_copied", "o_turned", "rden_done", "o_normed"))
        att_turned, attT_done, projected, added = (sem(n) for n in ("att_turned", "attT_done", "projected", "added"))
        stored = [sem(f"stored{q}") for q in range(2)]
        block = ctx.enter_context(nc.Block())

        class Head:

            def __init__(self, base, k):
                self.base, self.k = base, k
                self.h, self.u = k % H, k // H % 2

            def count(self, per_period, extra):
                return self.base * per_period + extra

        def uses(step, first, period=PERIOD):
            n = -((first - step.k) // period)
            n = step.base * (PERIOD // period) + n
            return min(max(0, n), SEQS * H // period) if isinstance(n, int) else n

        def walk(eng, stages):
            deepest = max(lag for lag, _ in stages)
            total = SEQS * H

            def step(base, k, peeled):
                for lag, stage in stages:
                    if peeled and not 0 <= PERIOD * base + k - lag < total:
                        continue
                    stage(Head(base, k - lag), Head(base, k))

            for k in range(PERIOD):
                step(0, k, True)
            with eng.Fori(1, SEQS // 2) as base:
                for k in range(PERIOD):
                    step(base, k, False)
            for k in range(deepest):
                step(SEQS // 2, k, True)

        A_TURN = (H - 1 + L_ATT, H - 1 + L_ATT + 3)
        A_PROJ = (H - 1 + L_ATT + 1, H - 1 + L_ATT + 5)

        def ps_w_free(pe, step):
            wait(pe, m_low, uses(step, HALF - 1 + L_TURN, HALF))
            wait(pe, o_normed, uses(step, 3 + L_OTURN, 4))
            wait(pe, attT_done, uses(step, A_TURN[0], H) + uses(step, A_TURN[1], H))
            wait(pe, added, uses(step, A_PROJ[0], H) + uses(step, A_PROJ[1], H))

        @block.sync
        def _(sp):
            sp.dma_start(wo_rows[:], wo.rearrange("(c p) d -> p c d", p=P)).then_inc(const_in, 16)
            sp.dma_start(ident[:], const["ident"]).then_inc(const_in, 16)

            def load_qk(b, u, f):
                wait(sp, s_ready, 2 * (H * (b - 2) + HALF * (f + 1)))
                heads = slice(f * HALF, (f + 1) * HALF)
                for tiles, parts_of, half in ((qs, Q_PARTS, 0), (ks, K_PARTS, 2)):
                    for slot, part in enumerate(parts_of):
                        src = dram["parts"][b, 4 * part + half + f].rearrange("(h d) t -> d h t", d=DK)
                        sp.dma_start(tiles[u][slot * DK:(slot + 1) * DK, heads, :], src).then_inc(qk_loaded[u][f], 16)

            def load_m(b, u, f):
                wait(sp, m_low, 2 * b + f + 1)
                wait(sp, m_high, 2 * b + f + 1)
                heads = slice(f * HALF, (f + 1) * HALF)
                for part in range(2):
                    sp.dma_start(qs[u][K_MAX + part:K_MAX + part + 1, heads, :], m_parts[:, f, part, :]).then_inc(m_loaded[f], 16)

            def sequence(b, u, last):
                load_m(b, u, 0)
                wait(sp, pv_done, H * (b - 1))
                rows = x_rows(dram["v_aug"], b)
                sp.dma_start(va[u][:], rows).then_inc(va_loaded[u], 16)
                if not last:
                    for f in range(2):
                        load_qk(b + 1, 1 - u, f)
                load_m(b, u, 1)
                wait(sp, added, 2 * (b - 1))
                sp.dma_start(xr[u][:], x_rows(x_in, b)).then_inc(xr_loaded[u], 16)

            def x_rows(t, b):
                return t[bass.ds(b * S, S), :].rearrange("(t p) d -> p t d", p=P)

            for f in range(2):
                load_qk(0, 0, f)
            sequence(0, 0, False)
            sequence(1, 1, False)
            with sp.Fori(1, SEQS // 2 - 1) as i:
                for u in range(2):
                    sequence(2 * i + u, u, False)
            sequence(SEQS - 2, 0, False)
            sequence(SEQS - 1, 1, True)

        @block.gpsimd
        def _(pool):
            for u in range(2):
                last = nc.gpsimd.memset(ks[u][K_MAX:K_ALL, :, :], 1.0)
            last.then_inc(ones_set, 1)

            def store(b):
                for q in range(2):
                    pool.wait_ge(added, 2 * b + q + 1)
                    pool.dma_start(x_out[bass.ds(b * S + q * 2 * P, 2 * P), :].rearrange("(t p) d -> p t d", p=P), xo[:, q]).then_inc(stored[q], 16)

            with pool.Fori(0, SEQS) as b:
                store(b)
            for q in range(2):
                pool.wait_ge(stored[q], 16 * SEQS)

        @block.tensor
        def _(pe):
            pe.wait_ge(const_in, 32)
            for i in range(2):
                wait(pe, w_copied, i)
                for c in range(2):
                    last = nc.tensor.transpose(ps_w[:, c, :], wo_rows[:, i, c * P:(c + 1) * P], ident[:])
                last.then_inc(w_turned, 1)
            pe.wait_ge(w_copied, 2)

            def max_products(t):
                def stage(n, step):
                    u, h = n.u, n.h
                    if h % HALF == 0 and t == 0:
                        pe.wait_ge(qk_loaded[u][h // HALF], 16 * 2 * SLOTS * (n.base + 1))
                    wait(pe, max_done, n.count(QT * PERIOD, QT * n.k + t - 1))
                    nc.tensor.matmul(ps_m[t % 2][:], qs[u][0:K_MAX, h, t * P:(t + 1) * P], ks[u][0:K_MAX, h, :],
                                     start=True, stop=True).then_inc(max_ready, 1)
                return stage

            def turn_max(n, step):
                if n.h % HALF != HALF - 1:
                    return
                pe.wait_ge(max_done, n.count(QT * PERIOD, QT * (n.k + 1)))
                ps_w_free(pe, step)
                h0 = n.h - HALF + 1
                for t in range(QT):
                    last = nc.tensor.transpose(ps_w[0:HALF, t, :], row_max[:, n.u, t, h0:h0 + HALF], ident[:])
                last.then_inc(m_turned, 1)

            def scores(half):
                def stage(n, step):
                    u, h = n.u, n.h
                    if isinstance(n.base, int) and n.base == 0 and n.k == 0:
                        pe.wait_ge(ones_set, 1)
                    if h % HALF == 0 and half == 0:
                        pe.wait_ge(m_loaded[h // HALF], n.count(64, 32 * (n.k // H + 1)))
                    wait(pe, exp_done, n.count(2 * PERIOD, 2 * n.k + half - 1))
                    for i in range(2):
                        t = 2 * half + i
                        last = nc.tensor.matmul(ps_s[half][:, i, :], ks[u][0:K_ALL, h, t * P:(t + 1) * P], qs[u][0:K_ALL, h, :],
                                                start=True, stop=True)
                    last.then_inc(s_ready, 1)
                return stage

            def mix_values(n, step):
                t = n.h % 4
                group = n.k // 4
                if t == 0:
                    pe.wait_ge(exp_done, n.count(2 * PERIOD, 2 * n.k + 8))
                    wait(pe, o_copied, n.count(PERIOD // 4, group))
                    if n.h == 0:
                        pe.wait_ge(va_loaded[n.u], n.count(16, 16 * (n.k // PERIOD + 1)))
                for j in range(4):
                    h = n.h - t + j
                    last = nc.tensor.matmul(ps_o[VW * j:VW * (j + 1), :], va[n.u][:, t, h * VW:(h + 1) * VW],
                                            probs[:, group % 2, j, t, :], start=t == 0, stop=t == QT - 1)
                last.then_inc(pv_done, 1)

            def turn_output(n, step):
                if n.h % 4 != 3:
                    return
                group = n.k // 4
                pe.wait_ge(o_copied, n.count(PERIOD // 4, group + 1))
                ps_w_free(pe, step)
                for t in range(QT):
                    last = nc.tensor.transpose(ps_w[:, t, :], o_sb[:, group % 2, t * P:(t + 1) * P], ident[:])
                last.then_inc(o_turned, 1)

            def turn_att(q):
                def stage(n, step):
                    if n.h != H - 1:
                        return
                    pe.wait_ge(o_normed, n.count(PERIOD // 4, n.k // 4 + 1))
                    ps_w_free(pe, step)
                    for t in range(2):
                        for c in range(2):
                            last = nc.tensor.transpose(ps_w[:, 2 * t + c, :], att[:, n.u, 2 * q + t, c * P:(c + 1) * P], ident[:])
                    last.then_inc(att_turned, 1)
                return stage

            def project(q):
                def stage(n, step):
                    if n.h != H - 1:
                        return
                    pe.wait_ge(attT_done, n.count(4, 2 * (n.k // H) + q + 1))
                    ps_w_free(pe, step)
                    out = ps_w[:].rearrange("p a b -> p (a b)")
                    for t in range(2):
                        for c in range(2):
                            last = nc.tensor.matmul(out[:, t * D:(t + 1) * D], attT[:, q, 2 * t + c, :], woT[:, c, :], start=c == 0, stop=c == 1)
                    last.then_inc(projected, 1)
                return stage

            walk(pe, [(0, max_products(0)), (L_S, scores(0)), (0, max_products(1)), (L_PV, mix_values), (0, max_products(2)),
                      (L_S, scores(1)), (0, max_products(3)), (L_TURN, turn_max), (L_OTURN, turn_output),
                      (A_TURN[0] - H + 1, turn_att(0)), (A_PROJ[0] - H + 1, project(0)),
                      (A_TURN[1] - H + 1, turn_att(1)), (A_PROJ[1] - H + 1, project(1))])

        @block.vector
        def _(dve):
            for i in range(2):
                dve.wait_ge(w_turned, i + 1)
                for c in range(2):
                    last = nc.vector.tensor_copy(woT[:, c, i * P:(i + 1) * P], ps_w[:, c, :])
                last.then_inc(w_copied, 1)

            def maxima(n, step):
                for t in range(QT):
                    dve.wait_ge(max_ready, n.count(QT * PERIOD, QT * n.k + t + 1))
                    nc.vector.tensor_reduce(row_max[:, n.u, t, n.h:n.h + 1], ps_m[t % 2][:], AX.X, ALU.max).then_inc(max_done, 1)

            def low_max(n, step):
                if n.h % HALF != HALF - 1:
                    return
                f = n.h // HALF
                dve.wait_ge(m_high, n.count(4, n.k // HALF + 1))
                nc.vector.scalar_tensor_tensor(m_parts[:, f, 1, :], ps_w[0:HALF].rearrange("p a b -> p (a b)"), -1.0, m_parts[:, f, 0, :],
                                               ALU.mult, ALU.subtract).then_inc(m_low, 1)

            def normalise(n, step):
                if n.h % 4 != 3:
                    return
                group = n.k // 4
                dve.wait_ge(o_turned, n.count(PERIOD // 4, group + 1))
                heads = ps_w[:].rearrange("p t (j w) -> p t j w", w=VW)
                nc.vector.reciprocal(rden[:, group % 2], heads[:, :, :, DK]).then_inc(rden_done, 1)
                dve.wait_ge(rden_done, n.count(PERIOD // 4, group + 1))
                h0 = n.h - 3
                for t in range(QT):
                    dst = att[:, n.u, t, h0 * DK:(h0 + 4) * DK].rearrange("p (j d) -> p j d", d=DK)
                    last = nc.vector.tensor_tensor(dst, heads[:, t, :, 0:DK],
                                                   rden[:, group % 2, t, :].rearrange("p (j o) -> p j o", o=1).to_broadcast([P, 4, DK]), ALU.mult)
                last.then_inc(o_normed, 1)

            def residual(q):
                def stage(n, step):
                    if n.h != H - 1:
                        return
                    dve.wait_ge(projected, n.count(4, 2 * (n.k // H) + q + 1))
                    if q == 0:
                        dve.wait_ge(xr_loaded[n.u], n.count(16, 16 * (n.k // PERIOD + 1)))
                    wait(dve, stored[q], n.count(32, 16 * (n.k // H)))
                    out = ps_w[:].rearrange("p a b -> p (a b)").rearrange("p (t d) -> p t d", d=D)
                    nc.vector.tensor_tensor(xo[:, q], out, xr[n.u][:, 2 * q:2 * q + 2, :], ALU.add).then_inc(added, 1)
                return stage

            walk(dve, [(L_MSPLIT, low_max), (0, maxima), (L_ONORM, normalise),
                       (A_PROJ[0] - H + 2, residual(0)), (A_PROJ[1] - H + 2, residual(1))])

        @block.scalar
        def _(act):
            def high_max(n, step):
                if n.h % HALF != HALF - 1:
                    return
                f = n.h // HALF
                act.wait_ge(m_turned, n.count(4, n.k // HALF + 1))
                wait(act, m_loaded[f], n.count(64, 32 * (n.k // H)))
                nc.scalar.activation(m_parts[:, f, 0, :], ps_w[0:HALF].rearrange("p a b -> p (a b)"), ACT.Copy, scale=-1.0).then_inc(m_high, 1)

            def exponentials(n, step):
                group = n.k // 4
                if n.h % 4 == 0:
                    wait(act, pv_done, n.count(PERIOD, n.k - 4))
                for half in range(2):
                    act.wait_ge(s_ready, n.count(2 * PERIOD, 2 * n.k + half + 1))
                    nc.scalar.activation(probs[:, group % 2, n.h % 4, 2 * half:2 * half + 2, :], ps_s[half][:], ACT.Exp,
                                         scale=DK ** -0.5).then_inc(exp_done, 1)

            def copy_output(n, step):
                if n.h % 4 != 3:
                    return
                group = n.k // 4
                act.wait_ge(pv_done, n.count(PERIOD, n.k + 1))
                wait(act, o_turned, n.count(PERIOD // 4, group - 1))
                nc.scalar.activation(o_sb[:, group % 2, :], ps_o[:], ACT.Copy).then_inc(o_copied, 1)

            def copy_att(q):
                def stage(n, step):
                    if n.h != H - 1:
                        return
                    act.wait_ge(att_turned, n.count(4, 2 * (n.k // H) + q + 1))
                    nc.scalar.activation(attT[:, q], ps_w[:], ACT.Copy).then_inc(attT_done, 1)
                return stage

            walk(act, [(L_MSPLIT, high_max), (L_OCOPY, copy_output), (L_S, exponentials),
                       (A_TURN[0] - H + 1, copy_att(0)), (A_TURN[1] - H + 1, copy_att(1))])


def moe_route(nc, tag, dram, x_in, router_w, const):
    import concourse.bass as bass
    from concourse import mybir
    from contextlib import ExitStack
    fp32 = mybir.dt.float32
    ALU, ACT, AX = mybir.AluOpType, mybir.ActivationFunctionType, mybir.AxisListType
    P, D, T, E, B = 128, 256, 8192, 64, 4
    TILES = T // P
    order = const["order"]

    with ExitStack() as ctx:
        def sb(name, shape, dt=fp32):
            return ctx.enter_context(nc.sbuf_tensor(f"{tag}r_" + name, shape, dt))

        def pb(name, shape, dt=fp32):
            return ctx.enter_context(nc.psum_tensor(f"{tag}r_" + name, shape, dt))

        def sem(name):
            return nc.alloc_semaphore(f"{tag}r_" + name)

        rw_rows = sb("rw_rows", [E, D])
        rwT = sb("rwT", [P, 2, E])
        ident = sb("ident", [P, P])
        rank_value = sb("rank_value", [P, TILES])
        minus_half = sb("minus_half", [P, 1])
        eps = sb("eps", [P, 1])
        zeros = sb("zeros", [P, D + E])
        xt = sb("xt", [P, B, D])
        stats = sb("stats", [P, B, 6])
        mean_var = sb("mean_var", [P, B, 2])
        var_eps = sb("var_eps", [P, B, 1])
        rstd = sb("rstd", [P, B, 1])
        xn = sb("xn", [P, B, D])
        xnT = sb("xnT", [P, B, 2, P])
        top_logit = sb("top_logit", [P, B, 1])
        logit = sb("logit", [P, B, E])
        expd = sb("expd", [P, B, E])
        top8 = sb("top8", [P, B, 8])
        marked = sb("marked", [P, B, E])
        value = sb("value", [P, B, E])
        picked = sb("picked", [P, B, E])
        total = sb("total", [P, B, 1])
        gate = sb("gate", [P, B, E])
        ps_x = [pb(f"ps_x{u}", [P, 2, P]) for u in range(2)]
        ps_l = [pb(f"ps_l{u}", [P, E]) for u in range(2)]
        ps_v = [pb(f"ps_v{u}", [P, P]) for u in range(2)]

        const_in, setup, w_turned, w_copied, pad_stored = (sem(n) for n in ("const_in", "setup", "w_turned", "w_copied", "pad_stored"))
        x_loaded = [sem(f"x_loaded{k}") for k in range(B)]
        xn_stored = [sem(f"xn_stored{k}") for k in range(B)]
        xnT_stored = [sem(f"xnT_stored{k}") for k in range(B)]
        gate_stored = [sem(f"gate_stored{k}") for k in range(B)]
        (stats_done, mv_done, ve_done, rstd_done, xn_done, x_turned, xnT_done, logits_ready, top_done, logit_done, exp_done, top8_done,
         marked_done, value_done, picked_done, recip_done, gate_done, value_turned, order_done) = (sem(n) for n in (
             "stats_done", "mv_done", "ve_done", "rstd_done", "xn_done", "x_turned", "xnT_done", "logits_ready", "top_done", "logit_done",
             "exp_done", "top8_done", "marked_done", "value_done", "picked_done", "recip_done", "gate_done", "value_turned", "order_done"))
        dve_passed = sem("dve_passed")
        block = ctx.enter_context(nc.Block())
        MARK = -1e30

        def tile(n, k):
            return k % 2 * (TILES // 2) + turns(n, k % 2, 2)

        def rows(t, n, k):
            return t[bass.ds(tile(n, k) * P, P), :]

        @block.sync
        def _(sp):
            sp.dma_start(rw_rows[:], router_w).then_inc(const_in, 16)
            sp.dma_start(ident[:], const["ident"]).then_inc(const_in, 16)
            sp.dma_start(rank_value[:], const["rank_value"]).then_inc(const_in, 16)
            sp.wait_ge(setup, 3)
            sp.dma_start(dram["rows"][T:T + P, :], zeros[:]).then_inc(pad_stored, 16)

            def load(n, k):
                wait(sp, xn_done, n - B + 1)
                sp.dma_start(xt[:, k, :], rows(x_in, n, k)).then_inc(x_loaded[k], 16)

            def store_rows(n, k):
                sp.wait_ge(xn_done, n + 1)
                sp.dma_start(rows(dram["rows"], n, k)[:, 0:D], xn[:, k, :]).then_inc(xn_stored[k], 16)

            def store_gates(n, k):
                sp.wait_ge(gate_done, n + 1)
                sp.dma_start(rows(dram["rows"], n, k)[:, D:D + E], gate[:, k, :]).then_inc(gate_stored[k], 16)

            walk(sp, TILES, B, B, [(0, load), (2, store_rows), (12, store_gates)])
            sp.wait_ge(pad_stored, 16)
            for k in range(B):
                sp.wait_ge(xn_stored[k], 16 * TILES // B)
                sp.wait_ge(gate_stored[k], 16 * TILES // B)

        @block.gpsimd
        def _(pool):
            nc.gpsimd.memset(minus_half[:], -0.5).then_inc(setup, 1)
            nc.gpsimd.memset(eps[:], 1e-5).then_inc(setup, 1)
            nc.gpsimd.memset(zeros[:], 0.0).then_inc(setup, 1)
            pool.wait_ge(setup, 3)

            def inverse_deviation(n, k):
                pool.wait_ge(mv_done, n + 1)
                nc.gpsimd.tensor_tensor(var_eps[:, k], mean_var[:, k, 1:2], eps[:], ALU.add).then_inc(ve_done, 1)
                pool.wait_ge(ve_done, n + 1)
                wait(pool, xn_done, n - B + 1)
                nc.gpsimd.tensor_tensor(rstd[:, k], var_eps[:, k], minus_half[:], ALU.pow).then_inc(rstd_done, 1)

            def store_turned(n, k):
                pool.wait_ge(xnT_done, n + 1)
                pool.dma_start(dram["turned"].rearrange("(c p) t -> p c t", p=P)[:, :, bass.ds(tile(n, k) * P, P)],
                               xnT[:, k]).then_inc(xnT_stored[k], 16)

            walk(pool, TILES, B, B, [(0, inverse_deviation), (3, store_turned)])
            for k in range(B):
                pool.wait_ge(xnT_stored[k], 16 * TILES // B)

        @block.vector
        def _(dve):
            dve.wait_ge(w_turned, 1)
            nc.vector.tensor_copy(rwT[:], ps_x[0][:, :, 0:E]).then_inc(w_copied, 1)
            dve.wait_ge(const_in, 48)

            def statistics(n, k):
                dve.wait_ge(x_loaded[k], 16 * (turns(n, k, B) + 1))
                nc.vector.bn_stats(stats[:, k, :], xt[:, k, :]).then_inc(stats_done, 1)

            def aggregate(n, k):
                dve.wait_ge(stats_done, n + 1)
                passed_by(dve, dve_passed)
                nc.vector.bn_aggr(mean_var[:, k, :], stats[:, k, :]).then_inc(mv_done, 1)

            def normalise(n, k):
                dve.wait_ge(rstd_done, n + 1)
                wait(dve, x_turned, n - B + 1)
                wait(dve, xn_stored[k], 16 * turns(n, k, B))
                nc.vector.tensor_scalar(xn[:, k, :], xt[:, k, :], mean_var[:, k, 0:1], rstd[:, k],
                                        ALU.subtract, ALU.mult).then_inc(xn_done, 1)

            def maximum(n, k):
                dve.wait_ge(logits_ready, n + 1)
                nc.vector.tensor_reduce(top_logit[:, k], ps_l[k % 2][:], AX.X, ALU.max).then_inc(top_done, 1)

            def shift(n, k):
                dve.wait_ge(top_done, n + 1)
                wait(dve, exp_done, n - B + 1)
                nc.vector.tensor_scalar(logit[:, k, :], ps_l[k % 2][:], top_logit[:, k], -104.0, ALU.subtract, ALU.max).then_inc(logit_done, 1)

            def eight_largest(n, k):
                dve.wait_ge(logit_done, n + 1)
                passed_by(dve, dve_passed)
                nc.vector.max(top8[:, k, :], logit[:, k, :]).then_inc(top8_done, 1)

            def mark(n, k):
                dve.wait_ge(top8_done, n + 1)
                passed_by(dve, dve_passed)
                nc.vector.match_replace(marked[:, k, :], top8[:, k, :], logit[:, k, :], MARK).then_inc(marked_done, 1)

            def values(n, k):
                dve.wait_ge(marked_done, n + 1)
                wait(dve, value_turned, n - B + 1)
                nc.vector.tensor_scalar(value[:, k, :], marked[:, k, :], MARK / 2, rank_value[:, bass.ds(n, 1)], ALU.is_lt, ALU.mult).then_inc(value_done, 1)

            def pick(n, k):
                dve.wait_ge(exp_done, n + 1)
                dve.wait_ge(marked_done, n + 1)
                nc.vector.scalar_tensor_tensor(picked[:, k, :], marked[:, k, :], MARK / 2, expd[:, k, :], ALU.is_lt, ALU.mult,
                                               accum_out=total[:, k]).then_inc(picked_done, 1)

            def invert(n, k):
                dve.wait_ge(picked_done, n + 1)
                nc.vector.reciprocal(total[:, k], total[:, k]).then_inc(recip_done, 1)

            def gates(n, k):
                dve.wait_ge(recip_done, n + 1)
                wait(dve, gate_stored[k], 16 * turns(n, k, B))
                nc.vector.tensor_scalar(gate[:, k, :], picked[:, k, :], total[:, k], None, ALU.mult).then_inc(gate_done, 1)

            walk(dve, TILES, B, B, [(0, statistics), (10, gates), (9, invert), (8, pick), (8, values), (7, mark), (6, eight_largest),
                                    (0, aggregate), (5, shift), (4, maximum), (1, normalise)])

        @block.scalar
        def _(act):
            def evacuate_x(n, k):
                act.wait_ge(x_turned, n + 1)
                wait(act, logits_ready, n - B + 1)
                wait(act, xnT_stored[k], 16 * turns(n, k, B))
                nc.scalar.activation(xnT[:, k], ps_x[k % 2][:], ACT.Copy).then_inc(xnT_done, 1)

            def exponential(n, k):
                act.wait_ge(logit_done, n + 1)
                wait(act, picked_done, n - B + 1)
                nc.scalar.activation(expd[:, k, :], logit[:, k, :], ACT.Exp).then_inc(exp_done, 1)

            def put_order(n, k):
                act.wait_ge(value_turned, n + 1)
                half = slice(k % 2 * E, (k % 2 + 1) * E)
                nc.scalar.activation(order[half, bass.ds(turns(n, k % 2, 2) * P, P)], ps_v[k % 2][half, :], ACT.Copy).then_inc(order_done, 1)

            walk(act, TILES, B, B, [(2, evacuate_x), (6, exponential), (10, put_order)])
            act.wait_ge(order_done, TILES)

        @block.tensor
        def _(pe):
            pe.wait_ge(const_in, 48)
            for c in range(2):
                last = nc.tensor.transpose(ps_x[0][:, c, 0:E], rw_rows[:, c * P:(c + 1) * P], ident[0:E, 0:E])
            last.then_inc(w_turned, 1)
            pe.wait_ge(w_copied, 1)

            def turn_x(n, k):
                pe.wait_ge(xn_done, n + 1)
                wait(pe, xnT_done, n - 1)
                for c in range(2):
                    last = nc.tensor.transpose(ps_x[k % 2][:, c, :], xn[:, k, c * P:(c + 1) * P], ident[:])
                last.then_inc(x_turned, 1)

            def logits(n, k):
                pe.wait_ge(xnT_done, n + 1)
                wait(pe, logit_done, n - 1)
                for c in range(2):
                    last = nc.tensor.matmul(ps_l[k % 2][:], xnT[:, k, c, :], rwT[:, c, :], start=c == 0, stop=c == 1)
                last.then_inc(logits_ready, 1)

            def turn_values(n, k):
                pe.wait_ge(value_done, n + 1)
                wait(pe, order_done, n - 1)
                half = slice(k % 2 * E, (k % 2 + 1) * E)
                nc.tensor.matmul(ps_v[k % 2][half, :], value[:, k, :], ident[:], start=True, stop=True).then_inc(value_turned, 1)

            walk(pe, TILES, B, B, [(2, turn_x), (3, logits), (9, turn_values)])


def moe_shared(nc, tag, dram, x_in, x_out, ws_gate_up, ws_down, const):
    import concourse.bass as bass
    from concourse import mybir
    from contextlib import ExitStack
    fp32, u32 = mybir.dt.float32, mybir.dt.uint32
    ALU, ACT = mybir.AluOpType, mybir.ActivationFunctionType
    P, D, T, E, SF, CAP = 128, 256, 8192, 64, 192, 128
    FC = SF // 2
    S = 512
    ROUNDS = CAP // 8
    assert T // S == ROUNDS
    order, slots = const["order"], const["slots"]

    with ExitStack() as ctx:
        def sb(name, shape, dt=fp32):
            return ctx.enter_context(nc.sbuf_tensor(f"{tag}s_" + name, shape, dt))

        def pb(name, shape, dt=fp32):
            return ctx.enter_context(nc.psum_tensor(f"{tag}s_" + name, shape, dt))

        def sem(name):
            return nc.alloc_semaphore(f"{tag}s_" + name)

        w_gu = sb("w_gu", [P, 2, 2 * SF])
        w_d = sb("w_d", [FC, 2, D])
        ident = sb("ident", [P, P])
        spare_row = sb("spare_row", [P, 1])
        xnT = sb("xnT", [P, 2, 2, S])
        xr = sb("xr", [P, 2, 4, D])
        act_g = sb("act_g", [FC, 2, S])
        hT = sb("hT", [FC, 2, 2, S])
        xo = sb("xo", [P, 2, 4, D])
        top8 = sb("top8", [P, 2, 8])
        first = sb("first", [P, CAP])
        merged = sb("merged", [E, 2 * CAP])
        best8 = sb("best8", [E, 2, 8])
        best = sb("best", [E, CAP])
        empty = sb("empty", [P, E])
        number = sb("number", [P, E])
        ps_g = [pb(f"ps_g{c}", [P, S]) for c in range(2)]
        ps_u = [pb(f"ps_u{c}", [P, S]) for c in range(2)]
        ps_d = [pb(f"ps_d{q}", [P, 2, D]) for q in range(2)]
        ps_t = pb("ps_t", [P, E])

        const_in = sem("const_in")
        xT_loaded = [sem(f"xT_loaded{u}") for u in range(2)]
        xr_loaded = [sem(f"xr_loaded{u}") for u in range(2)]
        stored = [sem(f"stored{u}") for u in range(2)]
        gated, silu_done, h_done, down_done, added = (sem(n) for n in ("gated", "silu_done", "h_done", "down_done", "added"))
        top_found, top_kept, top_removed, halves_moved, best_found, best_kept, best_removed, best_turned, empty_done, number_done, slots_done = (
            sem(n) for n in ("top_found", "top_kept", "top_removed", "halves_moved", "best_found", "best_kept", "best_removed", "best_turned",
                             "empty_done", "number_done", "slots_done"))
        dve_passed = sem("dve_passed")
        block = ctx.enter_context(nc.Block())

        def rows(t, r):
            return t[bass.ds(r * S, S), :].rearrange("(t p) d -> p t d", p=P)

        @block.sync
        def _(sp):
            sp.dma_start(w_gu[:], ws_gate_up.rearrange("(c p) f -> p c f", p=P)).then_inc(const_in, 16)
            sp.dma_start(w_d[:], ws_down.rearrange("(c p) d -> p c d", p=FC)).then_inc(const_in, 16)
            sp.dma_start(ident[:], const["ident"]).then_inc(const_in, 16)
            sp.dma_start(spare_row[:], const["spare_row"]).then_inc(const_in, 16)

            def load(r, u):
                wait(sp, gated, 2 * (r - 1))
                sp.dma_start(xnT[:, u], dram["turned"].rearrange("(c p) t -> p c t", p=P)[:, :, bass.ds(r * S, S)]).then_inc(xT_loaded[u], 16)

            def load_rows(r, u):
                wait(sp, added, 2 * (r - 1))
                sp.dma_start(xr[:, u], rows(x_in, r)).then_inc(xr_loaded[u], 16)

            def store(r, u):
                sp.wait_ge(added, 2 * (r + 1))
                sp.dma_start(rows(x_out, r), xo[:, u]).then_inc(stored[u], 16)

            walk(sp, ROUNDS, 2, 2, [(2, store), (0, load), (0, load_rows)])
            for u in range(2):
                sp.wait_ge(stored[u], 16 * ROUNDS // 2)

        @block.tensor
        def _(pe):
            pe.wait_ge(const_in, 64)

            def gate_up(r, u):
                pe.wait_ge(xT_loaded[u], 16 * (turns(r, u, 2) + 1))
                for f in range(2):
                    wait(pe, silu_done, 2 * (r - 1) + f + 1)
                    wait(pe, h_done, 2 * (r - 1) + f + 1)
                    for ps, col in ((ps_g[f], f * FC), (ps_u[f], SF + f * FC)):
                        for c in range(2):
                            last = nc.tensor.matmul(ps[0:FC, :], w_gu[:, c, col:col + FC], xnT[:, u, c, :], start=c == 0, stop=c == 1)
                    last.then_inc(gated, 1)

            def down(r, u):
                pe.wait_ge(h_done, 2 * (r + 1))
                for q in range(2):
                    wait(pe, added, 2 * (r - 1) + q + 1)
                    for t in range(2):
                        at = (2 * q + t) * P
                        for f in range(2):
                            last = nc.tensor.matmul(ps_d[q][:, t, :], hT[:, u, f, at:at + P], w_d[:, f, :], start=f == 0, stop=f == 1)
                    last.then_inc(down_done, 1)

            walk(pe, ROUNDS, 2, 2, [(0, gate_up), (1, down)])
            pe.wait_ge(best_kept, ROUNDS)
            nc.tensor.transpose(ps_t[:], best[:], ident[0:E, 0:E]).then_inc(best_turned, 1)

        @block.scalar
        def _(act):
            def silu(r, u):
                for f in range(2):
                    act.wait_ge(gated, 2 * r + f + 1)
                    wait(act, h_done, 2 * (r - 1) + f + 1)
                    nc.scalar.activation(act_g[:, f, :], ps_g[f][0:FC, :], ACT.Silu).then_inc(silu_done, 1)

            walk(act, ROUNDS, 2, 2, [(0, silu)])

        @block.gpsimd
        def _(pool):
            def keep(r, u):
                pool.wait_ge(top_found, r + 1)
                nc.gpsimd.tensor_copy(first[:, bass.ds(r * 8, 8)], top8[:, u, :]).then_inc(top_kept, 1)

            def keep_best(r, u):
                pool.wait_ge(best_found, r + 1)
                nc.gpsimd.tensor_copy(best[:, bass.ds(r * 8, 8)], best8[:, u, :]).then_inc(best_kept, 1)

            walk(pool, ROUNDS, 2, 2, [(0, keep)])
            walk(pool, ROUNDS, 2, 2, [(0, keep_best)])

        @block.vector
        def _(dve):
            def hidden(f):
                def stage(r, u):
                    dve.wait_ge(silu_done, 2 * r + f + 1)
                    wait(dve, down_done, 2 * (r - 1))
                    nc.vector.tensor_tensor(hT[:, u, f, :], act_g[:, f, :], ps_u[f][0:FC, :], ALU.mult).then_inc(h_done, 1)
                return stage

            def find(r, u):
                wait(dve, top_removed, r)
                wait(dve, top_kept, r - 1)
                passed_by(dve, dve_passed)
                nc.vector.max(top8[:, u, :], order[:]).then_inc(top_found, 1)

            def remove(r, u):
                dve.wait_ge(top_found, r + 1)
                passed_by(dve, dve_passed)
                nc.vector.match_replace(order[:], top8[:, u, :], order[:], 0.0).then_inc(top_removed, 1)

            def add(r, u):
                dve.wait_ge(xr_loaded[u], 16 * (turns(r, u, 2) + 1))
                wait(dve, stored[u], 16 * turns(r, u, 2))
                for q in range(2):
                    dve.wait_ge(down_done, 2 * r + q + 1)
                    nc.vector.tensor_tensor(xo[:, u, 2 * q:2 * q + 2, :], ps_d[q][:], xr[:, u, 2 * q:2 * q + 2, :], ALU.add).then_inc(added, 1)

            walk(dve, ROUNDS, 2, 2, [(0, hidden(0)), (0, find), (0, hidden(1)), (0, remove), (1, add)])

            dve.wait_ge(top_kept, ROUNDS)
            for half in range(2):
                last = nc.vector.tensor_copy(merged[:, half * CAP:(half + 1) * CAP], first[half * E:(half + 1) * E, :])
            last.then_inc(halves_moved, 1)
            dve.wait_ge(halves_moved, 1)

            def find_best(r, u):
                wait(dve, best_removed, r)
                wait(dve, best_kept, r - 1)
                passed_by(dve, dve_passed)
                nc.vector.max(best8[:, u, :], merged[:]).then_inc(best_found, 1)

            def remove_best(r, u):
                dve.wait_ge(best_found, r + 1)
                passed_by(dve, dve_passed)
                nc.vector.match_replace(merged[:], best8[:, u, :], merged[:], 0.0).then_inc(best_removed, 1)

            walk(dve, ROUNDS, 2, 2, [(0, find_best), (0, remove_best)])
            dve.wait_ge(best_turned, 1)
            nc.vector.tensor_scalar(empty[:], ps_t[:], 0.5, spare_row[:], ALU.is_lt, ALU.mult).then_inc(empty_done, 1)
            nc.vector.tensor_scalar(number[:], ps_t[:], -1.0, float(T), ALU.mult, ALU.add).then_inc(number_done, 1)
            dve.wait_ge(empty_done, 1)
            dve.wait_ge(number_done, 1)
            nc.vector.tensor_tensor(slots[:], number[:], empty[:], ALU.add).then_inc(slots_done, 1)
            dve.wait_ge(slots_done, 1)


def moe_experts(nc, tag, dram, x_out, w_gate, w_up, w_down, const):
    import concourse.bass as bass
    from concourse import mybir
    from contextlib import ExitStack
    fp32, u32 = mybir.dt.float32, mybir.dt.uint32
    ALU, ACT = mybir.AluOpType, mybir.ActivationFunctionType
    P, D, T, E, F, B = 128, 256, 8192, 64, 192, 8
    FC = F // 2
    slots = const["slots"]

    with ExitStack() as ctx:
        def sb(name, shape, dt=fp32):
            return ctx.enter_context(nc.sbuf_tensor(f"{tag}e_" + name, shape, dt))

        def pb(name, shape, dt=fp32):
            return ctx.enter_context(nc.psum_tensor(f"{tag}e_" + name, shape, dt))

        def sem(name):
            return nc.alloc_semaphore(f"{tag}e_" + name)

        ident = sb("ident", [P, P])
        wg = sb("wg", [P, B, 2, F])
        wu = sb("wu", [P, B, 2, F])
        wd = sb("wd", [FC, B, 2, D])
        index = sb("index", [P, B, 1], u32)
        xg = sb("xg", [P, B, D + E])
        xgT = sb("xgT", [P, 2, 2, P])
        act_g = sb("act_g", [FC, 2, 2, P])
        hT = sb("hT", [FC, 2, 2, P])
        y = sb("y", [P, B, D])
        ps_x = [pb(f"ps_x{u}", [P, 2, P]) for u in range(2)]
        ps_h = [pb(f"ps_h{u}", [P, 4, P]) for u in range(2)]
        ps_y = [pb(f"ps_y{u}", [P, D]) for u in range(2)]

        const_in = sem("const_in")
        w_loaded = [sem(f"w_loaded{k}") for k in range(B)]
        gathered = [sem(f"gathered{k}") for k in range(B)]
        index_done, x_turned, xT_done, h_ready, silu_done, h_done, y_ready, y_done, scattered = (sem(n) for n in (
            "index_done", "x_turned", "xT_done", "h_ready", "silu_done", "h_done", "y_ready", "y_done", "scattered"))
        pool_passed = sem("pool_passed")
        block = ctx.enter_context(nc.Block())

        @block.sync
        def _(sp):
            sp.dma_start(ident[:], const["ident"]).then_inc(const_in, 16)

            def load(e, k):
                wait(sp, y_ready, e - B + 1)
                for tile, w, p in ((wg, w_gate, P), (wu, w_up, P), (wd, w_down, FC)):
                    sp.dma_start(tile[:, k], w[bass.ds(e, 1)].rearrange("o (c p) f -> p (o c) f", p=p)).then_inc(w_loaded[k], 16)

            walk(sp, E, B, B, [(0, load)])

        @block.gpsimd
        def _(pool):
            def gather(e, k):
                wait(pool, y_done, e - B + 1)
                nc.gpsimd.tensor_copy(index[:, k], slots[:, bass.ds(e, 1)]).then_inc(index_done, 1)
                pool.wait_ge(index_done, e + 1)
                passed_by(pool, pool_passed)
                pool.indirect_dma_start(xg[:, k, :], None, dram["rows"][:, :], bass.IndirectOffsetOnAxis(index[:, k], 0)).then_inc(gathered[k], 16)

            def scatter(e, k):
                pool.wait_ge(y_done, e + 1)
                wait(pool, scattered, 16 * e)
                passed_by(pool, pool_passed)
                pool.indirect_dma_start(x_out[:, :], bass.IndirectOffsetOnAxis(index[:, k], 0), y[:, k, :], None,
                                        compute_op=ALU.add).then_inc(scattered, 16)

            walk(pool, E, B, B, [(7, scatter), (0, gather)])
            pool.wait_ge(scattered, 16 * E)

        @block.tensor
        def _(pe):
            pe.wait_ge(const_in, 16)

            def turn(e, k):
                u = k % 2
                pe.wait_ge(gathered[k], 16 * (turns(e, k, B) + 1))
                wait(pe, xT_done, e - 1)
                for c in range(2):
                    last = nc.tensor.transpose(ps_x[u][:, c, :], xg[:, k, c * P:(c + 1) * P], ident[:])
                last.then_inc(x_turned, 1)

            def gate_up(e, k):
                u = k % 2
                pe.wait_ge(w_loaded[k], 48 * (turns(e, k, B) + 1))
                pe.wait_ge(xT_done, e + 1)
                wait(pe, h_done, e - 1)
                for i, w in enumerate((wg, wu)):
                    for f in range(2):
                        for c in range(2):
                            last = nc.tensor.matmul(ps_h[u][0:FC, 2 * i + f, :], w[:, k, c, f * FC:(f + 1) * FC], xgT[:, u, c, :], start=c == 0, stop=c == 1)
                last.then_inc(h_ready, 1)

            def down(e, k):
                u = k % 2
                pe.wait_ge(h_done, e + 1)
                wait(pe, y_done, e - 1)
                for f in range(2):
                    last = nc.tensor.matmul(ps_y[u][:], hT[:, u, f, :], wd[:, k, f, :], start=f == 0, stop=f == 1)
                last.then_inc(y_ready, 1)

            walk(pe, E, B, B, [(2, turn), (3, gate_up), (4, down)])

        @block.scalar
        def _(act):
            def copy_x(e, k):
                u = k % 2
                act.wait_ge(x_turned, e + 1)
                wait(act, h_ready, e - 1)
                nc.scalar.activation(xgT[:, u], ps_x[u][:], ACT.Copy).then_inc(xT_done, 1)

            def silu(e, k):
                u = k % 2
                act.wait_ge(h_ready, e + 1)
                wait(act, h_done, e - 1)
                nc.scalar.activation(act_g[:, u], ps_h[u][0:FC, 0:2, :], ACT.Silu).then_inc(silu_done, 1)

            walk(act, E, B, B, [(2, copy_x), (3, silu)])

        @block.vector
        def _(dve):
            def hidden(e, k):
                u = k % 2
                dve.wait_ge(silu_done, e + 1)
                wait(dve, y_ready, e - 1)
                nc.vector.tensor_tensor(hT[:, u], act_g[:, u], ps_h[u][0:FC, 2:4, :], ALU.mult).then_inc(h_done, 1)

            def weigh(e, k):
                u = k % 2
                dve.wait_ge(y_ready, e + 1)
                wait(dve, scattered, 16 * (e - B + 1))
                nc.vector.tensor_scalar(y[:, k, :], ps_y[u][:], xg[:, k, bass.ds(e + D, 1)], None, ALU.mult).then_inc(y_done, 1)

            walk(dve, E, B, B, [(3, hidden), (4, weigh)])


def forget_attention(nc, x_in, x_out, w, bias, const):
    import concourse.bass as bass
    from concourse import mybir
    from contextlib import ExitStack
    fp32 = mybir.dt.float32
    ALU, ACT = mybir.AluOpType, mybir.ActivationFunctionType
    P, D, H, DK, B = 128, 256, 16, 16, 8
    STEPS, COLS, GROUPS = 16, 8, 64
    VW = 2 * DK
    VF = D + H
    L_ROWS = 10
    L_NORM, L_TURN, L_PROJ, L_BIAS, L_NEG, L_EXP, L_PHI = 1, 2, 3, 4, 5, 6, 7
    L_QK, L_BD, L_LOG, L_LSUM, L_DECAY, L_EXPAND, L_S, L_PV, L_COPY, L_OUT, L_ATT = 8, 9, 8, 9, 9, 10, 11, 12, 13, 13, 14

    with ExitStack() as ctx:
        def sb(name, shape, dt=fp32):
            return ctx.enter_context(nc.sbuf_tensor("b_" + name, shape, dt))

        def pb(name, shape, dt=fp32):
            return ctx.enter_context(nc.psum_tensor("b_" + name, shape, dt))

        def sem(name):
            return nc.alloc_semaphore("b_" + name)

        w_rows = sb("w_rows", [P, 8, D])
        f_rows = sb("f_rows", [H, D])
        w_qk = sb("w_qk", [P, 2, 2 * D])
        w_vf = sb("w_vf", [P, 2, VF])
        w_o = sb("w_o", [P, 2, D])
        b_qk = sb("b_qk", [P, 2 * D])
        b_vf = sb("b_vf", [P, VF])
        b_o = sb("b_o", [P, D])
        ident = sb("ident", [P, P])
        later = sb("later", [P, P])
        upto = sb("upto", [P, STEPS])
        own = sb("own", [P, P])
        head_rows = sb("head_rows", [P, COLS])
        minus_half = sb("minus_half", [P, 1])
        eps = sb("eps", [P, 1])
        xt = sb("xt", [P, B, D])
        stats = sb("stats", [P, B, 6])
        mean_var = sb("mean_var", [P, B, 2])
        var_eps = sb("var_eps", [P, B, 1])
        rstd = sb("rstd", [P, B, 1])
        xn = sb("xn", [P, B, D])
        xnT = sb("xnT", [P, B, 2, P])
        z_qk = sb("z_qk", [P, B, 2 * D])
        e_qk = sb("e_qk", [P, 2, 2 * D])
        phi = sb("phi", [P, 2, 2 * D])
        v_aug = sb("v_aug", [P, B, H, VW])
        z_f = sb("z_f", [P, B, H])
        low_f = sb("low_f", [P, B, H])
        abs_f = sb("abs_f", [P, B, H])
        log_f = sb("log_f", [P, B, H])
        log_upto = sb("log_upto", [P, 2, H, STEPS])
        decay = sb("decay", [P, 2, H, STEPS])
        spread = sb("spread", [P, 2, H, STEPS, COLS])
        q_bd = sb("q_bd", [P, 2, 2, COLS, P])
        kT = sb("kT", [P, 4, 2, P])
        weight = sb("weight", [P, 2, H, P])
        o_sb = sb("o_sb", [P, 2, 4 * P])
        den = sb("den", [P, 2, H])
        att = sb("att", [P, 2, D])
        attT = sb("attT", [P, 2, 2, P])
        xr = sb("xr", [P, B, D])
        xo = sb("xo", [P, B, D])
        ps_xl = pb("ps_xl", [P, 2, 2 * P])
        ps_qk = pb("ps_qk", [P, 2 * D])
        ps_vf = pb("ps_vf", [P, VF])
        ps_t = pb("ps_t", [P, 4, P])
        ps_s = [pb(f"ps_s{u}", [P, 4, P]) for u in range(2)]
        ps_o = pb("ps_o", [P, 4, P])
        ps_w = pb("ps_w", [P, 4, P])

        const_in, setup, w_turned, w_copied = (sem(n) for n in ("const_in", "setup", "w_turned", "w_copied"))
        x_loaded = [sem(f"x_loaded{k}") for k in range(B)]
        xr_loaded = [sem(f"xr_loaded{k}") for k in range(B)]
        stored = [sem(f"stored{k}") for k in range(B)]
        (stats_done, mv_done, ve_done, rstd_done, xn_done, x_turned, xnT_done, qk_ready, vf_ready, qk_biased, v_biased, f_biased,
         neg_done, low_done, abs_done, exp_done, f_exp_done, f_log_done, phi_done, log_done, qk_turned, bd_done, kT_done, upto_done,
         sums_ready, decay_done, spread_done, s_ready, weight_done, o_ready, o_copied, o_turned, den_done, att_done, att_turned,
         attT_done, out_ready, rows_ready, added) = (sem(n) for n in (
             "stats_done", "mv_done", "ve_done", "rstd_done", "xn_done", "x_turned", "xnT_done", "qk_ready", "vf_ready", "qk_biased",
             "v_biased", "f_biased", "neg_done", "low_done", "abs_done", "exp_done", "f_exp_done", "f_log_done", "phi_done", "log_done",
             "qk_turned", "bd_done", "kT_done", "upto_done", "sums_ready", "decay_done", "spread_done", "s_ready", "weight_done",
             "o_ready", "o_copied", "o_turned", "den_done", "att_done", "att_turned", "attT_done", "out_ready", "rows_ready", "added"))
        dve_passed = sem("dve_passed")
        block = ctx.enter_context(nc.Block())
        N_CONST = 4 + 1 + 6 + 5

        def group_rows(t, n):
            return t.rearrange("(s c) d -> s c d", s=STEPS)[:, bass.ds(n * COLS, COLS), :]

        @block.sync
        def _(sp):
            for i, m in enumerate((w["q"], w["k"], w["v"], w["o"])):
                sp.dma_start(w_rows[:, 2 * i:2 * i + 2, :], m.rearrange("(c p) d -> p c d", p=P)).then_inc(const_in, 16)
            sp.dma_start(f_rows[:], w["f"]).then_inc(const_in, 16)
            for tile, lo, b in ((b_qk, 0, "q"), (b_qk, D, "k"), (b_vf, 0, "v"), (b_vf, D, "f"), (b_o, 0, "o")):
                n = bias[b].shape[0]
                sp.dma_start(tile[:, lo:lo + n], bias[b].rearrange("(o n) -> o n", o=1).to_broadcast([P, n])).then_inc(const_in, 16)
            for tile, name in ((ident, "ident"), (later, "later"), (upto, "upto"), (own, "own"), (head_rows, "head_rows")):
                sp.dma_start(tile[:], const[name]).then_inc(const_in, 16)

            def load(n, k):
                wait(sp, xn_done, n - B + 1)
                sp.dma_start(xt[:, k, :], group_rows(x_in, n)).then_inc(x_loaded[k], 16)

            def load_rows(n, k):
                wait(sp, added, n - B + 1)
                sp.dma_start(xr[:, k, :], group_rows(x_in, n)).then_inc(xr_loaded[k], 16)

            def store(n, k):
                sp.wait_ge(added, n + 1)
                sp.dma_start(group_rows(x_out, n), xo[:, k, :]).then_inc(stored[k], 16)

            walk(sp, GROUPS, B, B, [(0, load), (L_ROWS, load_rows), (L_ATT + 1, store)])
            for k in range(B):
                sp.wait_ge(stored[k], 16 * GROUPS // B)

        @block.gpsimd
        def _(pool):
            nc.gpsimd.memset(minus_half[:], -0.5).then_inc(setup, 1)
            nc.gpsimd.memset(eps[:], 1e-5).then_inc(setup, 1)
            nc.gpsimd.memset(v_aug[:], 0.0).then_inc(setup, 1)
            pool.wait_ge(setup, 3)
            nc.gpsimd.memset(v_aug[:, :, :, DK:DK + 1], 1.0).then_inc(setup, 1)
            pool.wait_ge(const_in, 16 * (N_CONST - 1))

            def inverse_deviation(n, k):
                pool.wait_ge(mv_done, n + 1)
                nc.gpsimd.tensor_tensor(var_eps[:, k], mean_var[:, k, 1:2], eps[:], ALU.add).then_inc(ve_done, 1)
                pool.wait_ge(ve_done, n + 1)
                wait(pool, xn_done, n - B + 1)
                nc.gpsimd.tensor_tensor(rstd[:, k], var_eps[:, k], minus_half[:], ALU.pow).then_inc(rstd_done, 1)

            def log_gates(n, k):
                pool.wait_ge(log_done, n + 1)
                wait(pool, sums_ready, n - 1)
                nc.gpsimd.tensor_tensor(log_upto[:, k % 2], log_f[:, k, :].rearrange("p (h o) -> p h o", o=1).to_broadcast([P, H, STEPS]),
                                        upto[:].rearrange("p (o t) -> p o t", o=1).to_broadcast([P, H, STEPS]), ALU.mult).then_inc(upto_done, 1)

            def expand(n, k):
                pool.wait_ge(decay_done, n + 1)
                wait(pool, weight_done, 4 * (n - 1))
                nc.gpsimd.tensor_tensor(spread[:, k % 2].rearrange("p h t c -> p (h t) c"),
                                        decay[:, k % 2].rearrange("p h (t o) -> p (h t) o", o=1).to_broadcast([P, H * STEPS, COLS]),
                                        own[:].rearrange("p (o t) -> p o t", o=1).to_broadcast([P, H, P]), ALU.mult).then_inc(spread_done, 1)

            def rows(n, k):
                pool.wait_ge(xr_loaded[k], 16 * (turns(n, k, B) + 1))
                nc.gpsimd.tensor_tensor(xr[:, k, :], xr[:, k, :], b_o[:], ALU.add).then_inc(rows_ready, 1)

            walk(pool, GROUPS, B, B, [(0, inverse_deviation), (L_LOG, log_gates), (L_EXPAND, expand), (L_ATT - 1, rows)])

        @block.vector
        def _(dve):
            for i in range(5):
                dve.wait_ge(w_turned, i + 1)
                bank = (ps_t, ps_w)[i % 2]
                if i < 4:
                    dst = (w_qk[:, :, 0:D], w_qk[:, :, D:2 * D], w_vf[:, :, 0:D], w_o[:])[i]
                    nc.vector.tensor_copy(dst, bank[:].rearrange("p (c r) a -> p c (r a)", c=2)).then_inc(w_copied, 1)
                else:
                    nc.vector.tensor_copy(w_vf[:, :, D:VF], bank[:, 0:2, 0:H]).then_inc(w_copied, 1)
            dve.wait_ge(const_in, 16 * (N_CONST - 1))

            def statistics(n, k):
                dve.wait_ge(x_loaded[k], 16 * (turns(n, k, B) + 1))
                nc.vector.bn_stats(stats[:, k, :], xt[:, k, :]).then_inc(stats_done, 1)

            def aggregate(n, k):
                dve.wait_ge(stats_done, n + 1)
                passed_by(dve, dve_passed)
                nc.vector.bn_aggr(mean_var[:, k, :], stats[:, k, :]).then_inc(mv_done, 1)

            def normalise(n, k):
                dve.wait_ge(rstd_done, n + 1)
                wait(dve, x_turned, n - B + 1)
                nc.vector.tensor_scalar(xn[:, k, :], xt[:, k, :], mean_var[:, k, 0:1], rstd[:, k],
                                        ALU.subtract, ALU.mult).then_inc(xn_done, 1)

            def add_bias(n, k):
                dve.wait_ge(qk_ready, n + 1)
                nc.vector.tensor_tensor(z_qk[:, k, :], ps_qk[:], b_qk[:], ALU.add).then_inc(qk_biased, 1)
                dve.wait_ge(vf_ready, n + 1)
                if isinstance(n, int) and n == 0:
                    dve.wait_ge(setup, 4)
                wait(dve, o_ready, n - B + 1)
                nc.vector.tensor_tensor(v_aug[:, k, :, 0:DK], ps_vf[:, 0:D].rearrange("p (h d) -> p h d", d=DK),
                                        b_vf[:, 0:D].rearrange("p (h d) -> p h d", d=DK), ALU.add).then_inc(v_biased, 1)
                nc.vector.tensor_tensor(z_f[:, k, :], ps_vf[:, D:VF], b_vf[:, D:VF], ALU.add).then_inc(f_biased, 1)

            def negative_part(n, k):
                dve.wait_ge(qk_biased, n + 1)
                dve.wait_ge(f_biased, n + 1)
                wait(dve, phi_done, n - 1)
                nc.vector.tensor_scalar(e_qk[:, k % 2, :], z_qk[:, k, :], 0.0, None, ALU.min).then_inc(neg_done, 1)
                nc.vector.tensor_scalar(low_f[:, k, :], z_f[:, k, :], 0.0, None, ALU.min).then_inc(low_done, 1)
                dve.wait_ge(low_done, n + 1)
                nc.vector.scalar_tensor_tensor(abs_f[:, k, :], low_f[:, k, :], 2.0, z_f[:, k, :], ALU.mult, ALU.subtract).then_inc(abs_done, 1)

            def features(n, k):
                dve.wait_ge(exp_done, n + 1)
                wait(dve, qk_turned, n - 1)
                nc.vector.scalar_tensor_tensor(phi[:, k % 2, :], z_qk[:, k, :], 0.0, e_qk[:, k % 2, :], ALU.max, ALU.add).then_inc(phi_done, 1)
                dve.wait_ge(f_log_done, n + 1)
                nc.vector.tensor_tensor(log_f[:, k, :], low_f[:, k, :], abs_f[:, k, :], ALU.subtract).then_inc(log_done, 1)

            def block_queries(n, k):
                dve.wait_ge(kT_done, n + 1)
                wait(dve, s_ready, 4 * (n - 1))
                for half in range(2):
                    last = nc.vector.tensor_tensor(q_bd[:, k % 2, half], ps_t[:, half, :].rearrange("p (o t) -> p o t", o=1).to_broadcast([P, COLS, P]),
                                                   head_rows[:].rearrange("p (j o) -> p j o", o=1).to_broadcast([P, COLS, P]), ALU.mult)
                last.then_inc(bd_done, 1)

            def weigh(i):
                def stage(n, k):
                    dve.wait_ge(s_ready, 4 * n + i + 1)
                    if i == 0:
                        dve.wait_ge(spread_done, n + 1)
                        wait(dve, o_ready, n - 1)
                    heads = slice(4 * i, 4 * i + 4)
                    nc.vector.tensor_tensor(weight[:, k % 2, heads, :], ps_s[i % 2][:], spread[:, k % 2, heads].rearrange("p h t c -> p h (t c)"),
                                            ALU.mult).then_inc(weight_done, 1)
                return stage

            def divide(n, k):
                dve.wait_ge(o_turned, n + 1)
                heads = ps_w[:].rearrange("p i (j w) -> p (i j) w", w=VW)
                nc.vector.tensor_scalar(den[:, k % 2, :], heads[:, :, DK], 1e-6, None, ALU.add).then_inc(den_done, 1)
                dve.wait_ge(den_done, 2 * n + 1)
                nc.vector.reciprocal(den[:, k % 2, :], den[:, k % 2, :]).then_inc(den_done, 1)
                dve.wait_ge(den_done, 2 * n + 2)
                wait(dve, att_turned, n - 1)
                nc.vector.tensor_tensor(att[:, k % 2, :].rearrange("p (h d) -> p h d", d=DK), heads[:, :, 0:DK],
                                        den[:, k % 2, :].rearrange("p (h o) -> p h o", o=1).to_broadcast([P, H, DK]), ALU.mult).then_inc(att_done, 1)

            def add(n, k):
                dve.wait_ge(out_ready, n + 1)
                dve.wait_ge(rows_ready, n + 1)
                wait(dve, stored[k], 16 * turns(n, k, B))
                nc.vector.tensor_tensor(xo[:, k, :], ps_w[:].rearrange("p i a -> p (i a)")[:, D:2 * D], xr[:, k, :], ALU.add).then_inc(added, 1)

            walk(dve, GROUPS, B, B, [(0, statistics), (L_S, weigh(0)), (L_S, weigh(1)), (L_ATT, add), (L_NORM, normalise), (L_S, weigh(2)),
                                     (L_BIAS, add_bias), (L_S, weigh(3)), (L_PHI, features), (L_NEG, negative_part), (L_BD, block_queries),
                                     (0, aggregate), (L_OUT, divide)])

        @block.scalar
        def _(act):
            def evacuate_x(n, k):
                act.wait_ge(x_turned, n + 1)
                wait(act, vf_ready, n - B + 1)
                nc.scalar.activation(xnT[:, k], ps_xl[:, 0, :].rearrange("p (c t) -> p c t", c=2), ACT.Copy).then_inc(xnT_done, 1)

            def exponentials(n, k):
                act.wait_ge(neg_done, n + 1)
                nc.scalar.activation(e_qk[:, k % 2, :], e_qk[:, k % 2, :], ACT.Exp).then_inc(exp_done, 1)
                act.wait_ge(abs_done, n + 1)
                nc.scalar.activation(abs_f[:, k, :], abs_f[:, k, :], ACT.Exp).then_inc(f_exp_done, 1)
                act.wait_ge(f_exp_done, n + 1)
                nc.scalar.activation(abs_f[:, k, :], abs_f[:, k, :], ACT.Ln, bias=1.0).then_inc(f_log_done, 1)

            def copy_keys(n, k):
                act.wait_ge(qk_turned, n + 1)
                wait(act, s_ready, 4 * (n - 3))
                nc.scalar.activation(kT[:, k % 4], ps_t[:, 2:4, :], ACT.Copy).then_inc(kT_done, 1)

            def decays(n, k):
                act.wait_ge(sums_ready, n + 1)
                wait(act, spread_done, n - 1)
                nc.scalar.activation(decay[:, k % 2].rearrange("p h t -> p (h t)"), ps_xl[:, 1, :], ACT.Exp).then_inc(decay_done, 1)

            def copy_output(n, k):
                act.wait_ge(o_ready, n + 1)
                wait(act, o_turned, n - 1)
                nc.scalar.activation(o_sb[:, k % 2, :], ps_o[:].rearrange("p i a -> p (i a)"), ACT.Copy).then_inc(o_copied, 1)

            def copy_att(n, k):
                act.wait_ge(att_turned, n + 1)
                wait(act, out_ready, n - 1)
                nc.scalar.activation(attT[:, k % 2], ps_w[:, 0:2, :], ACT.Copy).then_inc(attT_done, 1)

            walk(act, GROUPS, B, B, [(L_EXP, exponentials), (L_ATT, copy_att), (L_COPY, copy_output), (L_TURN, evacuate_x),
                                     (L_QK, copy_keys), (L_DECAY, decays)])

        @block.tensor
        def _(pe):
            pe.wait_ge(const_in, 16 * N_CONST - 16)
            for i in range(5):
                wait(pe, w_copied, i - 1)
                bank = (ps_t, ps_w)[i % 2]
                for c in range(2):
                    if i < 4:
                        for r in range(2):
                            last = nc.tensor.transpose(bank[:, 2 * c + r, :], w_rows[:, 2 * i + r, c * P:(c + 1) * P], ident[:])
                    else:
                        last = nc.tensor.transpose(bank[:, c, 0:H], f_rows[:, c * P:(c + 1) * P], ident[0:H, 0:H])
                last.then_inc(w_turned, 1)
            pe.wait_ge(w_copied, 5)

            def turn_x(n, k):
                pe.wait_ge(xn_done, n + 1)
                wait(pe, xnT_done, n)
                wait(pe, decay_done, n + L_TURN - L_LSUM)
                for c in range(2):
                    last = nc.tensor.transpose(ps_xl[:, 0, c * P:(c + 1) * P], xn[:, k, c * P:(c + 1) * P], ident[:])
                last.then_inc(x_turned, 1)

            def project(n, k):
                pe.wait_ge(xnT_done, n + 1)
                wait(pe, qk_biased, n)
                for c in range(2):
                    last = nc.tensor.matmul(ps_qk[:], xnT[:, k, c, :], w_qk[:, c, :], start=c == 0, stop=c == 1)
                last.then_inc(qk_ready, 1)
                wait(pe, f_biased, n)
                wait(pe, v_biased, n)
                for c in range(2):
                    last = nc.tensor.matmul(ps_vf[:], xnT[:, k, c, :], w_vf[:, c, :], start=c == 0, stop=c == 1)
                last.then_inc(vf_ready, 1)

            def turn_qk(n, k):
                pe.wait_ge(phi_done, n + 1)
                wait(pe, bd_done, n)
                wait(pe, kT_done, n)
                for g in range(4):
                    last = nc.tensor.transpose(ps_t[:, g, :], phi[:, k % 2, g * P:(g + 1) * P], ident[:])
                last.then_inc(qk_turned, 1)

            def sum_logs(n, k):
                pe.wait_ge(upto_done, n + 1)
                seen = n + L_LSUM - L_TURN + 1
                pe.wait_ge(xnT_done, min(seen, GROUPS) if isinstance(seen, int) else seen)
                nc.tensor.matmul(ps_xl[:, 1, :], later[:], log_upto[:, k % 2].rearrange("p h t -> p (h t)"), start=True, stop=True).then_inc(sums_ready, 1)

            def scores(i):
                def stage(n, k):
                    if i == 0:
                        pe.wait_ge(bd_done, n + 1)
                        pe.wait_ge(kT_done, n + 1)
                    wait(pe, weight_done, 4 * n + i - 1)
                    half, quarter = i // 2, i % 2
                    nc.tensor.matmul(ps_s[i % 2][:], kT[:, k % 4, half, :], q_bd[:, k % 2, half, 4 * quarter:4 * quarter + 4, :],
                                     start=True, stop=True).then_inc(s_ready, 1)
                return stage

            def mix_values(n, k):
                pe.wait_ge(weight_done, 4 * n + 4)
                wait(pe, o_copied, n)
                for i in range(4):
                    for j in range(4):
                        h = 4 * i + j
                        last = nc.tensor.matmul(ps_o[VW * j:VW * (j + 1), i, :], v_aug[:, k, h, :], weight[:, k % 2, h, :], start=True, stop=True)
                last.then_inc(o_ready, 1)

            def turn_output(n, k):
                pe.wait_ge(o_copied, n + 1)
                wait(pe, added, n)
                for i in range(4):
                    last = nc.tensor.transpose(ps_w[:, i, :], o_sb[:, k % 2, i * P:(i + 1) * P], ident[:])
                last.then_inc(o_turned, 1)

            def turn_att(n, k):
                pe.wait_ge(att_done, n + 1)
                for c in range(2):
                    last = nc.tensor.transpose(ps_w[:, c, :], att[:, k % 2, c * P:(c + 1) * P], ident[:])
                last.then_inc(att_turned, 1)

            def project_out(n, k):
                pe.wait_ge(attT_done, n + 1)
                out = ps_w[:].rearrange("p i a -> p (i a)")[:, D:2 * D]
                for c in range(2):
                    last = nc.tensor.matmul(out, attT[:, k % 2, c, :], w_o[:, c, :], start=c == 0, stop=c == 1)
                last.then_inc(out_ready, 1)

            walk(pe, GROUPS, B, B, [(L_ATT, turn_att), (L_S, scores(0)), (L_PV, mix_values), (L_S, scores(1)), (L_ATT, project_out), (L_S, scores(2)), (L_TURN, turn_x),
                                    (L_PROJ, project), (L_S, scores(3)), (L_QK, turn_qk), (L_OUT, turn_output), (L_LSUM, sum_logs)])


def program(nc, a):
    from concourse import mybir
    fp32, bf16, u32 = mybir.dt.float32, mybir.dt.bfloat16, mybir.dt.uint32
    P, D, T, E, SEQS, S, H, VW = 128, 256, 8192, 64, 16, 512, 16, 32
    SPARE = P

    def scratch(name, shape, dt=fp32):
        return nc.dram_tensor(name, shape, dt).ap()

    split = {"parts": scratch("parts", (SEQS, 12, P, S), bf16), "v_aug": scratch("v_aug", (T, H * VW))}
    routed = {"rows": scratch("rows", (T + SPARE, D + E)), "turned": scratch("turned", (D, T))}
    x0 = a["L0_attn_a_x"].rearrange("b s d -> (b s) d")
    x1, x3 = scratch("x1", (T, D)), scratch("x3", (T, D))
    x2 = scratch("x2", (T + SPARE, D))

    def mixture(tag, x_in, x_out):
        with nc.sbuf_tensor(tag + "_order", [P, T // 2], fp32) as order, nc.sbuf_tensor(tag + "_slots", [P, E], u32) as slots:
            const = dict(a, order=order, slots=slots)
            with nc.cleanup_on_exit():
                moe_route(nc, tag, routed, x_in, a["L0_ffn_router_w"], const)
            with nc.cleanup_on_exit():
                moe_shared(nc, tag, routed, x_in, x_out, a["L0_ffn_ws_gate_up"], a["L0_ffn_ws_down"], const)
            with nc.cleanup_on_exit():
                moe_experts(nc, tag, routed, x_out, a["L0_ffn_w_gate"], a["L0_ffn_w_up"], a["L0_ffn_w_down"], const)

    with nc.cleanup_on_exit():
        attention_project(nc, split, x0, a["L0_attn_a_Wq"], a["L0_attn_a_Wk"], a["L0_attn_a_Wv"], a)
    with nc.cleanup_on_exit():
        attention_mix(nc, split, x0, x1, a["L0_attn_a_Wo"], a)
    mixture("m1", x1, x2)
    with nc.cleanup_on_exit():
        forget_attention(nc, x2[0:T, :], x3, {m: a["L0_attn_b_W" + m] for m in "qkvfo"}, {m: a["L0_attn_b_b" + m] for m in "qkvfo"}, a)
    mixture("m2", x3, a["out"])


_INS = ["L0_attn_a_x", "L0_attn_a_Wq", "L0_attn_a_Wk", "L0_attn_a_Wv", "L0_attn_a_Wo", "L0_attn_b_Wq", "L0_attn_b_bq", "L0_attn_b_Wk",
        "L0_attn_b_bk", "L0_attn_b_Wv", "L0_attn_b_bv", "L0_attn_b_Wf", "L0_attn_b_bf", "L0_attn_b_Wo", "L0_attn_b_bo",
        "L0_ffn_router_w", "L0_ffn_w_gate", "L0_ffn_w_up", "L0_ffn_w_down", "L0_ffn_ws_gate_up", "L0_ffn_ws_down"]


def constants():
    P, S, DK, T = 128, 512, 16, 8192
    p = np.arange(P)
    angle = np.arange(S, dtype=np.float32)[:, None] * (1.0 / 10000.0 ** (np.arange(0, DK, 2, dtype=np.float32) / DK)).astype(np.float32)
    by_tile = lambda t: t.reshape(S // P, P, DK).transpose(1, 0, 2)
    item = np.arange(T // P)
    tile = item % 2 * (T // P // 2) + item // 2
    step, col = p // 8, p % 8
    tables = {
        "ident": np.eye(P),
        "cos": by_tile(np.concatenate([np.cos(angle), np.cos(angle)], 1)),
        "sin": by_tile(np.concatenate([-np.sin(angle), np.sin(angle)], 1)),
        "rank_value": T - (tile[None, :] * P + p[:, None]),
        "spare_row": p[:, None],
        "later": (col[:, None] == col) & (step[:, None] > step),
        "upto": step[:, None] <= np.arange(16),
        "own": (col[:, None] == col) & (step[:, None] <= step),
        "head_rows": p[:, None] // DK == np.arange(P // DK),
    }
    return {name: np.ascontiguousarray(t, dtype=np.float32) for name, t in tables.items()}


def kernel(**inputs):
    import concourse.bacc as _bacc
    from concourse import mybir as _mybir
    from concourse.bass_utils import run_bass_kernel_spmd as _run

    nc = _bacc.Bacc("TRN2", target_bir_lowering=False, num_devices=1)
    data = {name: np.ascontiguousarray(inputs[name]) for name in _INS}
    data.update(constants())
    arrays, a = {}, {}
    for name, t in data.items():
        arrays[f"in_{name}_dram"] = t
        a[name] = nc.dram_tensor(f"in_{name}_dram", t.shape, _mybir.dt.from_np(t.dtype), kind="ExternalInput").ap()
    tokens, features = 16 * 512, 256
    a["out"] = nc.dram_tensor("out_0_dram", (tokens + 128, features), _mybir.dt.float32, kind="ExternalOutput").ap()
    program(nc, a)
    r = _run(nc, [arrays], core_ids=[0])
    return r.results[0]["out_0_dram"][:tokens].reshape(16, 512, features)
```

```python
import numpy as np


def wait(eng, sem, value):
    if not isinstance(value, int) or value > 0:
        eng.wait_ge(sem, value)


def passed_by(eng, passed):
    eng.sem_inc(passed, 1)


def walk(eng, total, trip, look_back, stages):
    deepest = max(lag for lag, _ in stages)
    lead = trip * -(-(deepest + look_back) // trip)

    def step(s, k, peeled):
        for lag, stage in stages:
            if not peeled or 0 <= s - lag < total:
                stage(s - lag, (k - lag) % trip)

    for s in range(lead):
        step(s, s % trip, True)
    with eng.Fori(lead // trip, total // trip) as i:
        for k in range(trip):
            step(i * trip + k, k, False)
    for s in range(total, total + deepest):
        step(s, s % trip, True)


def turns(n, k, trip):
    return n // trip if isinstance(n, int) else (n - k) // trip


def attention_project(nc, dram, x_in, wq, wk, wv, const):
    import concourse.bass as bass
    from concourse import mybir
    from contextlib import ExitStack
    fp32, bf16 = mybir.dt.float32, mybir.dt.bfloat16
    ALU, ACT = mybir.AluOpType, mybir.ActivationFunctionType
    P, D, H, DK = 128, 256, 16, 16
    TPB = 4
    SEQS = 16
    TILES = SEQS * TPB
    HALF = DK // 2

    with ExitStack() as ctx:
        def sb(name, shape, dt=fp32):
            return ctx.enter_context(nc.sbuf_tensor("a1_" + name, shape, dt))

        def pb(name, shape, dt=fp32):
            return ctx.enter_context(nc.psum_tensor("a1_" + name, shape, dt))

        def sem(name):
            return nc.alloc_semaphore("a1_" + name)

        w_rows = sb("w_rows", [P, 6, D])
        w_qk = sb("w_qk", [P, 2, 2 * D])
        w_v = sb("w_v", [P, 2, D])
        ident = sb("ident", [P, P])
        cos = sb("cos", [P, TPB, DK])
        sin = sb("sin", [P, TPB, DK])
        minus_half = sb("minus_half", [P, 1])
        eps = sb("eps", [P, 1])
        xt = sb("xt", [P, TPB, D])
        stats = sb("stats", [P, 2, 6])
        mean_var = sb("mean_var", [P, TPB, 2])
        var_eps = sb("var_eps", [P, 2, 1])
        rstd = sb("rstd", [P, TPB, 1])
        xn = sb("xn", [P, TPB, D])
        xnT = sb("xnT", [P, 2, 2, P])
        rot_cos = sb("rot_cos", [P, 2, 2 * D])
        rot_sin = sb("rot_sin", [P, 2, 2 * D])
        qk = sb("qk", [P, 2, 2 * D])
        v_aug = sb("v_aug", [P, 2, H, 2 * DK])
        rest = sb("rest", [P, 2, 2 * D])
        parts = sb("parts", [P, TPB, 3, 4, P], bf16)
        ps_x = pb("ps_x", [P, 2, P])
        ps_qk = [pb(f"ps_qk{u}", [P, 2 * D]) for u in range(2)]
        ps_v = [pb(f"ps_v{u}", [P, D]) for u in range(2)]
        ps_t = [pb(f"ps_t{u}", [P, 4, P]) for u in range(2)]

        const_in, w_turned, w_copied, setup = sem("const_in"), sem("w_turned"), sem("w_copied"), sem("setup")
        x_loaded = [sem(f"x_loaded{u}") for u in range(TPB)]
        stats_done, mv_done, ve_done, rstd_done, xn_done = (sem(n) for n in ("stats_done", "mv_done", "ve_done", "rstd_done", "xn_done"))
        x_turned, xnT_done, qk_projected, v_projected, v_copied = (sem(n) for n in ("x_turned", "xnT_done", "qk_projected", "v_projected", "v_copied"))
        rot_done, qk_done, qk_turned, high_done, rest_done, mid_done, low_done = (sem(n) for n in (
            "rot_done", "qk_done", "qk_turned", "high_done", "rest_done", "mid_done", "low_done"))
        v_stored = [sem(f"v_stored{u}") for u in range(2)]
        parts_stored = [sem(f"parts_stored{u}") for u in range(TPB)]
        dve_passed = sem("dve_passed")
        block = ctx.enter_context(nc.Block())

        @block.sync
        def _(sp):
            for i, w in enumerate((wq, wk, wv)):
                sp.dma_start(w_rows[:, 2 * i:2 * i + 2, :], w.rearrange("(c p) d -> p c d", p=P)).then_inc(const_in, 16)
            sp.dma_start(ident[:], const["ident"]).then_inc(const_in, 16)
            sp.dma_start(cos[:], const["cos"]).then_inc(const_in, 16)
            sp.dma_start(sin[:], const["sin"]).then_inc(const_in, 16)

            def load(n, j):
                u = j % 2
                wait(sp, xn_done, n - 3)
                sp.dma_start(xt[:, j, :], x_in[bass.ds(n * P, P), :]).then_inc(x_loaded[j], 16)

            def store_parts(n, j):
                u = j % 2
                sp.wait_ge(low_done, n + 1)
                sp.wait_ge(mid_done, n + 1)
                sp.wait_ge(high_done, n + 1)
                sp.dma_start(dram["parts"][turns(n, j, TPB)].rearrange("(k g) p t -> p k g t", k=3)[:, :, :, j * P:(j + 1) * P],
                             parts[:, j]).then_inc(parts_stored[j], 16)

            walk(sp, TILES, TPB, TPB, [(0, load), (8, store_parts)])
            for j in range(TPB):
                sp.wait_ge(parts_stored[j], 16 * SEQS)

        @block.gpsimd
        def _(pool):
            nc.gpsimd.memset(minus_half[:], -0.5).then_inc(setup, 1)
            nc.gpsimd.memset(eps[:], 1e-5).then_inc(setup, 1)
            nc.gpsimd.memset(v_aug[:], 0.0).then_inc(setup, 1)
            pool.wait_ge(setup, 3)
            nc.gpsimd.memset(v_aug[:, :, :, DK:DK + 1], 1.0).then_inc(setup, 1)

            def inverse_deviation(n, j):
                u = j % 2
                pool.wait_ge(mv_done, n + 1)
                nc.gpsimd.tensor_tensor(var_eps[:, u], mean_var[:, j, 1:2], eps[:], ALU.add).then_inc(ve_done, 1)
                pool.wait_ge(ve_done, n + 1)
                nc.gpsimd.tensor_tensor(rstd[:, j], var_eps[:, u], minus_half[:], ALU.pow).then_inc(rstd_done, 1)

            def split(n, j):
                u = j % 2
                pool.wait_ge(mid_done, n + 1)
                nc.gpsimd.tensor_tensor(parts[:, j, 2], rest[:, u, :].rearrange("p (g t) -> p g t", g=4), parts[:, j, 1],
                                        ALU.subtract).then_inc(low_done, 1)

            walk(pool, TILES, TPB, TPB, [(0, inverse_deviation), (7, split)])

        @block.vector
        def _(dve):
            for i in range(6):
                dve.wait_ge(w_turned, i + 1)
                for c in range(2):
                    dst = w_qk[:, c, i * P:(i + 1) * P] if i < 4 else w_v[:, c, (i - 4) * P:(i - 3) * P]
                    last = nc.vector.tensor_copy(dst, ps_t[i % 2][:, c, :])
                last.then_inc(w_copied, 1)

            def statistics(n, j):
                u = j % 2
                dve.wait_ge(x_loaded[j], 16 * (turns(n, j, TPB) + 1))
                nc.vector.bn_stats(stats[:, u, :], xt[:, j, :]).then_inc(stats_done, 1)
                dve.wait_ge(stats_done, n + 1)
                wait(dve, xn_done, n - 3)
                passed_by(dve, dve_passed)
                nc.vector.bn_aggr(mean_var[:, j, :], stats[:, u, :]).then_inc(mv_done, 1)

            def normalise(n, j):
                u = j % 2
                dve.wait_ge(rstd_done, n + 1)
                wait(dve, x_turned, n - 3)
                nc.vector.tensor_scalar(xn[:, j, :], xt[:, j, :], mean_var[:, j, 0:1], rstd[:, j],
                                        ALU.subtract, ALU.mult).then_inc(xn_done, 1)

            def rotate(n, j):
                u = j % 2
                if j == 0 and isinstance(n, int) and n == 0:
                    dve.wait_ge(const_in, 16 * 6)
                dve.wait_ge(qk_projected, n + 1)
                heads = ps_qk[u][:].rearrange("p (h d) -> p h d", d=DK)
                turned = rot_sin[:, u, :].rearrange("p (h d) -> p h d", d=DK)
                cos_b = cos[:, j, :].rearrange("p (o d) -> p o d", o=1).to_broadcast([P, 2 * H, DK])
                nc.vector.tensor_tensor(rot_cos[:, u, :].rearrange("p (h d) -> p h d", d=DK), heads, cos_b, ALU.mult)
                for part in range(2):
                    dims = slice(part * HALF, (part + 1) * HALF)
                    sin_b = sin[:, j, dims].rearrange("p (o d) -> p o d", o=1).to_broadcast([P, 2 * H, HALF])
                    last = nc.vector.tensor_tensor(turned[:, :, dims], heads[:, :, 1 - part::2], sin_b, ALU.mult)
                last.then_inc(rot_done, 1)
                dve.wait_ge(rot_done, n + 1)
                wait(dve, qk_turned, n - 1)
                nc.vector.tensor_tensor(qk[:, u, :], rot_cos[:, u, :], rot_sin[:, u, :], ALU.add).then_inc(qk_done, 1)

            def remainder(n, j):
                u = j % 2
                dve.wait_ge(high_done, n + 1)
                wait(dve, low_done, n - 1)
                nc.vector.tensor_tensor(rest[:, u, :].rearrange("p (g t) -> p g t", g=4), ps_t[u][:], parts[:, j, 0],
                                        ALU.subtract).then_inc(rest_done, 1)

            walk(dve, TILES, TPB, TPB, [(0, statistics), (4, rotate), (6, remainder), (1, normalise)])

        @block.scalar
        def _(act):
            def evacuate_x(n, j):
                u = j % 2
                act.wait_ge(x_turned, n + 1)
                wait(act, v_projected, n - 1)
                nc.scalar.activation(xnT[:, u], ps_x[:], ACT.Copy).then_inc(xnT_done, 1)

            def evacuate_v(n, j):
                u = j % 2
                act.wait_ge(v_projected, n + 1)
                if isinstance(n, int) and n == 0:
                    act.wait_ge(setup, 4)
                wait(act, v_stored[u], 16 * turns(n, u, 2))
                nc.scalar.activation(v_aug[:, u, :, 0:DK], ps_v[u][:].rearrange("p (h d) -> p h d", d=DK), ACT.Copy).then_inc(v_copied, 1)
                act.wait_ge(v_copied, n + 1)
                act.dma_start(dram["v_aug"][bass.ds(n * P, P), :], v_aug[:, u].rearrange("p h d -> p (h d)")).then_inc(v_stored[u], 16)

            def high(n, j):
                u = j % 2
                act.wait_ge(qk_turned, n + 1)
                wait(act, parts_stored[j], 16 * turns(n, j, TPB))
                nc.scalar.activation(parts[:, j, 0], ps_t[u][:], ACT.Copy).then_inc(high_done, 1)

            def middle(n, j):
                u = j % 2
                act.wait_ge(rest_done, n + 1)
                nc.scalar.activation(parts[:, j, 1], rest[:, u, :].rearrange("p (g t) -> p g t", g=4), ACT.Copy).then_inc(mid_done, 1)

            walk(act, TILES, TPB, TPB, [(7, middle), (2, evacuate_x), (3, evacuate_v), (5, high)])
            for u in range(2):
                act.wait_ge(v_stored[u], 16 * TILES // 2)

        @block.tensor
        def _(pe):
            pe.wait_ge(const_in, 16 * 6)
            for i in range(6):
                wait(pe, w_copied, i - 1)
                for c in range(2):
                    last = nc.tensor.transpose(ps_t[i % 2][:, c, :], w_rows[:, i, c * P:(c + 1) * P], ident[:])
                last.then_inc(w_turned, 1)
            pe.wait_ge(w_copied, 6)

            def turn_x(n, j):
                u = j % 2
                pe.wait_ge(xn_done, n + 1)
                wait(pe, xnT_done, n)
                for c in range(2):
                    last = nc.tensor.transpose(ps_x[:, c, :], xn[:, j, c * P:(c + 1) * P], ident[:])
                last.then_inc(x_turned, 1)

            def project(n, j):
                u = j % 2
                pe.wait_ge(xnT_done, n + 1)
                wait(pe, rot_done, n - 1)
                for c in range(2):
                    last = nc.tensor.matmul(ps_qk[u][:], xnT[:, u, c, :], w_qk[:, c, :], start=c == 0, stop=c == 1)
                last.then_inc(qk_projected, 1)
                wait(pe, v_copied, n - 1)
                for c in range(2):
                    last = nc.tensor.matmul(ps_v[u][:], xnT[:, u, c, :], w_v[:, c, :], start=c == 0, stop=c == 1)
                last.then_inc(v_projected, 1)

            def turn_qk(n, j):
                u = j % 2
                pe.wait_ge(qk_done, n + 1)
                wait(pe, rest_done, n - 1)
                for g in range(4):
                    last = nc.tensor.transpose(ps_t[u][:, g, :], qk[:, u, g * P:(g + 1) * P], ident[:])
                last.then_inc(qk_turned, 1)

            walk(pe, TILES, TPB, TPB, [(2, turn_x), (3, project), (5, turn_qk)])


def attention_mix(nc, dram, x_in, x_out, wo, const):
    import concourse.bass as bass
    from concourse import mybir
    from contextlib import ExitStack
    fp32, bf16 = mybir.dt.float32, mybir.dt.bfloat16
    ALU, ACT, AX = mybir.AluOpType, mybir.ActivationFunctionType, mybir.AxisListType
    P, D, H, DK, S = 128, 256, 16, 16, 512
    SEQS, QT = 16, S // P
    PERIOD = 2 * H
    Q_PARTS = (0, 0, 1, 1, 0, 2)
    K_PARTS = (0, 1, 0, 1, 2, 0)
    SLOTS = len(Q_PARTS)
    K_MAX = SLOTS * DK
    K_ALL = K_MAX + 2
    HALF = H // 2
    VW = 2 * DK
    L_TURN, L_MSPLIT, L_S, L_PV, L_OCOPY, L_OTURN, L_ONORM = 1, 2, 12, 17, 18, 19, 20
    L_ATT = L_ONORM + 1

    with ExitStack() as ctx:
        def sb(name, shape, dt=fp32):
            return ctx.enter_context(nc.sbuf_tensor("a2_" + name, shape, dt))

        def pb(name, shape, dt=fp32):
            return ctx.enter_context(nc.psum_tensor("a2_" + name, shape, dt))

        def sem(name):
            return nc.alloc_semaphore("a2_" + name)

        wo_rows = sb("wo_rows", [P, 2, D])
        woT = sb("woT", [P, 2, D])
        ident = sb("ident", [P, P])
        qs = [sb(f"qs{u}", [P, H, S], bf16) for u in range(2)]
        ks = [sb(f"ks{u}", [P, H, S], bf16) for u in range(2)]
        va = [sb(f"va{u}", [P, QT, H * VW]) for u in range(2)]
        xr = [sb(f"xr{u}", [P, QT, D]) for u in range(2)]
        row_max = sb("row_max", [P, 2, QT, H])
        m_parts = sb("m_parts", [HALF, 2, 2, S], bf16)
        probs = sb("probs", [P, 2, 4, QT, S])
        o_sb = sb("o_sb", [P, 2, S])
        rden = sb("rden", [P, 2, QT, 4])
        att = sb("att", [P, 2, QT, D])
        attT = sb("attT", [P, 2, 4, P])
        xo = sb("xo", [P, 2, 2, D])
        ps_m = [pb(f"ps_m{u}", [P, S]) for u in range(2)]
        ps_s = [pb(f"ps_s{u}", [P, 2, S]) for u in range(2)]
        ps_o = pb("ps_o", [P, S])
        ps_w = pb("ps_w", [P, 4, P])

        const_in, w_turned, w_copied, ones_set = sem("const_in"), sem("w_turned"), sem("w_copied"), sem("ones_set")
        qk_loaded = [[sem(f"qk_loaded{u}{f}") for f in range(2)] for u in range(2)]
        va_loaded = [sem(f"va_loaded{u}") for u in range(2)]
        xr_loaded = [sem(f"xr_loaded{u}") for u in range(2)]
        m_loaded = [sem(f"m_loaded{f}") for f in range(2)]
        max_ready, max_done, m_turned, m_high, m_low = (sem(n) for n in ("max_ready", "max_done", "m_turned", "m_high", "m_low"))
        s_ready, exp_done, pv_done, o_copied, o_turned, rden_done, o_normed = (sem(n) for n in (
            "s_ready", "exp_done", "pv_done", "o_copied", "o_turned", "rden_done", "o_normed"))
        att_turned, attT_done, projected, added = (sem(n) for n in ("att_turned", "attT_done", "projected", "added"))
        stored = [sem(f"stored{q}") for q in range(2)]
        block = ctx.enter_context(nc.Block())

        class Head:

            def __init__(self, base, k):
                self.base, self.k = base, k
                self.h, self.u = k % H, k // H % 2

            def count(self, per_period, extra):
                return self.base * per_period + extra

        def uses(step, first, period=PERIOD):
            n = -((first - step.k) // period)
            n = step.base * (PERIOD // period) + n
            return min(max(0, n), SEQS * H // period) if isinstance(n, int) else n

        def walk(eng, stages):
            deepest = max(lag for lag, _ in stages)
            total = SEQS * H

            def step(base, k, peeled):
                for lag, stage in stages:
                    if peeled and not 0 <= PERIOD * base + k - lag < total:
                        continue
                    stage(Head(base, k - lag), Head(base, k))

            for k in range(PERIOD):
                step(0, k, True)
            with eng.Fori(1, SEQS // 2) as base:
                for k in range(PERIOD):
                    step(base, k, False)
            for k in range(deepest):
                step(SEQS // 2, k, True)

        A_TURN = (H - 1 + L_ATT, H - 1 + L_ATT + 8)
        A_PROJ = (H - 1 + L_ATT + 1, H - 1 + L_ATT + 9)

        def ps_w_free(pe, step):
            wait(pe, m_low, uses(step, HALF - 1 + L_TURN, HALF))
            wait(pe, o_normed, uses(step, 3 + L_OTURN, 4))
            wait(pe, attT_done, uses(step, A_TURN[0], H) + uses(step, A_TURN[1], H))
            wait(pe, added, uses(step, A_PROJ[0], H) + uses(step, A_PROJ[1], H))

        @block.sync
        def _(sp):
            sp.dma_start(wo_rows[:], wo.rearrange("(c p) d -> p c d", p=P)).then_inc(const_in, 16)
            sp.dma_start(ident[:], const["ident"]).then_inc(const_in, 16)

            def load_qk(b, u, f):
                wait(sp, s_ready, 2 * (H * (b - 2) + HALF * (f + 1)))
                heads = slice(f * HALF, (f + 1) * HALF)
                for tiles, parts_of, half in ((qs, Q_PARTS, 0), (ks, K_PARTS, 2)):
                    for slot, part in enumerate(parts_of):
                        src = dram["parts"][b, 4 * part + half + f].rearrange("(h d) t -> d h t", d=DK)
                        sp.dma_start(tiles[u][slot * DK:(slot + 1) * DK, heads, :], src).then_inc(qk_loaded[u][f], 16)

            def load_m(b, u, f):
                wait(sp, m_low, 2 * b + f + 1)
                wait(sp, m_high, 2 * b + f + 1)
                heads = slice(f * HALF, (f + 1) * HALF)
                for part in range(2):
                    sp.dma_start(qs[u][K_MAX + part:K_MAX + part + 1, heads, :], m_parts[:, f, part, :]).then_inc(m_loaded[f], 16)

            def sequence(b, u, last):
                load_m(b, u, 0)
                wait(sp, pv_done, H * (b - 1))
                rows = x_rows(dram["v_aug"], b)
                sp.dma_start(va[u][:], rows).then_inc(va_loaded[u], 16)
                if not last:
                    for f in range(2):
                        load_qk(b + 1, 1 - u, f)
                load_m(b, u, 1)
                wait(sp, added, 2 * (b - 1))
                sp.dma_start(xr[u][:], x_rows(x_in, b)).then_inc(xr_loaded[u], 16)

            def x_rows(t, b):
                return t[bass.ds(b * S, S), :].rearrange("(t p) d -> p t d", p=P)

            for f in range(2):
                load_qk(0, 0, f)
            sequence(0, 0, False)
            sequence(1, 1, False)
            with sp.Fori(1, SEQS // 2 - 1) as i:
                for u in range(2):
                    sequence(2 * i + u, u, False)
            sequence(SEQS - 2, 0, False)
            sequence(SEQS - 1, 1, True)

        @block.gpsimd
        def _(pool):
            for u in range(2):
                last = nc.gpsimd.memset(ks[u][K_MAX:K_ALL, :, :], 1.0)
            last.then_inc(ones_set, 1)

            def store(b):
                for q in range(2):
                    pool.wait_ge(added, 2 * b + q + 1)
                    pool.dma_start(x_out[bass.ds(b * S + q * 2 * P, 2 * P), :].rearrange("(t p) d -> p t d", p=P), xo[:, q]).then_inc(stored[q], 16)

            with pool.Fori(0, SEQS) as b:
                store(b)
            for q in range(2):
                pool.wait_ge(stored[q], 16 * SEQS)

        @block.tensor
        def _(pe):
            pe.wait_ge(const_in, 32)
            for i in range(2):
                wait(pe, w_copied, i)
                for c in range(2):
                    last = nc.tensor.transpose(ps_w[:, c, :], wo_rows[:, i, c * P:(c + 1) * P], ident[:])
                last.then_inc(w_turned, 1)
            pe.wait_ge(w_copied, 2)

            def max_products(t):
                def stage(n, step):
                    u, h = n.u, n.h
                    if h % HALF == 0 and t == 0:
                        pe.wait_ge(qk_loaded[u][h // HALF], 16 * 2 * SLOTS * (n.base + 1))
                    wait(pe, max_done, n.count(QT * PERIOD, QT * n.k + t - 1))
                    nc.tensor.matmul(ps_m[t % 2][:], qs[u][0:K_MAX, h, t * P:(t + 1) * P], ks[u][0:K_MAX, h, :],
                                     start=True, stop=True).then_inc(max_ready, 1)
                return stage

            def turn_max(n, step):
                if n.h % HALF != HALF - 1:
                    return
                pe.wait_ge(max_done, n.count(QT * PERIOD, QT * (n.k + 1)))
                ps_w_free(pe, step)
                h0 = n.h - HALF + 1
                for t in range(QT):
                    last = nc.tensor.transpose(ps_w[0:HALF, t, :], row_max[:, n.u, t, h0:h0 + HALF], ident[:])
                last.then_inc(m_turned, 1)

            def scores(half):
                def stage(n, step):
                    u, h = n.u, n.h
                    if isinstance(n.base, int) and n.base == 0 and n.k == 0:
                        pe.wait_ge(ones_set, 1)
                    if h % HALF == 0 and half == 0:
                        pe.wait_ge(m_loaded[h // HALF], n.count(64, 32 * (n.k // H + 1)))
                    wait(pe, exp_done, n.count(2 * PERIOD, 2 * n.k + half - 1))
                    for i in range(2):
                        t = 2 * half + i
                        last = nc.tensor.matmul(ps_s[half][:, i, :], ks[u][0:K_ALL, h, t * P:(t + 1) * P], qs[u][0:K_ALL, h, :],
                                                start=True, stop=True)
                    last.then_inc(s_ready, 1)
                return stage

            def mix_values(first):
                def stage(n, step):
                    if (n.h % 4 == 0) != first:
                        return
                    t = n.h % 4
                    group = n.k // 4
                    if t == 0:
                        pe.wait_ge(exp_done, n.count(2 * PERIOD, 2 * n.k + 8))
                        wait(pe, o_copied, n.count(PERIOD // 4, group))
                        if n.h == 0:
                            pe.wait_ge(va_loaded[n.u], n.count(16, 16 * (n.k // PERIOD + 1)))
                    for j in range(4):
                        h = n.h - t + j
                        last = nc.tensor.matmul(ps_o[VW * j:VW * (j + 1), :], va[n.u][:, t, h * VW:(h + 1) * VW],
                                                probs[:, group % 2, j, t, :], start=t == 0, stop=t == QT - 1)
                    last.then_inc(pv_done, 1)
                return stage

            def turn_output(n, step):
                if n.h % 4 != 3:
                    return
                group = n.k // 4
                pe.wait_ge(o_copied, n.count(PERIOD // 4, group + 1))
                ps_w_free(pe, step)
                for t in range(QT):
                    last = nc.tensor.transpose(ps_w[:, t, :], o_sb[:, group % 2, t * P:(t + 1) * P], ident[:])
                last.then_inc(o_turned, 1)

            def turn_att(q):
                def stage(n, step):
                    if n.h != H - 1:
                        return
                    pe.wait_ge(o_normed, n.count(PERIOD // 4, n.k // 4 + 1))
                    ps_w_free(pe, step)
                    for t in range(2):
                        for c in range(2):
                            last = nc.tensor.transpose(ps_w[:, 2 * t + c, :], att[:, n.u, 2 * q + t, c * P:(c + 1) * P], ident[:])
                    last.then_inc(att_turned, 1)
                return stage

            def project(q):
                def stage(n, step):
                    if n.h != H - 1:
                        return
                    pe.wait_ge(attT_done, n.count(4, 2 * (n.k // H) + q + 1))
                    ps_w_free(pe, step)
                    out = ps_w[:].rearrange("p a b -> p (a b)")
                    for t in range(2):
                        for c in range(2):
                            last = nc.tensor.matmul(out[:, t * D:(t + 1) * D], attT[:, q, 2 * t + c, :], woT[:, c, :], start=c == 0, stop=c == 1)
                    last.then_inc(projected, 1)
                return stage

            walk(pe, [(0, max_products(0)), (L_S, scores(0)), (0, max_products(1)), (L_PV, mix_values(False)), (0, max_products(2)),
                      (L_S, scores(1)), (0, max_products(3)), (L_PV, mix_values(True)), (L_TURN, turn_max), (L_OTURN, turn_output),
                      (A_TURN[0] - H + 1, turn_att(0)), (A_PROJ[0] - H + 1, project(0)),
                      (A_TURN[1] - H + 1, turn_att(1)), (A_PROJ[1] - H + 1, project(1))])

        @block.vector
        def _(dve):
            for i in range(2):
                dve.wait_ge(w_turned, i + 1)
                for c in range(2):
                    last = nc.vector.tensor_copy(woT[:, c, i * P:(i + 1) * P], ps_w[:, c, :])
                last.then_inc(w_copied, 1)

            def maxima(half):
                def stage(n, step):
                    for t in (2 * half, 2 * half + 1):
                        dve.wait_ge(max_ready, n.count(QT * PERIOD, QT * n.k + t + 1))
                        nc.vector.tensor_reduce(row_max[:, n.u, t, n.h:n.h + 1], ps_m[t % 2][:], AX.X, ALU.max).then_inc(max_done, 1)
                return stage

            def low_max(n, step):
                if n.h % HALF != HALF - 1:
                    return
                f = n.h // HALF
                dve.wait_ge(m_high, n.count(4, n.k // HALF + 1))
                nc.vector.scalar_tensor_tensor(m_parts[:, f, 1, :], ps_w[0:HALF].rearrange("p a b -> p (a b)"), -1.0, m_parts[:, f, 0, :],
                                               ALU.mult, ALU.subtract).then_inc(m_low, 1)

            def normalise(n, step):
                if n.h % 4 != 3:
                    return
                group = n.k // 4
                dve.wait_ge(o_turned, n.count(PERIOD // 4, group + 1))
                heads = ps_w[:].rearrange("p t (j w) -> p t j w", w=VW)
                nc.vector.reciprocal(rden[:, group % 2], heads[:, :, :, DK]).then_inc(rden_done, 1)
                dve.wait_ge(rden_done, n.count(PERIOD // 4, group + 1))
                h0 = n.h - 3
                dst = att[:, n.u, :, h0 * DK:(h0 + 4) * DK].rearrange("p t (j d) -> p t j d", d=DK)
                over = rden[:, group % 2].rearrange("p t (j o) -> p t j o", o=1).to_broadcast([P, QT, 4, DK])
                nc.vector.tensor_tensor(dst, heads[:, :, :, 0:DK], over, ALU.mult).then_inc(o_normed, 1)

            def residual(q):
                def stage(n, step):
                    if n.h != H - 1:
                        return
                    dve.wait_ge(projected, n.count(4, 2 * (n.k // H) + q + 1))
                    if q == 0:
                        dve.wait_ge(xr_loaded[n.u], n.count(16, 16 * (n.k // PERIOD + 1)))
                    wait(dve, stored[q], n.count(32, 16 * (n.k // H)))
                    out = ps_w[:].rearrange("p a b -> p (a b)").rearrange("p (t d) -> p t d", d=D)
                    nc.vector.tensor_tensor(xo[:, q], out, xr[n.u][:, 2 * q:2 * q + 2, :], ALU.add).then_inc(added, 1)
                return stage

            walk(dve, [(0, maxima(0)), (L_MSPLIT, low_max), (A_PROJ[0] - H + 2, residual(0)), (A_PROJ[1] - H + 2, residual(1)),
                       (L_ONORM, normalise), (0, maxima(1))])

        @block.scalar
        def _(act):
            def high_max(n, step):
                if n.h % HALF != HALF - 1:
                    return
                f = n.h // HALF
                act.wait_ge(m_turned, n.count(4, n.k // HALF + 1))
                wait(act, m_loaded[f], n.count(64, 32 * (n.k // H)))
                nc.scalar.activation(m_parts[:, f, 0, :], ps_w[0:HALF].rearrange("p a b -> p (a b)"), ACT.Copy, scale=-1.0).then_inc(m_high, 1)

            def exponentials(n, step):
                group = n.k // 4
                if n.h % 4 == 0:
                    wait(act, pv_done, n.count(PERIOD, n.k - 4))
                for half in range(2):
                    act.wait_ge(s_ready, n.count(2 * PERIOD, 2 * n.k + half + 1))
                    nc.scalar.activation(probs[:, group % 2, n.h % 4, 2 * half:2 * half + 2, :], ps_s[half][:], ACT.Exp,
                                         scale=DK ** -0.5).then_inc(exp_done, 1)

            def copy_output(n, step):
                if n.h % 4 != 3:
                    return
                group = n.k // 4
                act.wait_ge(pv_done, n.count(PERIOD, n.k + 1))
                wait(act, o_turned, n.count(PERIOD // 4, group - 1))
                nc.scalar.activation(o_sb[:, group % 2, :], ps_o[:], ACT.Copy).then_inc(o_copied, 1)

            def copy_att(q):
                def stage(n, step):
                    if n.h != H - 1:
                        return
                    act.wait_ge(att_turned, n.count(4, 2 * (n.k // H) + q + 1))
                    nc.scalar.activation(attT[:, q], ps_w[:], ACT.Copy).then_inc(attT_done, 1)
                return stage

            walk(act, [(L_MSPLIT, high_max), (A_TURN[0] - H + 2, copy_att(0)), (A_TURN[1] - H + 2, copy_att(1)), (L_OCOPY, copy_output),
                       (L_S, exponentials)])


def moe_route(nc, tag, dram, x_in, router_w, const):
    import concourse.bass as bass
    from concourse import mybir
    from contextlib import ExitStack
    fp32 = mybir.dt.float32
    ALU, ACT, AX = mybir.AluOpType, mybir.ActivationFunctionType, mybir.AxisListType
    P, D, T, E, B = 128, 256, 8192, 64, 4
    TILES = T // P
    order = const["order"]
    x_rows, x_turned_all = const["x_rows"], const["x_turned"]

    with ExitStack() as ctx:
        def sb(name, shape, dt=fp32):
            return ctx.enter_context(nc.sbuf_tensor(f"{tag}r_" + name, shape, dt))

        def pb(name, shape, dt=fp32):
            return ctx.enter_context(nc.psum_tensor(f"{tag}r_" + name, shape, dt))

        def sem(name):
            return nc.alloc_semaphore(f"{tag}r_" + name)

        rw_rows = sb("rw_rows", [E, D])
        rwT = sb("rwT", [P, 2, E])
        ident = sb("ident", [P, P])
        rank_value = sb("rank_value", [P, TILES])
        minus_half = sb("minus_half", [P, 1])
        eps = sb("eps", [P, 1])
        zeros = sb("zeros", [P, D + E])
        stats = sb("stats", [P, B, 6])
        mean_var = sb("mean_var", [P, B, 2])
        var_eps = sb("var_eps", [P, B, 1])
        rstd = sb("rstd", [P, B, 1])
        xn = sb("xn", [P, B, D])
        xnT = sb("xnT", [P, B, 2, P])
        top_logit = sb("top_logit", [P, B, 1])
        logit = sb("logit", [P, B, E])
        expd = sb("expd", [P, B, E])
        top8 = sb("top8", [P, B, 8])
        marked = sb("marked", [P, B, E])
        value = sb("value", [P, B, E])
        picked = sb("picked", [P, B, E])
        total = sb("total", [P, B, 1])
        gate = sb("gate", [P, B, E])
        ps_x = [pb(f"ps_x{u}", [P, 2, P]) for u in range(2)]
        ps_l = [pb(f"ps_l{u}", [P, E]) for u in range(2)]
        ps_v = [pb(f"ps_v{u}", [P, P]) for u in range(2)]

        const_in, setup, w_turned, w_copied, pad_stored = (sem(n) for n in ("const_in", "setup", "w_turned", "w_copied", "pad_stored"))
        x_loaded = [sem(f"x_loaded{k}") for k in range(B)]
        xn_stored = [sem(f"xn_stored{k}") for k in range(B)]
        gate_stored = [sem(f"gate_stored{k}") for k in range(B)]
        (stats_done, mv_done, ve_done, rstd_done, xn_done, x_turned, xnT_done, xnT_kept, logits_ready, top_done, logit_done, exp_done, top8_done,
         marked_done, value_done, picked_done, recip_done, gate_done, value_turned, order_done) = (sem(n) for n in (
             "stats_done", "mv_done", "ve_done", "rstd_done", "xn_done", "x_turned", "xnT_done", "xnT_kept", "logits_ready", "top_done", "logit_done",
             "exp_done", "top8_done", "marked_done", "value_done", "picked_done", "recip_done", "gate_done", "value_turned", "order_done"))
        dve_passed = sem("dve_passed")
        block = ctx.enter_context(nc.Block())
        MARK = -1e30

        def tile(n, k):
            return k % 2 * (TILES // 2) + turns(n, k % 2, 2)

        def rows(t, n, k):
            return t[bass.ds(tile(n, k) * P, P), :]

        @block.sync
        def _(sp):
            sp.dma_start(rw_rows[:], router_w).then_inc(const_in, 16)
            sp.dma_start(ident[:], const["ident"]).then_inc(const_in, 16)
            sp.dma_start(rank_value[:], const["rank_value"]).then_inc(const_in, 16)
            sp.wait_ge(setup, 3)
            sp.dma_start(dram["rows"][T:T + P, :], zeros[:]).then_inc(pad_stored, 16)

            def load(n, k):
                wait(sp, x_loaded[k], 16 * turns(n, k, B))
                sp.dma_start(x_rows[:, bass.ds(tile(n, k), 1), :], rows(x_in, n, k)).then_inc(x_loaded[k], 16)

            def store_rows(n, k):
                sp.wait_ge(xn_done, n + 1)
                sp.dma_start(rows(dram["rows"], n, k)[:, 0:D], xn[:, k, :]).then_inc(xn_stored[k], 16)

            def store_gates(n, k):
                sp.wait_ge(gate_done, n + 1)
                sp.dma_start(rows(dram["rows"], n, k)[:, D:D + E], gate[:, k, :]).then_inc(gate_stored[k], 16)

            walk(sp, TILES, B, B, [(0, load), (8, store_rows), (16, store_gates)])
            sp.wait_ge(pad_stored, 16)
            for k in range(B):
                sp.wait_ge(xn_stored[k], 16 * TILES // B)
                sp.wait_ge(gate_stored[k], 16 * TILES // B)

        @block.gpsimd
        def _(pool):
            nc.gpsimd.memset(minus_half[:], -0.5).then_inc(setup, 1)
            nc.gpsimd.memset(eps[:], 1e-5).then_inc(setup, 1)
            nc.gpsimd.memset(zeros[:], 0.0).then_inc(setup, 1)
            pool.wait_ge(setup, 3)

            def inverse_deviation(n, k):
                pool.wait_ge(mv_done, n + 1)
                nc.gpsimd.tensor_tensor(var_eps[:, k], mean_var[:, k, 1:2], eps[:], ALU.add).then_inc(ve_done, 1)
                pool.wait_ge(ve_done, n + 1)
                wait(pool, xn_done, n - B + 1)
                nc.gpsimd.tensor_tensor(rstd[:, k], var_eps[:, k], minus_half[:], ALU.pow).then_inc(rstd_done, 1)

            walk(pool, TILES, B, B, [(0, inverse_deviation)])

        @block.vector
        def _(dve):
            dve.wait_ge(w_turned, 1)
            nc.vector.tensor_copy(rwT[:], ps_x[0][:, :, 0:E]).then_inc(w_copied, 1)
            dve.wait_ge(const_in, 48)

            def statistics(n, k):
                dve.wait_ge(x_loaded[k], 16 * (turns(n, k, B) + 1))
                nc.vector.bn_stats(stats[:, k, :], x_rows[:, bass.ds(tile(n, k), 1), :]).then_inc(stats_done, 1)

            def aggregate(n, k):
                dve.wait_ge(stats_done, n + 1)
                passed_by(dve, dve_passed)
                nc.vector.bn_aggr(mean_var[:, k, :], stats[:, k, :]).then_inc(mv_done, 1)

            def normalise(n, k):
                dve.wait_ge(rstd_done, n + 1)
                wait(dve, x_turned, n - B + 1)
                wait(dve, xn_stored[k], 16 * turns(n, k, B))
                nc.vector.tensor_scalar(xn[:, k, :], x_rows[:, bass.ds(tile(n, k), 1), :], mean_var[:, k, 0:1], rstd[:, k],
                                        ALU.subtract, ALU.mult).then_inc(xn_done, 1)

            def maximum(n, k):
                dve.wait_ge(logits_ready, n + 1)
                nc.vector.tensor_reduce(top_logit[:, k], ps_l[k % 2][:], AX.X, ALU.max).then_inc(top_done, 1)

            def shift(n, k):
                dve.wait_ge(top_done, n + 1)
                wait(dve, exp_done, n - B + 1)
                nc.vector.tensor_scalar(logit[:, k, :], ps_l[k % 2][:], top_logit[:, k], -104.0, ALU.subtract, ALU.max).then_inc(logit_done, 1)

            def eight_largest(n, k):
                dve.wait_ge(logit_done, n + 1)
                passed_by(dve, dve_passed)
                nc.vector.max(top8[:, k, :], logit[:, k, :]).then_inc(top8_done, 1)

            def mark(n, k):
                dve.wait_ge(top8_done, n + 1)
                passed_by(dve, dve_passed)
                nc.vector.match_replace(marked[:, k, :], top8[:, k, :], logit[:, k, :], MARK).then_inc(marked_done, 1)

            def values(n, k):
                dve.wait_ge(marked_done, n + 1)
                wait(dve, value_turned, n - B + 1)
                nc.vector.tensor_scalar(value[:, k, :], marked[:, k, :], MARK / 2, rank_value[:, bass.ds(n, 1)], ALU.is_lt, ALU.mult).then_inc(value_done, 1)

            def pick(n, k):
                dve.wait_ge(exp_done, n + 1)
                dve.wait_ge(marked_done, n + 1)
                wait(dve, gate_done, n - B + 1)
                nc.vector.scalar_tensor_tensor(picked[:, k, :], marked[:, k, :], MARK / 2, expd[:, k, :], ALU.is_lt, ALU.mult,
                                               accum_out=total[:, k]).then_inc(picked_done, 1)

            def invert(n, k):
                dve.wait_ge(picked_done, n + 1)
                nc.vector.reciprocal(total[:, k], total[:, k]).then_inc(recip_done, 1)

            walk(dve, TILES, B, B, [(0, statistics), (10, invert), (9, pick), (9, values), (8, mark), (7, eight_largest),
                                    (0, aggregate), (6, shift), (5, maximum), (1, normalise)])

        @block.scalar
        def _(act):
            def evacuate_x(n, k):
                act.wait_ge(x_turned, n + 1)
                wait(act, logits_ready, n - B + 1)
                nc.scalar.activation(xnT[:, k], ps_x[k % 2][:], ACT.Copy).then_inc(xnT_done, 1)
                nc.scalar.activation(x_turned_all[:, :, bass.ds(tile(n, k) * P, P)], ps_x[k % 2][:], ACT.Copy).then_inc(xnT_kept, 1)

            def gates(n, k):
                act.wait_ge(recip_done, n + 1)
                wait(act, gate_stored[k], 16 * turns(n, k, B))
                nc.scalar.activation(gate[:, k, :], picked[:, k, :], ACT.Copy, scale=total[:, k]).then_inc(gate_done, 1)

            def exponential(n, k):
                act.wait_ge(logit_done, n + 1)
                wait(act, picked_done, n - B + 1)
                nc.scalar.activation(expd[:, k, :], logit[:, k, :], ACT.Exp).then_inc(exp_done, 1)

            def put_order(n, k):
                act.wait_ge(value_turned, n + 1)
                half = slice(k % 2 * E, (k % 2 + 1) * E)
                nc.scalar.activation(order[half, bass.ds(turns(n, k % 2, 2) * P, P)], ps_v[k % 2][half, :], ACT.Copy).then_inc(order_done, 1)

            walk(act, TILES, B, B, [(3, evacuate_x), (7, exponential), (11, put_order), (11, gates)])
            act.wait_ge(order_done, TILES)
            act.wait_ge(xnT_kept, TILES)

        @block.tensor
        def _(pe):
            pe.wait_ge(const_in, 48)
            for c in range(2):
                last = nc.tensor.transpose(ps_x[0][:, c, 0:E], rw_rows[:, c * P:(c + 1) * P], ident[0:E, 0:E])
            last.then_inc(w_turned, 1)
            pe.wait_ge(w_copied, 1)

            def turn_x(n, k):
                pe.wait_ge(xn_done, n + 1)
                wait(pe, xnT_kept, n - 1)
                for c in range(2):
                    last = nc.tensor.transpose(ps_x[k % 2][:, c, :], xn[:, k, c * P:(c + 1) * P], ident[:])
                last.then_inc(x_turned, 1)

            def logits(n, k):
                pe.wait_ge(xnT_done, n + 1)
                wait(pe, logit_done, n - 1)
                for c in range(2):
                    last = nc.tensor.matmul(ps_l[k % 2][:], xnT[:, k, c, :], rwT[:, c, :], start=c == 0, stop=c == 1)
                last.then_inc(logits_ready, 1)

            def turn_values(n, k):
                pe.wait_ge(value_done, n + 1)
                wait(pe, order_done, n - 1)
                half = slice(k % 2 * E, (k % 2 + 1) * E)
                nc.tensor.matmul(ps_v[k % 2][half, :], value[:, k, :], ident[:], start=True, stop=True).then_inc(value_turned, 1)

            walk(pe, TILES, B, B, [(3, turn_x), (4, logits), (10, turn_values)])


def moe_shared(nc, tag, x_out, ws_gate_up, ws_down, const):
    import concourse.bass as bass
    from concourse import mybir
    from contextlib import ExitStack
    fp32 = mybir.dt.float32
    ALU, ACT = mybir.AluOpType, mybir.ActivationFunctionType
    P, D, T, E, SF, CAP = 128, 256, 8192, 64, 192, 128
    SR = SF - P
    S = 512
    ROUNDS, B = CAP // 8, 4
    assert T // S == ROUNDS
    order, slots, x_rows, x_turned = const["order"], const["slots"], const["x_rows"], const["x_turned"]

    with ExitStack() as ctx:
        def sb(name, shape, dt=fp32):
            return ctx.enter_context(nc.sbuf_tensor(f"{tag}s_" + name, shape, dt))

        def pb(name, shape, dt=fp32):
            return ctx.enter_context(nc.psum_tensor(f"{tag}s_" + name, shape, dt))

        def sem(name):
            return nc.alloc_semaphore(f"{tag}s_" + name)

        w_gu = sb("w_gu", [P, 2, 3, P])
        w_d = sb("w_d", [P, 2, D])
        ident = sb("ident", [P, P])
        spare_row = sb("spare_row", [P, 1])
        act_g = sb("act_g", [P, 2, 2, S])
        up = sb("up", [P, 2, 2, S])
        hT = sb("hT", [P, 2, 2, S])
        xo = sb("xo", [P, 2, 4, D])
        top8 = sb("top8", [P, B, 8])
        first = sb("first", [P, CAP])
        merged = sb("merged", [E, 2 * CAP])
        best8 = sb("best8", [E, B, 8])
        best = sb("best", [E, CAP])
        empty = sb("empty", [P, E])
        number = sb("number", [P, E])
        ps_h = [[pb(f"ps_h{u}{i}", [P, S]) for i in range(3)] for u in range(2)]
        ps_d = [pb(f"ps_d{q}", [P, 2, D]) for q in range(2)]
        ps_t = ps_d[0][:, 0, 0:E]

        const_in = sem("const_in")
        stored = [sem(f"stored{u}") for u in range(2)]
        gated, silu_done, h_done, down_done, down_copied, added = (
            sem(n) for n in ("gated", "silu_done", "h_done", "down_done", "down_copied", "added"))
        top_found, top_kept, top_removed, halves_moved, best_found, best_kept, best_removed, best_turned, empty_done, number_done, slots_done = (
            sem(n) for n in ("top_found", "top_kept", "top_removed", "halves_moved", "best_found", "best_kept", "best_removed", "best_turned",
                             "empty_done", "number_done", "slots_done"))
        dve_passed = sem("dve_passed")
        block = ctx.enter_context(nc.Block())

        @block.sync
        def _(sp):
            gate_up = ws_gate_up.rearrange("(c p) (h f) -> p c h f", p=P, h=2)
            for h in range(2):
                sp.dma_start(w_gu[:, :, h, :], gate_up[:, :, h, 0:P]).then_inc(const_in, 16)
                sp.dma_start(w_gu[:, :, 2, h * SR:(h + 1) * SR], gate_up[:, :, h, P:SF]).then_inc(const_in, 16)
            sp.dma_start(w_d[:, 0, :], ws_down[0:P, :]).then_inc(const_in, 16)
            sp.dma_start(w_d[0:SR, 1, :], ws_down[P:SF, :]).then_inc(const_in, 16)
            sp.dma_start(ident[:], const["ident"]).then_inc(const_in, 16)
            sp.dma_start(spare_row[:], const["spare_row"]).then_inc(const_in, 16)

            def store(r, k):
                sp.wait_ge(added, 2 * (r + 1))
                sp.dma_start(x_out[bass.ds(r * S, S), :].rearrange("(t p) d -> p t d", p=P), xo[:, k % 2]).then_inc(stored[k % 2], 16)

            walk(sp, ROUNDS, B, B, [(0, store)])
            for u in range(2):
                sp.wait_ge(stored[u], 16 * ROUNDS // 2)

        @block.tensor
        def _(pe):
            pe.wait_ge(const_in, 128)

            def gate_up(r, k):
                wait(pe, silu_done, 2 * (r - 1))
                for i in range(3):
                    for c in range(2):
                        last = nc.tensor.matmul(ps_h[k % 2][i][:], w_gu[:, c, i, :], x_turned[:, c, bass.ds(r * S, S)], start=c == 0, stop=c == 1)
                    last.then_inc(gated, 1)

            def down(r, k):
                pe.wait_ge(h_done, 2 * (r + 1))
                for q in range(2):
                    wait(pe, down_copied, 2 * r + q - 1)
                    for t in range(2):
                        at = (2 * q + t) * P
                        nc.tensor.matmul(ps_d[q][:, t, :], hT[:, k % 2, 0, at:at + P], w_d[:, 0, :], start=True, stop=False)
                        last = nc.tensor.matmul(ps_d[q][:, t, :], hT[0:SR, k % 2, 1, at:at + P], w_d[0:SR, 1, :], start=False, stop=True)
                    last.then_inc(down_done, 1)

            walk(pe, ROUNDS, B, B, [(0, gate_up), (1, down)])
            pe.wait_ge(down_copied, 2 * ROUNDS)
            pe.wait_ge(best_kept, ROUNDS)
            nc.tensor.transpose(ps_t, best[:], ident[0:E, 0:E]).then_inc(best_turned, 1)

        @block.scalar
        def _(act):
            def silu(r, k):
                wait(act, h_done, 2 * (r - 1))
                act.wait_ge(gated, 3 * r + 1)
                nc.scalar.activation(act_g[:, k % 2, 0, :], ps_h[k % 2][0][:], ACT.Silu)
                act.wait_ge(gated, 3 * r + 2)
                nc.scalar.activation(up[:, k % 2, 0, :], ps_h[k % 2][1][:], ACT.Copy).then_inc(silu_done, 1)
                act.wait_ge(gated, 3 * r + 3)
                nc.scalar.activation(act_g[0:SR, k % 2, 1, :], ps_h[k % 2][2][0:SR, :], ACT.Silu)
                nc.scalar.activation(up[0:SR, k % 2, 1, :], ps_h[k % 2][2][SR:P, :], ACT.Copy).then_inc(silu_done, 1)

            def copy_down(r, k):
                wait(act, stored[k % 2], 16 * turns(r, k % 2, 2))
                for q in range(2):
                    act.wait_ge(down_done, 2 * r + q + 1)
                    nc.scalar.activation(xo[:, k % 2, 2 * q:2 * q + 2, :], ps_d[q][:], ACT.Copy).then_inc(down_copied, 1)

            def keep(r, k):
                act.wait_ge(top_found, r + 1)
                nc.scalar.activation(first[:, bass.ds(r * 8, 8)], top8[:, k, :], ACT.Copy).then_inc(top_kept, 1)

            def keep_best(r, k):
                act.wait_ge(best_found, r + 1)
                nc.scalar.activation(best[:, bass.ds(r * 8, 8)], best8[:, k, :], ACT.Copy).then_inc(best_kept, 1)

            walk(act, ROUNDS, B, B, [(0, silu), (1, keep), (1, copy_down)])
            walk(act, ROUNDS, B, B, [(0, keep_best)])

        @block.gpsimd
        def _(pool):
            def hidden(r, k):
                wait(pool, down_done, 2 * (r - 1))
                for i, n in enumerate((P, SR)):
                    pool.wait_ge(silu_done, 2 * r + i + 1)
                    nc.gpsimd.tensor_tensor(hT[0:n, k % 2, i, :], act_g[0:n, k % 2, i, :], up[0:n, k % 2, i, :], ALU.mult).then_inc(h_done, 1)

            def add(r, k):
                for q in range(2):
                    half = xo[:, k % 2, 2 * q:2 * q + 2, :]
                    pool.wait_ge(down_copied, 2 * r + q + 1)
                    nc.gpsimd.tensor_tensor(half, half, x_rows[:, bass.ds(r * 4 + 2 * q, 2), :], ALU.add).then_inc(added, 1)

            walk(pool, ROUNDS, B, B, [(0, hidden), (1, add)])

        @block.vector
        def _(dve):
            def find(r, k):
                wait(dve, top_removed, r)
                wait(dve, top_kept, r - B + 1)
                passed_by(dve, dve_passed)
                nc.vector.max(top8[:, k, :], order[:]).then_inc(top_found, 1)

            def remove(r, k):
                dve.wait_ge(top_found, r + 1)
                passed_by(dve, dve_passed)
                nc.vector.match_replace(order[:], top8[:, k, :], order[:], 0.0).then_inc(top_removed, 1)

            walk(dve, ROUNDS, B, B, [(0, find), (0, remove)])
            dve.wait_ge(const_in, 128)
            dve.wait_ge(top_kept, ROUNDS)
            for half in range(2):
                last = nc.vector.tensor_copy(merged[:, half * CAP:(half + 1) * CAP], first[half * E:(half + 1) * E, :])
            last.then_inc(halves_moved, 1)
            dve.wait_ge(halves_moved, 1)

            def find_best(r, k):
                wait(dve, best_removed, r)
                wait(dve, best_kept, r - B + 1)
                passed_by(dve, dve_passed)
                nc.vector.max(best8[:, k, :], merged[:]).then_inc(best_found, 1)

            def remove_best(r, k):
                dve.wait_ge(best_found, r + 1)
                passed_by(dve, dve_passed)
                nc.vector.match_replace(merged[:], best8[:, k, :], merged[:], 0.0).then_inc(best_removed, 1)

            walk(dve, ROUNDS, B, B, [(0, find_best), (0, remove_best)])
            dve.wait_ge(best_turned, 1)
            nc.vector.tensor_scalar(empty[:], ps_t, 0.5, spare_row[:], ALU.is_lt, ALU.mult).then_inc(empty_done, 1)
            nc.vector.tensor_scalar(number[:], ps_t, -1.0, float(T), ALU.mult, ALU.add).then_inc(number_done, 1)
            dve.wait_ge(empty_done, 1)
            dve.wait_ge(number_done, 1)
            nc.vector.tensor_tensor(slots[:], number[:], empty[:], ALU.add).then_inc(slots_done, 1)
            dve.wait_ge(slots_done, 1)


def moe_experts(nc, tag, dram, x_out, w_gate, w_up, w_down, const):
    import concourse.bass as bass
    from concourse import mybir
    from contextlib import ExitStack
    fp32, u32 = mybir.dt.float32, mybir.dt.uint32
    ALU, ACT = mybir.AluOpType, mybir.ActivationFunctionType
    P, D, T, E, F, B = 128, 256, 8192, 64, 192, 8
    FR = F - P
    slots = const["slots"]

    with ExitStack() as ctx:
        def sb(name, shape, dt=fp32):
            return ctx.enter_context(nc.sbuf_tensor(f"{tag}e_" + name, shape, dt))

        def pb(name, shape, dt=fp32):
            return ctx.enter_context(nc.psum_tensor(f"{tag}e_" + name, shape, dt))

        def sem(name):
            return nc.alloc_semaphore(f"{tag}e_" + name)

        ident = sb("ident", [P, P])
        w_gu = sb("w_gu", [P, B, 2, 2 * F])
        w_d = sb("w_d", [P, B, 2, D])
        index = sb("index", [P, B, 1], u32)
        xg = sb("xg", [P, B, D + E])
        xgT = sb("xgT", [P, 2, 2, P])
        act_g = sb("act_g", [P, 2, 2, P])
        hT = sb("hT", [P, 2, 2, P])
        y = sb("y", [P, B, D])
        ps_x = [pb(f"ps_x{u}", [P, 2, P]) for u in range(2)]
        ps_h = [pb(f"ps_h{u}", [P, 3, P]) for u in range(2)]
        ps_y = [pb(f"ps_y{u}", [P, D]) for u in range(2)]

        const_in = sem("const_in")
        w_loaded = [sem(f"w_loaded{k}") for k in range(B)]
        gathered = [sem(f"gathered{k}") for k in range(B)]
        index_done, x_turned, xT_done, h_ready, silu_done, h_done, y_ready, y_done, scattered = (sem(n) for n in (
            "index_done", "x_turned", "xT_done", "h_ready", "silu_done", "h_done", "y_ready", "y_done", "scattered"))
        pool_passed = sem("pool_passed")
        block = ctx.enter_context(nc.Block())

        @block.sync
        def _(sp):
            sp.dma_start(ident[:], const["ident"]).then_inc(const_in, 16)

            def load(e, k):
                wait(sp, y_ready, e - B + 1)
                for i, w in enumerate((w_gate, w_up)):
                    sp.dma_start(w_gu[:, k, :, i * F:(i + 1) * F], w[bass.ds(e, 1)].rearrange("o (c p) f -> p (o c) f", p=P)).then_inc(w_loaded[k], 16)
                sp.dma_start(w_d[:, k, 0:1, :], w_down[bass.ds(e, 1), 0:P].rearrange("o p d -> p o d")).then_inc(w_loaded[k], 16)
                sp.dma_start(w_d[0:FR, k, 1:2, :], w_down[bass.ds(e, 1), P:F].rearrange("o p d -> p o d")).then_inc(w_loaded[k], 16)

            walk(sp, E, B, B, [(0, load)])

        @block.gpsimd
        def _(pool):
            def gather(e, k):
                wait(pool, y_done, e - B + 1)
                nc.gpsimd.tensor_copy(index[:, k], slots[:, bass.ds(e, 1)]).then_inc(index_done, 1)
                pool.wait_ge(index_done, e + 1)
                passed_by(pool, pool_passed)
                pool.indirect_dma_start(xg[:, k, :], None, dram["rows"][:, :], bass.IndirectOffsetOnAxis(index[:, k], 0)).then_inc(gathered[k], 16)

            def scatter(e, k):
                pool.wait_ge(y_done, e + 1)
                wait(pool, scattered, 16 * e)
                passed_by(pool, pool_passed)
                pool.indirect_dma_start(x_out[:, :], bass.IndirectOffsetOnAxis(index[:, k], 0), y[:, k, :], None,
                                        compute_op=ALU.add).then_inc(scattered, 16)

            walk(pool, E, B, B, [(7, scatter), (0, gather)])
            pool.wait_ge(scattered, 16 * E)

        @block.tensor
        def _(pe):
            pe.wait_ge(const_in, 16)

            def turn(e, k):
                u = k % 2
                pe.wait_ge(gathered[k], 16 * (turns(e, k, B) + 1))
                wait(pe, xT_done, e - 1)
                for c in range(2):
                    last = nc.tensor.transpose(ps_x[u][:, c, :], xg[:, k, c * P:(c + 1) * P], ident[:])
                last.then_inc(x_turned, 1)

            def gate_up(e, k):
                u = k % 2
                pe.wait_ge(w_loaded[k], 64 * (turns(e, k, B) + 1))
                pe.wait_ge(xT_done, e + 1)
                wait(pe, h_done, e - 1)
                for i in range(3):
                    for c in range(2):
                        last = nc.tensor.matmul(ps_h[u][:, i, :], w_gu[:, k, c, i * P:(i + 1) * P], xgT[:, u, c, :], start=c == 0, stop=c == 1)
                last.then_inc(h_ready, 1)

            def down(e, k):
                u = k % 2
                pe.wait_ge(h_done, e + 1)
                wait(pe, y_done, e - 1)
                nc.tensor.matmul(ps_y[u][:], hT[:, u, 0, :], w_d[:, k, 0, :], start=True, stop=False)
                last = nc.tensor.matmul(ps_y[u][:], hT[0:FR, u, 1, :], w_d[0:FR, k, 1, :], start=False, stop=True)
                last.then_inc(y_ready, 1)

            walk(pe, E, B, B, [(2, turn), (3, gate_up), (4, down)])

        @block.scalar
        def _(act):
            def copy_x(e, k):
                u = k % 2
                act.wait_ge(x_turned, e + 1)
                wait(act, h_ready, e - 1)
                nc.scalar.activation(xgT[:, u], ps_x[u][:], ACT.Copy).then_inc(xT_done, 1)

            def silu(e, k):
                u = k % 2
                act.wait_ge(h_ready, e + 1)
                wait(act, h_done, e - 1)
                nc.scalar.activation(act_g[:, u, 0, :], ps_h[u][:, 0, :], ACT.Silu)
                nc.scalar.activation(act_g[0:FR, u, 1, :], ps_h[u][0:FR, 1, :], ACT.Silu).then_inc(silu_done, 1)

            walk(act, E, B, B, [(2, copy_x), (3, silu)])

        @block.vector
        def _(dve):
            def hidden(e, k):
                u = k % 2
                dve.wait_ge(silu_done, e + 1)
                wait(dve, y_ready, e - 1)
                nc.vector.tensor_tensor(hT[0:FR, u, 0, :], act_g[0:FR, u, 0, :], ps_h[u][FR:P, 1, :], ALU.mult)
                nc.vector.tensor_tensor(hT[FR:P, u, 0, :], act_g[FR:P, u, 0, :], ps_h[u][0:FR, 2, :], ALU.mult)
                nc.vector.tensor_tensor(hT[0:FR, u, 1, :], act_g[0:FR, u, 1, :], ps_h[u][FR:P, 2, :], ALU.mult).then_inc(h_done, 1)

            def weigh(e, k):
                u = k % 2
                dve.wait_ge(y_ready, e + 1)
                wait(dve, scattered, 16 * (e - B + 1))
                nc.vector.tensor_scalar(y[:, k, :], ps_y[u][:], xg[:, k, bass.ds(e + D, 1)], None, ALU.mult).then_inc(y_done, 1)

            walk(dve, E, B, B, [(3, hidden), (4, weigh)])


def forget_attention(nc, x_in, x_out, w, bias, const):
    import concourse.bass as bass
    from concourse import mybir
    from contextlib import ExitStack
    fp32 = mybir.dt.float32
    ALU, ACT = mybir.AluOpType, mybir.ActivationFunctionType
    P, D, H, DK, B = 128, 256, 16, 16, 8
    STEPS, COLS, GROUPS = 16, 8, 64
    VW = 2 * DK
    VF = D + H
    L_NORM, L_TURN, L_PROJ, L_BIAS, L_NEG, L_EXP, L_PHI, L_LOG, L_QK = 1, 2, 3, 4, 5, 6, 7, 8, 8
    L_BD, L_LSUM, L_DECAY, L_EXPAND, L_S, L_PV, L_ROWS, L_ADD_ROWS, L_OUT = 9, 9, 9, 9, 10, 11, 10, 11, 12

    with ExitStack() as ctx:
        def sb(name, shape, dt=fp32):
            return ctx.enter_context(nc.sbuf_tensor("b_" + name, shape, dt))

        def pb(name, shape, dt=fp32):
            return ctx.enter_context(nc.psum_tensor("b_" + name, shape, dt))

        def sem(name):
            return nc.alloc_semaphore("b_" + name)

        w_rows = sb("w_rows", [P, 8, D])
        f_rows = sb("f_rows", [H, D])
        w_qk = sb("w_qk", [P, 2, 2 * D])
        w_vf = sb("w_vf", [P, 2, VF])
        w_o = sb("w_o", [P, 2, D])
        b_qk = sb("b_qk", [P, 2 * D])
        b_vf = sb("b_vf", [P, VF])
        b_o = sb("b_o", [P, D])
        ident = sb("ident", [P, P])
        later = sb("later", [P, P])
        upto = sb("upto", [P, STEPS])
        own = sb("own", [P, P])
        head_rows = sb("head_rows", [P, COLS])
        minus_half = sb("minus_half", [P, 1])
        eps = sb("eps", [P, 1])
        xt = sb("xt", [P, B, D])
        stats = sb("stats", [P, B, 6])
        mean_var = sb("mean_var", [P, B, 2])
        var_eps = sb("var_eps", [P, B, 1])
        rstd = sb("rstd", [P, B, 1])
        xn = sb("xn", [P, B, D])
        xnT = sb("xnT", [P, B, 2, P])
        z_qk = sb("z_qk", [P, B, 2 * D])
        e_qk = sb("e_qk", [P, 2, 2 * D])
        phi = sb("phi", [P, 2, 2 * D])
        v_aug = sb("v_aug", [P, B, H, VW])
        z_f = sb("z_f", [P, B, H])
        low_f = sb("low_f", [P, B, H])
        abs_f = sb("abs_f", [P, B, H])
        log_f = sb("log_f", [P, B, H])
        log_upto = sb("log_upto", [P, 2, H, STEPS])
        decay = sb("decay", [P, 2, H, STEPS])
        spread = sb("spread", [P, 2, H, STEPS, COLS])
        q_bd = sb("q_bd", [P, 2, 2, COLS, P])
        kT = sb("kT", [P, 4, 2, P])
        weight = sb("weight", [P, 2, H, P])
        o_sb = sb("o_sb", [P, 2, 4 * P])
        den = sb("den", [P, 2, H])
        att = sb("att", [P, 2, D])
        attT = sb("attT", [P, 2, 2, P])
        xr = sb("xr", [P, B, D])
        xo = sb("xo", [P, B, D])
        ps_xl = pb("ps_xl", [P, 2, 2 * P])
        ps_qk = pb("ps_qk", [P, 2 * D])
        ps_vf = pb("ps_vf", [P, VF])
        ps_t = pb("ps_t", [P, 4, P])
        ps_s = [pb(f"ps_s{u}", [P, 4, P]) for u in range(2)]
        ps_o = pb("ps_o", [P, 4, P])
        ps_w = pb("ps_w", [P, 4, P])

        const_in, setup, w_turned, w_copied = (sem(n) for n in ("const_in", "setup", "w_turned", "w_copied"))
        x_loaded = [sem(f"x_loaded{k}") for k in range(B)]
        xr_loaded = [sem(f"xr_loaded{k}") for k in range(B)]
        stored = [sem(f"stored{k}") for k in range(B)]
        (stats_done, mv_done, ve_done, rstd_done, xn_done, x_turned, xnT_done, qk_ready, vf_ready, qk_biased, v_biased, f_biased,
         neg_done, low_done, abs_done, exp_done, f_exp_done, f_log_done, phi_done, log_done, qk_turned, bd_done, kT_done, upto_done,
         sums_ready, decay_done, spread_done, s_ready, weight_done, o_ready, o_copied, o_turned, den_done, att_done, att_turned,
         attT_done, out_ready, rows_ready, added) = (sem(n) for n in (
             "stats_done", "mv_done", "ve_done", "rstd_done", "xn_done", "x_turned", "xnT_done", "qk_ready", "vf_ready", "qk_biased",
             "v_biased", "f_biased", "neg_done", "low_done", "abs_done", "exp_done", "f_exp_done", "f_log_done", "phi_done", "log_done",
             "qk_turned", "bd_done", "kT_done", "upto_done", "sums_ready", "decay_done", "spread_done", "s_ready", "weight_done",
             "o_ready", "o_copied", "o_turned", "den_done", "att_done", "att_turned", "attT_done", "out_ready", "rows_ready", "added"))
        dve_passed = sem("dve_passed")
        block = ctx.enter_context(nc.Block())
        N_CONST = 4 + 1 + 6 + 5

        def group_rows(t, n):
            return t.rearrange("(s c) d -> s c d", s=STEPS)[:, bass.ds(n * COLS, COLS), :]

        @block.sync
        def _(sp):
            for i, m in enumerate((w["q"], w["k"], w["v"], w["o"])):
                sp.dma_start(w_rows[:, 2 * i:2 * i + 2, :], m.rearrange("(c p) d -> p c d", p=P)).then_inc(const_in, 16)
            sp.dma_start(f_rows[:], w["f"]).then_inc(const_in, 16)
            for tile, lo, b in ((b_qk, 0, "q"), (b_qk, D, "k"), (b_vf, 0, "v"), (b_vf, D, "f"), (b_o, 0, "o")):
                n = bias[b].shape[0]
                sp.dma_start(tile[:, lo:lo + n], bias[b].rearrange("(o n) -> o n", o=1).to_broadcast([P, n])).then_inc(const_in, 16)
            for tile, name in ((ident, "ident"), (later, "later"), (upto, "upto"), (own, "own"), (head_rows, "head_rows")):
                sp.dma_start(tile[:], const[name]).then_inc(const_in, 16)

            def load(n, k):
                wait(sp, xn_done, n - B + 1)
                sp.dma_start(xt[:, k, :], group_rows(x_in, n)).then_inc(x_loaded[k], 16)

            def load_rows(n, k):
                wait(sp, added, n - B + 1)
                sp.dma_start(xr[:, k, :], group_rows(x_in, n)).then_inc(xr_loaded[k], 16)

            def store(n, k):
                sp.wait_ge(added, n + 1)
                sp.dma_start(group_rows(x_out, n), xo[:, k, :]).then_inc(stored[k], 16)

            walk(sp, GROUPS, B, B, [(0, load), (L_ROWS, load_rows), (L_OUT + 3, store)])
            for k in range(B):
                sp.wait_ge(stored[k], 16 * GROUPS // B)

        @block.gpsimd
        def _(pool):
            nc.gpsimd.memset(minus_half[:], -0.5).then_inc(setup, 1)
            nc.gpsimd.memset(eps[:], 1e-5).then_inc(setup, 1)
            nc.gpsimd.memset(v_aug[:], 0.0).then_inc(setup, 1)
            pool.wait_ge(setup, 3)
            nc.gpsimd.memset(v_aug[:, :, :, DK:DK + 1], 1.0).then_inc(setup, 1)
            pool.wait_ge(const_in, 16 * (N_CONST - 1))

            def inverse_deviation(n, k):
                pool.wait_ge(mv_done, n + 1)
                nc.gpsimd.tensor_tensor(var_eps[:, k], mean_var[:, k, 1:2], eps[:], ALU.add).then_inc(ve_done, 1)
                pool.wait_ge(ve_done, n + 1)
                wait(pool, xn_done, n - B + 1)
                nc.gpsimd.tensor_tensor(rstd[:, k], var_eps[:, k], minus_half[:], ALU.pow).then_inc(rstd_done, 1)

            def log_gates(n, k):
                pool.wait_ge(log_done, n + 1)
                wait(pool, sums_ready, n - 1)
                nc.gpsimd.tensor_tensor(log_upto[:, k % 2], log_f[:, k, :].rearrange("p (h o) -> p h o", o=1).to_broadcast([P, H, STEPS]),
                                        upto[:].rearrange("p (o t) -> p o t", o=1).to_broadcast([P, H, STEPS]), ALU.mult).then_inc(upto_done, 1)

            def expand(n, k):
                pool.wait_ge(decay_done, n + 1)
                wait(pool, weight_done, 4 * (n - 1))
                nc.gpsimd.tensor_tensor(spread[:, k % 2].rearrange("p h t c -> p (h t) c"),
                                        decay[:, k % 2].rearrange("p h (t o) -> p (h t) o", o=1).to_broadcast([P, H * STEPS, COLS]),
                                        own[:].rearrange("p (o t) -> p o t", o=1).to_broadcast([P, H, P]), ALU.mult).then_inc(spread_done, 1)

            def rows(n, k):
                pool.wait_ge(xr_loaded[k], 16 * (turns(n, k, B) + 1))
                nc.gpsimd.tensor_tensor(xr[:, k, :], xr[:, k, :], b_o[:], ALU.add).then_inc(rows_ready, 1)

            walk(pool, GROUPS, B, B, [(0, inverse_deviation), (L_LOG, log_gates), (L_ADD_ROWS, rows), (L_EXPAND, expand)])

        @block.vector
        def _(dve):
            for i in range(5):
                dve.wait_ge(w_turned, i + 1)
                bank = (ps_t, ps_w)[i % 2]
                if i < 4:
                    dst = (w_qk[:, :, 0:D], w_qk[:, :, D:2 * D], w_vf[:, :, 0:D], w_o[:])[i]
                    nc.vector.tensor_copy(dst, bank[:].rearrange("p (c r) a -> p c (r a)", c=2)).then_inc(w_copied, 1)
                else:
                    nc.vector.tensor_copy(w_vf[:, :, D:VF], bank[:, 0:2, 0:H]).then_inc(w_copied, 1)
            dve.wait_ge(const_in, 16 * (N_CONST - 1))

            def statistics(n, k):
                dve.wait_ge(x_loaded[k], 16 * (turns(n, k, B) + 1))
                nc.vector.bn_stats(stats[:, k, :], xt[:, k, :]).then_inc(stats_done, 1)

            def aggregate(n, k):
                dve.wait_ge(stats_done, n + 1)
                passed_by(dve, dve_passed)
                nc.vector.bn_aggr(mean_var[:, k, :], stats[:, k, :]).then_inc(mv_done, 1)

            def normalise(n, k):
                dve.wait_ge(rstd_done, n + 1)
                wait(dve, x_turned, n - B + 1)
                nc.vector.tensor_scalar(xn[:, k, :], xt[:, k, :], mean_var[:, k, 0:1], rstd[:, k],
                                        ALU.subtract, ALU.mult).then_inc(xn_done, 1)

            def add_bias(n, k):
                dve.wait_ge(qk_ready, n + 1)
                nc.vector.tensor_tensor(z_qk[:, k, :], ps_qk[:], b_qk[:], ALU.add).then_inc(qk_biased, 1)
                dve.wait_ge(vf_ready, n + 1)
                if isinstance(n, int) and n == 0:
                    dve.wait_ge(setup, 4)
                wait(dve, o_ready, n - B + 1)
                nc.vector.tensor_tensor(v_aug[:, k, :, 0:DK], ps_vf[:, 0:D].rearrange("p (h d) -> p h d", d=DK),
                                        b_vf[:, 0:D].rearrange("p (h d) -> p h d", d=DK), ALU.add).then_inc(v_biased, 1)
                nc.vector.tensor_tensor(z_f[:, k, :], ps_vf[:, D:VF], b_vf[:, D:VF], ALU.add).then_inc(f_biased, 1)

            def negative_part(n, k):
                dve.wait_ge(qk_biased, n + 1)
                dve.wait_ge(f_biased, n + 1)
                wait(dve, phi_done, n - 1)
                nc.vector.tensor_scalar(e_qk[:, k % 2, :], z_qk[:, k, :], 0.0, None, ALU.min).then_inc(neg_done, 1)
                nc.vector.tensor_scalar(low_f[:, k, :], z_f[:, k, :], 0.0, None, ALU.min).then_inc(low_done, 1)
                dve.wait_ge(low_done, n + 1)
                nc.vector.scalar_tensor_tensor(abs_f[:, k, :], low_f[:, k, :], 2.0, z_f[:, k, :], ALU.mult, ALU.subtract).then_inc(abs_done, 1)

            def features(n, k):
                dve.wait_ge(exp_done, n + 1)
                wait(dve, qk_turned, n - 1)
                nc.vector.scalar_tensor_tensor(phi[:, k % 2, :], z_qk[:, k, :], 0.0, e_qk[:, k % 2, :], ALU.max, ALU.add).then_inc(phi_done, 1)
                dve.wait_ge(f_log_done, n + 1)
                nc.vector.tensor_tensor(log_f[:, k, :], low_f[:, k, :], abs_f[:, k, :], ALU.subtract).then_inc(log_done, 1)

            def block_queries(n, k):
                dve.wait_ge(kT_done, n + 1)
                wait(dve, s_ready, 4 * (n - 1))
                for half in range(2):
                    last = nc.vector.tensor_tensor(q_bd[:, k % 2, half], ps_t[:, half, :].rearrange("p (o t) -> p o t", o=1).to_broadcast([P, COLS, P]),
                                                   head_rows[:].rearrange("p (j o) -> p j o", o=1).to_broadcast([P, COLS, P]), ALU.mult)
                last.then_inc(bd_done, 1)

            def weigh(i):
                def stage(n, k):
                    dve.wait_ge(s_ready, 4 * n + i + 1)
                    if i == 0:
                        dve.wait_ge(spread_done, n + 1)
                        wait(dve, o_ready, n - 1)
                    heads = slice(4 * i, 4 * i + 4)
                    nc.vector.tensor_tensor(weight[:, k % 2, heads, :], ps_s[i % 2][:], spread[:, k % 2, heads].rearrange("p h t c -> p h (t c)"),
                                            ALU.mult).then_inc(weight_done, 1)
                return stage

            def divide(n, k):
                dve.wait_ge(o_turned, n + 1)
                heads = ps_w[:].rearrange("p i (j w) -> p (i j) w", w=VW)
                nc.vector.tensor_scalar(den[:, k % 2, :], heads[:, :, DK], 1e-6, None, ALU.add).then_inc(den_done, 1)
                dve.wait_ge(den_done, 2 * n + 1)
                nc.vector.reciprocal(den[:, k % 2, :], den[:, k % 2, :]).then_inc(den_done, 1)
                dve.wait_ge(den_done, 2 * n + 2)
                wait(dve, att_turned, n - 1)
                nc.vector.tensor_tensor(att[:, k % 2, :].rearrange("p (h d) -> p h d", d=DK), heads[:, :, 0:DK],
                                        den[:, k % 2, :].rearrange("p (h o) -> p h o", o=1).to_broadcast([P, H, DK]), ALU.mult).then_inc(att_done, 1)

            def add(n, k):
                dve.wait_ge(out_ready, n + 1)
                dve.wait_ge(rows_ready, n + 1)
                wait(dve, stored[k], 16 * turns(n, k, B))
                nc.vector.tensor_tensor(xo[:, k, :], ps_w[:].rearrange("p i a -> p (i a)")[:, D:2 * D], xr[:, k, :], ALU.add).then_inc(added, 1)

            walk(dve, GROUPS, B, B, [(0, statistics), (0, aggregate), (L_OUT, divide), (L_S, weigh(0)), (L_S, weigh(1)), (L_BIAS, add_bias),
                                     (L_NORM, normalise), (L_S, weigh(2)), (L_PHI, features), (L_OUT, add), (L_S, weigh(3)),
                                     (L_BD, block_queries), (L_NEG, negative_part)])

        @block.scalar
        def _(act):
            def evacuate_x(n, k):
                act.wait_ge(x_turned, n + 1)
                wait(act, vf_ready, n - B + 1)
                nc.scalar.activation(xnT[:, k], ps_xl[:, 0, :].rearrange("p (c t) -> p c t", c=2), ACT.Copy).then_inc(xnT_done, 1)

            def exponentials(n, k):
                act.wait_ge(neg_done, n + 1)
                nc.scalar.activation(e_qk[:, k % 2, :], e_qk[:, k % 2, :], ACT.Exp).then_inc(exp_done, 1)
                act.wait_ge(abs_done, n + 1)
                nc.scalar.activation(abs_f[:, k, :], abs_f[:, k, :], ACT.Exp).then_inc(f_exp_done, 1)
                act.wait_ge(f_exp_done, n + 1)
                nc.scalar.activation(abs_f[:, k, :], abs_f[:, k, :], ACT.Ln, bias=1.0).then_inc(f_log_done, 1)

            def copy_keys(n, k):
                act.wait_ge(qk_turned, n + 1)
                wait(act, s_ready, 4 * (n - 3))
                nc.scalar.activation(kT[:, k % 4], ps_t[:, 2:4, :], ACT.Copy).then_inc(kT_done, 1)

            def decays(n, k):
                act.wait_ge(sums_ready, n + 1)
                wait(act, spread_done, n - 1)
                nc.scalar.activation(decay[:, k % 2].rearrange("p h t -> p (h t)"), ps_xl[:, 1, :], ACT.Exp).then_inc(decay_done, 1)

            def copy_output(n, k):
                act.wait_ge(o_ready, n + 1)
                wait(act, o_turned, n - 1)
                nc.scalar.activation(o_sb[:, k % 2, :], ps_o[:].rearrange("p i a -> p (i a)"), ACT.Copy).then_inc(o_copied, 1)

            def copy_att(n, k):
                act.wait_ge(att_turned, n + 1)
                wait(act, out_ready, n - 1)
                nc.scalar.activation(attT[:, k % 2], ps_w[:, 0:2, :], ACT.Copy).then_inc(attT_done, 1)

            walk(act, GROUPS, B, B, [(L_BD, copy_keys), (L_EXP, exponentials), (L_TURN, evacuate_x), (L_OUT, copy_att), (L_PV, copy_output),
                                     (L_DECAY, decays)])

        @block.tensor
        def _(pe):
            pe.wait_ge(const_in, 16 * N_CONST - 16)
            for i in range(5):
                wait(pe, w_copied, i - 1)
                bank = (ps_t, ps_w)[i % 2]
                for c in range(2):
                    if i < 4:
                        for r in range(2):
                            last = nc.tensor.transpose(bank[:, 2 * c + r, :], w_rows[:, 2 * i + r, c * P:(c + 1) * P], ident[:])
                    else:
                        last = nc.tensor.transpose(bank[:, c, 0:H], f_rows[:, c * P:(c + 1) * P], ident[0:H, 0:H])
                last.then_inc(w_turned, 1)
            pe.wait_ge(w_copied, 5)

            def turn_x(n, k):
                pe.wait_ge(xn_done, n + 1)
                wait(pe, xnT_done, n)
                wait(pe, decay_done, n + L_TURN - L_LSUM)
                for c in range(2):
                    last = nc.tensor.transpose(ps_xl[:, 0, c * P:(c + 1) * P], xn[:, k, c * P:(c + 1) * P], ident[:])
                last.then_inc(x_turned, 1)

            def project(n, k):
                pe.wait_ge(xnT_done, n + 1)
                wait(pe, qk_biased, n)
                for c in range(2):
                    last = nc.tensor.matmul(ps_qk[:], xnT[:, k, c, :], w_qk[:, c, :], start=c == 0, stop=c == 1)
                last.then_inc(qk_ready, 1)
                wait(pe, f_biased, n)
                wait(pe, v_biased, n)
                for c in range(2):
                    last = nc.tensor.matmul(ps_vf[:], xnT[:, k, c, :], w_vf[:, c, :], start=c == 0, stop=c == 1)
                last.then_inc(vf_ready, 1)

            def turn_qk(n, k):
                pe.wait_ge(phi_done, n + 1)
                wait(pe, bd_done, n)
                wait(pe, kT_done, n)
                for g in range(4):
                    last = nc.tensor.transpose(ps_t[:, g, :], phi[:, k % 2, g * P:(g + 1) * P], ident[:])
                last.then_inc(qk_turned, 1)

            def sum_logs(n, k):
                pe.wait_ge(upto_done, n + 1)
                seen = n + L_LSUM - L_TURN + 1
                pe.wait_ge(xnT_done, min(seen, GROUPS) if isinstance(seen, int) else seen)
                nc.tensor.matmul(ps_xl[:, 1, :], later[:], log_upto[:, k % 2].rearrange("p h t -> p (h t)"), start=True, stop=True).then_inc(sums_ready, 1)

            def scores(i):
                def stage(n, k):
                    if i == 0:
                        pe.wait_ge(bd_done, n + 1)
                        pe.wait_ge(kT_done, n + 1)
                    wait(pe, weight_done, 4 * n + i - 1)
                    half, quarter = i // 2, i % 2
                    nc.tensor.matmul(ps_s[i % 2][:], kT[:, k % 4, half, :], q_bd[:, k % 2, half, 4 * quarter:4 * quarter + 4, :],
                                     start=True, stop=True).then_inc(s_ready, 1)
                return stage

            def mix_values(n, k):
                pe.wait_ge(weight_done, 4 * n + 4)
                wait(pe, o_copied, n)
                for i in range(4):
                    for j in range(4):
                        h = 4 * i + j
                        last = nc.tensor.matmul(ps_o[VW * j:VW * (j + 1), i, :], v_aug[:, k, h, :], weight[:, k % 2, h, :], start=True, stop=True)
                last.then_inc(o_ready, 1)

            def turn_output(n, k):
                pe.wait_ge(o_copied, n + 1)
                wait(pe, added, n)
                for i in range(4):
                    last = nc.tensor.transpose(ps_w[:, i, :], o_sb[:, k % 2, i * P:(i + 1) * P], ident[:])
                last.then_inc(o_turned, 1)

            def turn_att(n, k):
                pe.wait_ge(att_done, n + 1)
                for c in range(2):
                    last = nc.tensor.transpose(ps_w[:, c, :], att[:, k % 2, c * P:(c + 1) * P], ident[:])
                last.then_inc(att_turned, 1)

            def project_out(n, k):
                pe.wait_ge(attT_done, n + 1)
                out = ps_w[:].rearrange("p i a -> p (i a)")[:, D:2 * D]
                for c in range(2):
                    last = nc.tensor.matmul(out, attT[:, k % 2, c, :], w_o[:, c, :], start=c == 0, stop=c == 1)
                last.then_inc(out_ready, 1)

            walk(pe, GROUPS, B, B, [(L_OUT, turn_output), (L_S, scores(0)), (L_S, scores(1)), (L_TURN, turn_x), (L_OUT, turn_att),
                                    (L_S, scores(2)), (L_PV, mix_values), (L_LSUM, sum_logs), (L_OUT, project_out), (L_S, scores(3)),
                                    (L_PROJ, project), (L_QK, turn_qk)])


def program(nc, a):
    from concourse import mybir
    fp32, bf16, u32 = mybir.dt.float32, mybir.dt.bfloat16, mybir.dt.uint32
    P, D, T, E, SEQS, S, H, VW = 128, 256, 8192, 64, 16, 512, 16, 32
    SPARE = P

    def scratch(name, shape, dt=fp32):
        return nc.dram_tensor(name, shape, dt).ap()

    split = {"parts": scratch("parts", (SEQS, 12, P, S), bf16), "v_aug": scratch("v_aug", (T, H * VW))}
    routed = {"rows": scratch("rows", (T + SPARE, D + E))}
    x0 = a["L0_attn_a_x"].rearrange("b s d -> (b s) d")
    x1, x3 = scratch("x1", (T, D)), scratch("x3", (T, D))
    x2 = scratch("x2", (T + SPARE, D))

    def mixture(tag, x_in, x_out):
        with nc.sbuf_tensor(tag + "_slots", [P, E], u32) as slots:
            with (nc.sbuf_tensor(tag + "_order", [P, T // 2], fp32) as order,
                  nc.sbuf_tensor(tag + "_x_rows", [P, T // P, D], fp32) as x_rows,
                  nc.sbuf_tensor(tag + "_x_turned", [P, D // P, T], fp32) as x_turned):
                const = dict(a, order=order, x_rows=x_rows, x_turned=x_turned, slots=slots)
                with nc.cleanup_on_exit():
                    moe_route(nc, tag, routed, x_in, a["L0_ffn_router_w"], const)
                with nc.cleanup_on_exit():
                    moe_shared(nc, tag, x_out, a["L0_ffn_ws_gate_up"], a["L0_ffn_ws_down"], const)
            with nc.cleanup_on_exit():
                moe_experts(nc, tag, routed, x_out, a["L0_ffn_w_gate"], a["L0_ffn_w_up"], a["L0_ffn_w_down"], dict(a, slots=slots))

    with nc.cleanup_on_exit():
        attention_project(nc, split, x0, a["L0_attn_a_Wq"], a["L0_attn_a_Wk"], a["L0_attn_a_Wv"], a)
    with nc.cleanup_on_exit():
        attention_mix(nc, split, x0, x1, a["L0_attn_a_Wo"], a)
    mixture("m1", x1, x2)
    with nc.cleanup_on_exit():
        forget_attention(nc, x2[0:T, :], x3, {m: a["L0_attn_b_W" + m] for m in "qkvfo"}, {m: a["L0_attn_b_b" + m] for m in "qkvfo"}, a)
    mixture("m2", x3, a["out"])


_INS = ["L0_attn_a_x", "L0_attn_a_Wq", "L0_attn_a_Wk", "L0_attn_a_Wv", "L0_attn_a_Wo", "L0_attn_b_Wq", "L0_attn_b_bq", "L0_attn_b_Wk",
        "L0_attn_b_bk", "L0_attn_b_Wv", "L0_attn_b_bv", "L0_attn_b_Wf", "L0_attn_b_bf", "L0_attn_b_Wo", "L0_attn_b_bo",
        "L0_ffn_router_w", "L0_ffn_w_gate", "L0_ffn_w_up", "L0_ffn_w_down", "L0_ffn_ws_gate_up", "L0_ffn_ws_down"]


def constants():
    P, S, DK, T = 128, 512, 16, 8192
    p = np.arange(P)
    angle = np.arange(S, dtype=np.float32)[:, None] * (1.0 / 10000.0 ** (np.arange(0, DK, 2, dtype=np.float32) / DK)).astype(np.float32)
    by_tile = lambda t: t.reshape(S // P, P, DK).transpose(1, 0, 2)
    item = np.arange(T // P)
    tile = item % 2 * (T // P // 2) + item // 2
    step, col = p // 8, p % 8
    tables = {
        "ident": np.eye(P),
        "cos": by_tile(np.concatenate([np.cos(angle), np.cos(angle)], 1)),
        "sin": by_tile(np.concatenate([-np.sin(angle), np.sin(angle)], 1)),
        "rank_value": T - (tile[None, :] * P + p[:, None]),
        "spare_row": p[:, None],
        "later": (col[:, None] == col) & (step[:, None] > step),
        "upto": step[:, None] <= np.arange(16),
        "own": (col[:, None] == col) & (step[:, None] <= step),
        "head_rows": p[:, None] // DK == np.arange(P // DK),
    }
    return {name: np.ascontiguousarray(t, dtype=np.float32) for name, t in tables.items()}


def kernel(**inputs):
    import concourse.bacc as _bacc
    from concourse import mybir as _mybir
    from concourse.bass_utils import run_bass_kernel_spmd as _run

    nc = _bacc.Bacc("TRN2", target_bir_lowering=False, num_devices=1)
    data = {name: np.ascontiguousarray(inputs[name]) for name in _INS}
    data.update(constants())
    arrays, a = {}, {}
    for name, t in data.items():
        arrays[f"in_{name}_dram"] = t
        a[name] = nc.dram_tensor(f"in_{name}_dram", t.shape, _mybir.dt.from_np(t.dtype), kind="ExternalInput").ap()
    tokens, features = 16 * 512, 256
    a["out"] = nc.dram_tensor("out_0_dram", (tokens + 128, features), _mybir.dt.float32, kind="ExternalOutput").ap()
    program(nc, a)
    r = _run(nc, [arrays], core_ids=[0])
    return r.results[0]["out_0_dram"][:tokens].reshape(16, 512, features)
```

```python
import numpy as np


def wait(eng, sem, value):
    if not isinstance(value, int) or value > 0:
        eng.wait_ge(sem, value)


def passed_by(eng, passed):
    eng.sem_inc(passed, 1)


def walk(eng, total, trip, look_back, stages):
    deepest = max(lag for lag, _ in stages)
    lead = trip * -(-(deepest + look_back) // trip)

    def step(s, k, peeled):
        for lag, stage in stages:
            if not peeled or 0 <= s - lag < total:
                stage(s - lag, (k - lag) % trip)

    for s in range(lead):
        step(s, s % trip, True)
    with eng.Fori(lead // trip, total // trip) as i:
        for k in range(trip):
            step(i * trip + k, k, False)
    for s in range(total, total + deepest):
        step(s, s % trip, True)


def turns(n, k, trip):
    return n // trip if isinstance(n, int) else (n - k) // trip


def attention_project(nc, dram, x_in, wq, wk, wv, const, ahead):
    import concourse.bass as bass
    from concourse import mybir
    from contextlib import ExitStack
    fp32, bf16 = mybir.dt.float32, mybir.dt.bfloat16
    ALU, ACT = mybir.AluOpType, mybir.ActivationFunctionType
    P, D, H, DK = 128, 256, 16, 16
    TPB, TRIP = 4, 8
    S = TPB * P
    SEQS = 16
    TILES = SEQS * TPB
    HALF = DK // 2

    with ExitStack() as ctx:
        def sb(name, shape, dt=fp32):
            return ctx.enter_context(nc.sbuf_tensor("a1_" + name, shape, dt))

        def pb(name, shape, dt=fp32):
            return ctx.enter_context(nc.psum_tensor("a1_" + name, shape, dt))

        def sem(name):
            return nc.alloc_semaphore("a1_" + name)

        w_rows = sb("w_rows", [P, 6, D])
        w_qk = sb("w_qk", [P, 2, 2 * D])
        w_v = sb("w_v", [P, 2, D])
        ident = const["ident_sb"]
        cos = sb("cos", [P, TPB, DK])
        sin = sb("sin", [P, TPB, DK])
        minus_half = sb("minus_half", [P, 1])
        eps = sb("eps", [P, 1])
        xt = sb("xt", [P, TRIP, D])
        stats = sb("stats", [P, 2, 6])
        mean_var = sb("mean_var", [P, TPB, 2])
        var_eps = sb("var_eps", [P, 2, 1])
        rstd = sb("rstd", [P, TPB, 1])
        xn = sb("xn", [P, TPB, D])
        xnT = sb("xnT", [P, 2, 2, P])
        rot_cos = sb("rot_cos", [P, 2, 2 * D])
        rot_sin = sb("rot_sin", [P, 2, 2 * D])
        qk = sb("qk", [P, 2, 2 * D])
        v = sb("v", [P, 2, TPB, D])
        rest = sb("rest", [P, 2, 2 * D])
        parts = sb("parts", [P, 2, 3, 4, S], bf16)
        ps_x = pb("ps_x", [P, 2, P])
        ps_qk = [pb(f"ps_qk{u}", [P, 2 * D]) for u in range(2)]
        ps_v = [pb(f"ps_v{u}", [P, D]) for u in range(2)]
        ps_t = [pb(f"ps_t{u}", [P, 4, P]) for u in range(2)]

        const_in, w_turned, w_copied, setup = sem("const_in"), sem("w_turned"), sem("w_copied"), sem("setup")
        x_loaded = [sem(f"x_loaded{k}") for k in range(TRIP)]
        stats_done, mv_done, ve_done, rstd_done, xn_done = (sem(n) for n in ("stats_done", "mv_done", "ve_done", "rstd_done", "xn_done"))
        x_turned, xnT_done, qk_projected, v_projected, v_copied = (sem(n) for n in ("x_turned", "xnT_done", "qk_projected", "v_projected", "v_copied"))
        rot_done, qk_done, qk_turned, high_done, rest_done, mid_done, low_done = (sem(n) for n in (
            "rot_done", "qk_done", "qk_turned", "high_done", "rest_done", "mid_done", "low_done"))
        v_stored = [sem(f"v_stored{u}") for u in range(2)]
        parts_stored = [sem(f"parts_stored{u}") for u in range(2)]
        dve_passed, ahead_loaded = sem("dve_passed"), sem("ahead_loaded")
        block = ctx.enter_context(nc.Block())

        @block.sync
        def _(sp):
            for i, w in enumerate((wq, wk, wv)):
                sp.dma_start(w_rows[:, 2 * i:2 * i + 2, :], w.rearrange("(c p) d -> p c d", p=P)).then_inc(const_in, 16)
            sp.dma_start(ident[:], const["ident"]).then_inc(const_in, 16)
            sp.dma_start(cos[:], const["cos"]).then_inc(const_in, 16)
            sp.dma_start(sin[:], const["sin"]).then_inc(const_in, 16)

            def load(n, k):
                wait(sp, xn_done, n - TRIP + 1)
                sp.dma_start(xt[:, k, :], x_in[bass.ds(n * P, P), :]).then_inc(x_loaded[k], 16)

            def store_v(n, k):
                if k % TPB == TPB - 1:
                    sp.wait_ge(v_copied, n + 1)
                    first = (n - TPB + 1) * P
                    sp.dma_start(dram["v"][bass.ds(first, S), :].rearrange("(t p) d -> p t d", p=P), v[:, k // TPB]).then_inc(v_stored[k // TPB], 16)

            def store_parts(n, k):
                if k % TPB == TPB - 1:
                    sp.wait_ge(high_done, n + 1)
                    sp.wait_ge(mid_done, n + 1)
                    sp.wait_ge(low_done, n + 1)
                    sp.dma_start(dram["parts"][turns(n, k % TPB, TPB)].rearrange("g p t -> p g t"),
                                 parts[:, k // TPB].rearrange("p k g t -> p (k g) t")).then_inc(parts_stored[k // TPB], 16)

            walk(sp, TILES, TRIP, TRIP, [(0, load), (11, store_v), (14, store_parts)])
            for s in range(2):
                sp.wait_ge(v_stored[s], 16 * SEQS // 2)
                sp.wait_ge(parts_stored[s], 16 * SEQS // 2)

        @block.gpsimd
        def _(pool):
            nc.gpsimd.memset(minus_half[:], -0.5).then_inc(setup, 1)
            nc.gpsimd.memset(eps[:], 1e-5).then_inc(setup, 1)
            pool.wait_ge(setup, 2)

            def inverse_deviation(n, k):
                j, u = k % TPB, k % 2
                pool.wait_ge(mv_done, n + 1)
                nc.gpsimd.tensor_tensor(var_eps[:, u], mean_var[:, j, 1:2], eps[:], ALU.add).then_inc(ve_done, 1)
                pool.wait_ge(ve_done, n + 1)
                nc.gpsimd.tensor_tensor(rstd[:, j], var_eps[:, u], minus_half[:], ALU.pow).then_inc(rstd_done, 1)

            def split(n, k):
                j, u = k % TPB, k % 2
                pool.wait_ge(mid_done, n + 1)
                nc.gpsimd.tensor_tensor(parts[:, k // TPB, 2, :, j * P:(j + 1) * P], rest[:, u, :].rearrange("p (g t) -> p g t", g=4), parts[:, k // TPB, 1, :, j * P:(j + 1) * P],
                                        ALU.subtract).then_inc(low_done, 1)

            def rotated(n, k):
                u = k % 2
                pool.wait_ge(rot_done, n + 1)
                wait(pool, qk_turned, n - 1)
                nc.gpsimd.tensor_tensor(qk[:, u, :], rot_cos[:, u, :], rot_sin[:, u, :], ALU.add).then_inc(qk_done, 1)

            walk(pool, TILES, TRIP, TRIP, [(0, inverse_deviation), (4, rotated), (7, split)])

        @block.vector
        def _(dve):
            for i in range(6):
                dve.wait_ge(w_turned, i + 1)
                for c in range(2):
                    dst = w_qk[:, c, i * P:(i + 1) * P] if i < 4 else w_v[:, c, (i - 4) * P:(i - 3) * P]
                    last = nc.vector.tensor_copy(dst, ps_t[i % 2][:, c, :])
                last.then_inc(w_copied, 1)

            def statistics(n, k):
                j, u = k % TPB, k % 2
                dve.wait_ge(x_loaded[k], 16 * (turns(n, k, TRIP) + 1))
                nc.vector.bn_stats(stats[:, u, :], xt[:, k, :]).then_inc(stats_done, 1)
                dve.wait_ge(stats_done, n + 1)
                wait(dve, xn_done, n - 3)
                passed_by(dve, dve_passed)
                nc.vector.bn_aggr(mean_var[:, j, :], stats[:, u, :]).then_inc(mv_done, 1)

            def normalise(n, k):
                j = k % TPB
                dve.wait_ge(rstd_done, n + 1)
                wait(dve, x_turned, n - 3)
                nc.vector.tensor_scalar(xn[:, j, :], xt[:, k, :], mean_var[:, j, 0:1], rstd[:, j],
                                        ALU.subtract, ALU.mult).then_inc(xn_done, 1)

            def rotate(n, k):
                j, u = k % TPB, k % 2
                if j == 0 and isinstance(n, int) and n == 0:
                    dve.wait_ge(const_in, 16 * 6)
                dve.wait_ge(qk_projected, n + 1)
                wait(dve, qk_done, n - 1)
                heads = ps_qk[u][:].rearrange("p (h d) -> p h d", d=DK)
                turned = rot_sin[:, u, :].rearrange("p (h d) -> p h d", d=DK)
                cos_b = cos[:, j, :].rearrange("p (o d) -> p o d", o=1).to_broadcast([P, 2 * H, DK])
                nc.vector.tensor_tensor(rot_cos[:, u, :].rearrange("p (h d) -> p h d", d=DK), heads, cos_b, ALU.mult)
                for part in range(2):
                    dims = slice(part * HALF, (part + 1) * HALF)
                    sin_b = sin[:, j, dims].rearrange("p (o d) -> p o d", o=1).to_broadcast([P, 2 * H, HALF])
                    last = nc.vector.tensor_tensor(turned[:, :, dims], heads[:, :, 1 - part::2], sin_b, ALU.mult)
                last.then_inc(rot_done, 1)

            def remainder(n, k):
                j, u = k % TPB, k % 2
                dve.wait_ge(high_done, n + 1)
                wait(dve, low_done, n - 1)
                nc.vector.tensor_tensor(rest[:, u, :].rearrange("p (g t) -> p g t", g=4), ps_t[u][:], parts[:, k // TPB, 0, :, j * P:(j + 1) * P],
                                        ALU.subtract).then_inc(rest_done, 1)

            walk(dve, TILES, TRIP, TRIP, [(0, statistics), (4, rotate), (6, remainder), (1, normalise)])

        @block.scalar
        def _(act):
            for held, source in ahead:
                act.dma_start(held, source).then_inc(ahead_loaded, 16)

            def evacuate_x(n, k):
                u = k % 2
                act.wait_ge(x_turned, n + 1)
                wait(act, v_projected, n - 1)
                nc.scalar.activation(xnT[:, u], ps_x[:], ACT.Copy).then_inc(xnT_done, 1)

            def evacuate_v(n, k):
                j, u = k % TPB, k % 2
                act.wait_ge(v_projected, n + 1)
                if j == 0:
                    wait(act, v_stored[k // TPB], 16 * turns(n, k, TRIP))
                nc.scalar.activation(v[:, k // TPB, j, :], ps_v[u][:], ACT.Copy).then_inc(v_copied, 1)

            def high(n, k):
                j, u = k % TPB, k % 2
                act.wait_ge(qk_turned, n + 1)
                if j == 0:
                    wait(act, parts_stored[k // TPB], 16 * turns(n, k, TRIP))
                nc.scalar.activation(parts[:, k // TPB, 0, :, j * P:(j + 1) * P], ps_t[u][:], ACT.Copy).then_inc(high_done, 1)

            def middle(n, k):
                j, u = k % TPB, k % 2
                act.wait_ge(rest_done, n + 1)
                nc.scalar.activation(parts[:, k // TPB, 1, :, j * P:(j + 1) * P], rest[:, u, :].rearrange("p (g t) -> p g t", g=4), ACT.Copy).then_inc(mid_done, 1)

            walk(act, TILES, TRIP, TRIP, [(7, middle), (2, evacuate_x), (3, evacuate_v), (5, high)])

            act.wait_ge(ahead_loaded, 16 * len(ahead))

        @block.tensor
        def _(pe):
            pe.wait_ge(const_in, 16 * 6)
            for i in range(6):
                wait(pe, w_copied, i - 1)
                for c in range(2):
                    last = nc.tensor.transpose(ps_t[i % 2][:, c, :], w_rows[:, i, c * P:(c + 1) * P], ident[:])
                last.then_inc(w_turned, 1)
            pe.wait_ge(w_copied, 6)

            def turn_x(n, k):
                j = k % TPB
                pe.wait_ge(xn_done, n + 1)
                wait(pe, xnT_done, n)
                for c in range(2):
                    last = nc.tensor.transpose(ps_x[:, c, :], xn[:, j, c * P:(c + 1) * P], ident[:])
                last.then_inc(x_turned, 1)

            def project(n, k):
                u = k % 2
                pe.wait_ge(xnT_done, n + 1)
                wait(pe, rot_done, n - 1)
                for c in range(2):
                    last = nc.tensor.matmul(ps_qk[u][:], xnT[:, u, c, :], w_qk[:, c, :], start=c == 0, stop=c == 1)
                last.then_inc(qk_projected, 1)
                wait(pe, v_copied, n - 1)
                for c in range(2):
                    last = nc.tensor.matmul(ps_v[u][:], xnT[:, u, c, :], w_v[:, c, :], start=c == 0, stop=c == 1)
                last.then_inc(v_projected, 1)

            def turn_qk(n, k):
                u = k % 2
                pe.wait_ge(qk_done, n + 1)
                wait(pe, rest_done, n - 1)
                for g in range(4):
                    last = nc.tensor.transpose(ps_t[u][:, g, :], qk[:, u, g * P:(g + 1) * P], ident[:])
                last.then_inc(qk_turned, 1)

            walk(pe, TILES, TRIP, TRIP, [(2, turn_x), (3, project), (5, turn_qk)])


def attention_mix(nc, dram, x_in, x_out, const):
    import concourse.bass as bass
    from concourse import mybir
    from contextlib import ExitStack
    fp32, bf16 = mybir.dt.float32, mybir.dt.bfloat16
    ALU, ACT, AX = mybir.AluOpType, mybir.ActivationFunctionType, mybir.AxisListType
    P, D, H, DK, S = 128, 256, 16, 16, 512
    SEQS, QT = 16, S // P
    PERIOD = 2 * H
    Q_PARTS = (0, 0, 1, 1, 0, 2)
    K_PARTS = (0, 1, 0, 1, 2, 0)
    SLOTS = len(Q_PARTS)
    K_MAX = SLOTS * DK
    K_ALL = K_MAX + 2
    HALF = H // 2
    VW = 2 * DK
    L_TURN, L_MSPLIT, L_S, L_PV, L_OCOPY, L_OTURN, L_ONORM = 1, 2, 12, 17, 18, 19, 20
    L_ATT = L_ONORM + 1

    with ExitStack() as ctx:
        def sb(name, shape, dt=fp32):
            return ctx.enter_context(nc.sbuf_tensor("a2_" + name, shape, dt))

        def pb(name, shape, dt=fp32):
            return ctx.enter_context(nc.psum_tensor("a2_" + name, shape, dt))

        def sem(name):
            return nc.alloc_semaphore("a2_" + name)

        woT = sb("woT", [P, 2, D])
        ident, wo_rows = const["ident_sb"], const["wo_rows"]
        qs = [sb(f"qs{u}", [P, H, S], bf16) for u in range(2)]
        ks = [sb(f"ks{u}", [P, H, S], bf16) for u in range(2)]
        vs = sb("vs", [P, QT, D])
        va = [sb(f"va{u}", [P, QT, H * VW]) for u in range(2)]
        xr = [sb(f"xr{u}", [P, QT, D]) for u in range(2)]
        row_max = sb("row_max", [P, 2, QT, H])
        m_parts = sb("m_parts", [HALF, 2, 2, S], bf16)
        probs = sb("probs", [P, 2, 4, QT, S])
        o_sb = sb("o_sb", [P, 2, S])
        rden = sb("rden", [P, 2, QT, 4])
        att = sb("att", [P, 2, QT, D])
        attT = sb("attT", [P, 2, 4, P])
        xo = sb("xo", [P, 2, 2, D])
        ps_m = [pb(f"ps_m{u}", [P, S]) for u in range(2)]
        ps_s = [pb(f"ps_s{u}", [P, 2, S]) for u in range(2)]
        ps_o = pb("ps_o", [P, S])
        ps_w = pb("ps_w", [P, 4, P])

        w_turned, w_copied, ones_set = sem("w_turned"), sem("w_copied"), sem("ones_set")
        va_zeroed, va_ones = sem("va_zeroed"), sem("va_ones")
        qk_loaded = [[sem(f"qk_loaded{u}{f}") for f in range(2)] for u in range(2)]
        v_loaded, va_done, pool_passed = sem("v_loaded"), sem("va_done"), sem("pool_passed")
        xr_loaded = [sem(f"xr_loaded{u}") for u in range(2)]
        m_loaded = [sem(f"m_loaded{f}") for f in range(2)]
        max_ready, max_done, m_turned, m_high, m_low = (sem(n) for n in ("max_ready", "max_done", "m_turned", "m_high", "m_low"))
        s_ready, exp_done, pv_done, o_copied, o_turned, rden_done, o_normed = (sem(n) for n in (
            "s_ready", "exp_done", "pv_done", "o_copied", "o_turned", "rden_done", "o_normed"))
        att_turned, attT_done, projected, added = (sem(n) for n in ("att_turned", "attT_done", "projected", "added"))
        stored = [sem(f"stored{q}") for q in range(2)]
        block = ctx.enter_context(nc.Block())

        class Head:

            def __init__(self, base, k):
                self.base, self.k = base, k
                self.h, self.u = k % H, k // H % 2

            def count(self, per_period, extra):
                return self.base * per_period + extra

        def uses(step, first, period=PERIOD):
            n = -((first - step.k) // period)
            n = step.base * (PERIOD // period) + n
            return min(max(0, n), SEQS * H // period) if isinstance(n, int) else n

        def walk_heads(eng, stages):
            deepest = max(lag for lag, _ in stages)
            total = SEQS * H

            def step(base, k, peeled):
                for lag, stage in stages:
                    if peeled and not 0 <= PERIOD * base + k - lag < total:
                        continue
                    stage(Head(base, k - lag), Head(base, k))

            for k in range(PERIOD):
                step(0, k, True)
            with eng.Fori(1, SEQS // 2) as base:
                for k in range(PERIOD):
                    step(base, k, False)
            for k in range(deepest):
                step(SEQS // 2, k, True)

        A_TURN = (H - 1 + L_ATT, H - 1 + L_ATT + 8)
        A_PROJ = (H - 1 + L_ATT + 1, H - 1 + L_ATT + 9)

        def ps_w_free(pe, step):
            wait(pe, m_low, uses(step, HALF - 1 + L_TURN, HALF))
            wait(pe, o_normed, uses(step, 3 + L_OTURN, 4))
            wait(pe, attT_done, uses(step, A_TURN[0], H) + uses(step, A_TURN[1], H))
            wait(pe, added, uses(step, A_PROJ[0], H) + uses(step, A_PROJ[1], H))

        @block.sync
        def _(sp):
            def load_qk(b, u, f):
                wait(sp, s_ready, 2 * (H * (b - 2) + HALF * (f + 1)))
                heads = slice(f * HALF, (f + 1) * HALF)
                for tiles, parts_of, half in ((qs, Q_PARTS, 0), (ks, K_PARTS, 2)):
                    for slot, part in enumerate(parts_of):
                        src = dram["parts"][b, 4 * part + half + f].rearrange("(h d) t -> d h t", d=DK)
                        sp.dma_start(tiles[u][slot * DK:(slot + 1) * DK, heads, :], src).then_inc(qk_loaded[u][f], 16)

            def load_m(b, u, f):
                wait(sp, m_low, 2 * b + f + 1)
                wait(sp, m_high, 2 * b + f + 1)
                heads = slice(f * HALF, (f + 1) * HALF)
                for part in range(2):
                    sp.dma_start(qs[u][K_MAX + part:K_MAX + part + 1, heads, :], m_parts[:, f, part, :]).then_inc(m_loaded[f], 16)

            def sequence(b, u, last):
                load_m(b, u, 0)
                wait(sp, va_done, b)
                sp.dma_start(vs[:], x_rows(dram["v"], b)).then_inc(v_loaded, 16)
                if not last:
                    for f in range(2):
                        load_qk(b + 1, 1 - u, f)
                load_m(b, u, 1)
                wait(sp, added, 2 * (b - 1))
                sp.dma_start(xr[u][:], x_rows(x_in, b)).then_inc(xr_loaded[u], 16)

            def x_rows(t, b):
                return t[bass.ds(b * S, S), :].rearrange("(t p) d -> p t d", p=P)

            for f in range(2):
                load_qk(0, 0, f)
            sequence(0, 0, False)
            sequence(1, 1, False)
            with sp.Fori(1, SEQS // 2 - 1) as i:
                for u in range(2):
                    sequence(2 * i + u, u, False)
            sequence(SEQS - 2, 0, False)
            sequence(SEQS - 1, 1, True)

        @block.gpsimd
        def _(pool):
            def heads_of(u):
                return va[u][:].rearrange("p t (h w) -> p t h w", w=VW)

            for u in range(2):
                nc.gpsimd.memset(ks[u][K_MAX:K_ALL, :, :], 1.0).then_inc(ones_set, 1)
            pool.wait_ge(ones_set, 2)
            for u in range(2):
                nc.gpsimd.memset(va[u][:], 0.0).then_inc(va_zeroed, 1)
            pool.wait_ge(va_zeroed, 2)
            for u in range(2):
                nc.gpsimd.memset(heads_of(u)[:, :, :, DK:DK + 1], 1.0).then_inc(va_ones, 1)
            pool.wait_ge(va_ones, 2)

            def spread(b, u):
                pool.wait_ge(v_loaded, 16 * (b + 1))
                wait(pool, pv_done, H * (b - 1))
                passed_by(pool, pool_passed)
                for t in range(QT):
                    last = nc.gpsimd.tensor_copy(heads_of(u)[:, t, :, 0:DK], vs[:, t, :].rearrange("p (h d) -> p h d", d=DK))
                last.then_inc(va_done, 1)

            def store(b, u):
                for q in range(2):
                    pool.wait_ge(added, 2 * b + q + 1)
                    pool.dma_start(x_out[bass.ds(b * S + q * 2 * P, 2 * P), :].rearrange("(t p) d -> p t d", p=P), xo[:, q]).then_inc(stored[q], 16)

            walk(pool, SEQS, 2, 2, [(0, spread), (2, store)])
            for q in range(2):
                pool.wait_ge(stored[q], 16 * SEQS)

        @block.tensor
        def _(pe):
            for i in range(2):
                wait(pe, w_copied, i)
                for c in range(2):
                    last = nc.tensor.transpose(ps_w[:, c, :], wo_rows[:, i, c * P:(c + 1) * P], ident[:])
                last.then_inc(w_turned, 1)
            pe.wait_ge(w_copied, 2)

            def max_products(t):
                def stage(n, step):
                    u, h = n.u, n.h
                    if h % HALF == 0 and t == 0:
                        pe.wait_ge(qk_loaded[u][h // HALF], 16 * 2 * SLOTS * (n.base + 1))
                    wait(pe, max_done, n.count(QT * PERIOD, QT * n.k + t - 1))
                    nc.tensor.matmul(ps_m[t % 2][:], qs[u][0:K_MAX, h, t * P:(t + 1) * P], ks[u][0:K_MAX, h, :],
                                     start=True, stop=True).then_inc(max_ready, 1)
                return stage

            def turn_max(n, step):
                if n.h % HALF != HALF - 1:
                    return
                pe.wait_ge(max_done, n.count(QT * PERIOD, QT * (n.k + 1)))
                ps_w_free(pe, step)
                h0 = n.h - HALF + 1
                for t in range(QT):
                    last = nc.tensor.transpose(ps_w[0:HALF, t, :], row_max[:, n.u, t, h0:h0 + HALF], ident[:])
                last.then_inc(m_turned, 1)

            def scores(half):
                def stage(n, step):
                    u, h = n.u, n.h
                    if isinstance(n.base, int) and n.base == 0 and n.k == 0:
                        pe.wait_ge(ones_set, 2)
                    if h % HALF == 0 and half == 0:
                        pe.wait_ge(m_loaded[h // HALF], n.count(64, 32 * (n.k // H + 1)))
                    wait(pe, exp_done, n.count(2 * PERIOD, 2 * n.k + half - 1))
                    for i in range(2):
                        t = 2 * half + i
                        last = nc.tensor.matmul(ps_s[half][:, i, :], ks[u][0:K_ALL, h, t * P:(t + 1) * P], qs[u][0:K_ALL, h, :],
                                                start=True, stop=True)
                    last.then_inc(s_ready, 1)
                return stage

            def mix_values(first):
                def stage(n, step):
                    if (n.h % 4 == 0) != first:
                        return
                    t = n.h % 4
                    group = n.k // 4
                    if t == 0:
                        pe.wait_ge(exp_done, n.count(2 * PERIOD, 2 * n.k + 8))
                        wait(pe, o_copied, n.count(PERIOD // 4, group))
                        if n.h == 0:
                            pe.wait_ge(va_done, n.count(2, n.k // H + 1))
                    for j in range(4):
                        h = n.h - t + j
                        last = nc.tensor.matmul(ps_o[VW * j:VW * (j + 1), :], va[n.u][:, t, h * VW:(h + 1) * VW],
                                                probs[:, group % 2, j, t, :], start=t == 0, stop=t == QT - 1)
                    last.then_inc(pv_done, 1)
                return stage

            def turn_output(n, step):
                if n.h % 4 != 3:
                    return
                group = n.k // 4
                pe.wait_ge(o_copied, n.count(PERIOD // 4, group + 1))
                ps_w_free(pe, step)
                for t in range(QT):
                    last = nc.tensor.transpose(ps_w[:, t, :], o_sb[:, group % 2, t * P:(t + 1) * P], ident[:])
                last.then_inc(o_turned, 1)

            def turn_att(q):
                def stage(n, step):
                    if n.h != H - 1:
                        return
                    pe.wait_ge(o_normed, n.count(PERIOD // 4, n.k // 4 + 1))
                    ps_w_free(pe, step)
                    for t in range(2):
                        for c in range(2):
                            last = nc.tensor.transpose(ps_w[:, 2 * t + c, :], att[:, n.u, 2 * q + t, c * P:(c + 1) * P], ident[:])
                    last.then_inc(att_turned, 1)
                return stage

            def project(q):
                def stage(n, step):
                    if n.h != H - 1:
                        return
                    pe.wait_ge(attT_done, n.count(4, 2 * (n.k // H) + q + 1))
                    ps_w_free(pe, step)
                    out = ps_w[:].rearrange("p a b -> p (a b)")
                    for t in range(2):
                        for c in range(2):
                            last = nc.tensor.matmul(out[:, t * D:(t + 1) * D], attT[:, q, 2 * t + c, :], woT[:, c, :], start=c == 0, stop=c == 1)
                    last.then_inc(projected, 1)
                return stage

            walk_heads(pe, [(0, max_products(0)), (L_S, scores(0)), (0, max_products(1)), (L_PV, mix_values(False)), (0, max_products(2)),
                      (L_S, scores(1)), (0, max_products(3)), (L_PV, mix_values(True)), (L_TURN, turn_max), (L_OTURN, turn_output),
                      (A_TURN[0] - H + 1, turn_att(0)), (A_PROJ[0] - H + 1, project(0)),
                      (A_TURN[1] - H + 1, turn_att(1)), (A_PROJ[1] - H + 1, project(1))])

        @block.vector
        def _(dve):
            for i in range(2):
                dve.wait_ge(w_turned, i + 1)
                for c in range(2):
                    last = nc.vector.tensor_copy(woT[:, c, i * P:(i + 1) * P], ps_w[:, c, :])
                last.then_inc(w_copied, 1)

            def maxima(half):
                def stage(n, step):
                    for t in (2 * half, 2 * half + 1):
                        dve.wait_ge(max_ready, n.count(QT * PERIOD, QT * n.k + t + 1))
                        nc.vector.tensor_reduce(row_max[:, n.u, t, n.h:n.h + 1], ps_m[t % 2][:], AX.X, ALU.max).then_inc(max_done, 1)
                return stage

            def low_max(n, step):
                if n.h % HALF != HALF - 1:
                    return
                f = n.h // HALF
                dve.wait_ge(m_high, n.count(4, n.k // HALF + 1))
                nc.vector.scalar_tensor_tensor(m_parts[:, f, 1, :], ps_w[0:HALF].rearrange("p a b -> p (a b)"), -1.0, m_parts[:, f, 0, :],
                                               ALU.mult, ALU.subtract).then_inc(m_low, 1)

            def normalise(n, step):
                if n.h % 4 != 3:
                    return
                group = n.k // 4
                dve.wait_ge(o_turned, n.count(PERIOD // 4, group + 1))
                heads = ps_w[:].rearrange("p t (j w) -> p t j w", w=VW)
                nc.vector.reciprocal(rden[:, group % 2], heads[:, :, :, DK]).then_inc(rden_done, 1)
                dve.wait_ge(rden_done, n.count(PERIOD // 4, group + 1))
                h0 = n.h - 3
                dst = att[:, n.u, :, h0 * DK:(h0 + 4) * DK].rearrange("p t (j d) -> p t j d", d=DK)
                over = rden[:, group % 2].rearrange("p t (j o) -> p t j o", o=1).to_broadcast([P, QT, 4, DK])
                nc.vector.tensor_tensor(dst, heads[:, :, :, 0:DK], over, ALU.mult).then_inc(o_normed, 1)

            def residual(q):
                def stage(n, step):
                    if n.h != H - 1:
                        return
                    dve.wait_ge(projected, n.count(4, 2 * (n.k // H) + q + 1))
                    if q == 0:
                        dve.wait_ge(xr_loaded[n.u], n.count(16, 16 * (n.k // PERIOD + 1)))
                    wait(dve, stored[q], n.count(32, 16 * (n.k // H)))
                    out = ps_w[:].rearrange("p a b -> p (a b)").rearrange("p (t d) -> p t d", d=D)
                    nc.vector.tensor_tensor(xo[:, q], out, xr[n.u][:, 2 * q:2 * q + 2, :], ALU.add).then_inc(added, 1)
                return stage

            walk_heads(dve, [(0, maxima(0)), (L_MSPLIT, low_max), (A_PROJ[0] - H + 2, residual(0)), (A_PROJ[1] - H + 2, residual(1)),
                       (L_ONORM, normalise), (0, maxima(1))])

        @block.scalar
        def _(act):
            def high_max(n, step):
                if n.h % HALF != HALF - 1:
                    return
                f = n.h // HALF
                act.wait_ge(m_turned, n.count(4, n.k // HALF + 1))
                wait(act, m_loaded[f], n.count(64, 32 * (n.k // H)))
                nc.scalar.activation(m_parts[:, f, 0, :], ps_w[0:HALF].rearrange("p a b -> p (a b)"), ACT.Copy, scale=-1.0).then_inc(m_high, 1)

            def exponentials(n, step):
                group = n.k // 4
                if n.h % 4 == 0:
                    wait(act, pv_done, n.count(PERIOD, n.k - 4))
                for half in range(2):
                    act.wait_ge(s_ready, n.count(2 * PERIOD, 2 * n.k + half + 1))
                    nc.scalar.activation(probs[:, group % 2, n.h % 4, 2 * half:2 * half + 2, :], ps_s[half][:], ACT.Exp,
                                         scale=DK ** -0.5).then_inc(exp_done, 1)

            def copy_output(n, step):
                if n.h % 4 != 3:
                    return
                group = n.k // 4
                act.wait_ge(pv_done, n.count(PERIOD, n.k + 1))
                wait(act, o_turned, n.count(PERIOD // 4, group - 1))
                nc.scalar.activation(o_sb[:, group % 2, :], ps_o[:], ACT.Copy).then_inc(o_copied, 1)

            def copy_att(q):
                def stage(n, step):
                    if n.h != H - 1:
                        return
                    act.wait_ge(att_turned, n.count(4, 2 * (n.k // H) + q + 1))
                    nc.scalar.activation(attT[:, q], ps_w[:], ACT.Copy).then_inc(attT_done, 1)
                return stage

            walk_heads(act, [(L_MSPLIT, high_max), (A_TURN[0] - H + 2, copy_att(0)), (A_TURN[1] - H + 2, copy_att(1)), (L_OCOPY, copy_output),
                       (L_S, exponentials)])


def moe_route(nc, tag, dram, x_in, const):
    import concourse.bass as bass
    from concourse import mybir
    from contextlib import ExitStack
    fp32 = mybir.dt.float32
    ALU, ACT, AX = mybir.AluOpType, mybir.ActivationFunctionType, mybir.AxisListType
    P, D, T, E, B = 128, 256, 8192, 64, 4
    TILES = T // P
    order = const["order"]
    x_rows, x_turned_all = const["x_rows"], const["x_turned"]

    with ExitStack() as ctx:
        def sb(name, shape, dt=fp32):
            return ctx.enter_context(nc.sbuf_tensor(f"{tag}r_" + name, shape, dt))

        def pb(name, shape, dt=fp32):
            return ctx.enter_context(nc.psum_tensor(f"{tag}r_" + name, shape, dt))

        def sem(name):
            return nc.alloc_semaphore(f"{tag}r_" + name)

        rwT = sb("rwT", [P, 2, E])
        ident, rw_rows = const["ident_sb"], const["rw_rows"]
        rank_value = const["rank_value_sb"]
        minus_half = sb("minus_half", [P, 1])
        eps = sb("eps", [P, 1])
        zeros = sb("zeros", [P, D + E])
        stats = sb("stats", [P, B, 6])
        mean_var = sb("mean_var", [P, B, 2])
        var_eps = sb("var_eps", [P, B, 1])
        rstd = sb("rstd", [P, B, 1])
        xn = sb("xn", [P, B, D])
        xnT = sb("xnT", [P, B, 2, P])
        top_logit = sb("top_logit", [P, B, 1])
        logit = sb("logit", [P, B, E])
        expd = sb("expd", [P, B, E])
        top8 = sb("top8", [P, B, 8])
        marked = sb("marked", [P, B, E])
        value = sb("value", [P, B, E])
        picked = sb("picked", [P, B, E])
        total = sb("total", [P, B, 1])
        gate = sb("gate", [P, B, E])
        ps_x = [pb(f"ps_x{u}", [P, 2, P]) for u in range(2)]
        ps_l = [pb(f"ps_l{u}", [P, E]) for u in range(2)]
        ps_v = [pb(f"ps_v{u}", [P, P]) for u in range(2)]

        setup, w_turned, w_copied, pad_stored = (sem(n) for n in ("setup", "w_turned", "w_copied", "pad_stored"))
        x_loaded = [sem(f"x_loaded{k}") for k in range(B)]
        xn_stored = [sem(f"xn_stored{k}") for k in range(B)]
        gate_stored = [sem(f"gate_stored{k}") for k in range(B)]
        (stats_done, mv_done, ve_done, rstd_done, xn_done, x_turned, xnT_done, xnT_kept, logits_ready, top_done, logit_done, exp_done, top8_done,
         marked_done, value_done, picked_done, recip_done, gate_done, value_turned, order_done) = (sem(n) for n in (
             "stats_done", "mv_done", "ve_done", "rstd_done", "xn_done", "x_turned", "xnT_done", "xnT_kept", "logits_ready", "top_done", "logit_done",
             "exp_done", "top8_done", "marked_done", "value_done", "picked_done", "recip_done", "gate_done", "value_turned", "order_done"))
        dve_passed = sem("dve_passed")
        block = ctx.enter_context(nc.Block())
        MARK = -1e30

        def tile(n, k):
            return k % 2 * (TILES // 2) + turns(n, k % 2, 2)

        def rows(t, n, k):
            return t[bass.ds(tile(n, k) * P, P), :]

        @block.sync
        def _(sp):
            sp.wait_ge(setup, 3)
            sp.dma_start(dram["rows"][T:T + P, :], zeros[:]).then_inc(pad_stored, 16)

            def load(n, k):
                wait(sp, x_loaded[k], 16 * turns(n, k, B))
                sp.dma_start(x_rows[:, bass.ds(tile(n, k), 1), :], rows(x_in, n, k)).then_inc(x_loaded[k], 16)

            def store_rows(n, k):
                sp.wait_ge(xn_done, n + 1)
                sp.dma_start(rows(dram["rows"], n, k)[:, 0:D], xn[:, k, :]).then_inc(xn_stored[k], 16)

            def store_gates(n, k):
                sp.wait_ge(gate_done, n + 1)
                sp.dma_start(rows(dram["rows"], n, k)[:, D:D + E], gate[:, k, :]).then_inc(gate_stored[k], 16)

            walk(sp, TILES, B, B, [(0, load), (8, store_rows), (16, store_gates)])
            sp.wait_ge(pad_stored, 16)
            for k in range(B):
                sp.wait_ge(xn_stored[k], 16 * TILES // B)
                sp.wait_ge(gate_stored[k], 16 * TILES // B)

        @block.gpsimd
        def _(pool):
            nc.gpsimd.memset(minus_half[:], -0.5).then_inc(setup, 1)
            nc.gpsimd.memset(eps[:], 1e-5).then_inc(setup, 1)
            nc.gpsimd.memset(zeros[:], 0.0).then_inc(setup, 1)
            pool.wait_ge(setup, 3)

            def inverse_deviation(n, k):
                pool.wait_ge(mv_done, n + 1)
                nc.gpsimd.tensor_tensor(var_eps[:, k], mean_var[:, k, 1:2], eps[:], ALU.add).then_inc(ve_done, 1)
                pool.wait_ge(ve_done, n + 1)
                wait(pool, xn_done, n - B + 1)
                nc.gpsimd.tensor_tensor(rstd[:, k], var_eps[:, k], minus_half[:], ALU.pow).then_inc(rstd_done, 1)

            walk(pool, TILES, B, B, [(0, inverse_deviation)])

        @block.vector
        def _(dve):
            dve.wait_ge(w_turned, 1)
            nc.vector.tensor_copy(rwT[:], ps_x[0][:, :, 0:E]).then_inc(w_copied, 1)

            def statistics(n, k):
                dve.wait_ge(x_loaded[k], 16 * (turns(n, k, B) + 1))
                nc.vector.bn_stats(stats[:, k, :], x_rows[:, bass.ds(tile(n, k), 1), :]).then_inc(stats_done, 1)

            def aggregate(n, k):
                dve.wait_ge(stats_done, n + 1)
                passed_by(dve, dve_passed)
                nc.vector.bn_aggr(mean_var[:, k, :], stats[:, k, :]).then_inc(mv_done, 1)

            def normalise(n, k):
                dve.wait_ge(rstd_done, n + 1)
                wait(dve, x_turned, n - B + 1)
                wait(dve, xn_stored[k], 16 * turns(n, k, B))
                nc.vector.tensor_scalar(xn[:, k, :], x_rows[:, bass.ds(tile(n, k), 1), :], mean_var[:, k, 0:1], rstd[:, k],
                                        ALU.subtract, ALU.mult).then_inc(xn_done, 1)

            def maximum(n, k):
                dve.wait_ge(logits_ready, n + 1)
                nc.vector.tensor_reduce(top_logit[:, k], ps_l[k % 2][:], AX.X, ALU.max).then_inc(top_done, 1)

            def shift(n, k):
                dve.wait_ge(top_done, n + 1)
                wait(dve, exp_done, n - B + 1)
                nc.vector.tensor_scalar(logit[:, k, :], ps_l[k % 2][:], top_logit[:, k], -104.0, ALU.subtract, ALU.max).then_inc(logit_done, 1)

            def eight_largest(n, k):
                dve.wait_ge(logit_done, n + 1)
                passed_by(dve, dve_passed)
                nc.vector.max(top8[:, k, :], logit[:, k, :]).then_inc(top8_done, 1)

            def mark(n, k):
                dve.wait_ge(top8_done, n + 1)
                passed_by(dve, dve_passed)
                nc.vector.match_replace(marked[:, k, :], top8[:, k, :], logit[:, k, :], MARK).then_inc(marked_done, 1)

            def values(n, k):
                dve.wait_ge(marked_done, n + 1)
                wait(dve, value_turned, n - B + 1)
                nc.vector.tensor_scalar(value[:, k, :], marked[:, k, :], MARK / 2, rank_value[:, bass.ds(n, 1)], ALU.is_lt, ALU.mult).then_inc(value_done, 1)

            def pick(n, k):
                dve.wait_ge(exp_done, n + 1)
                dve.wait_ge(marked_done, n + 1)
                wait(dve, gate_done, n - B + 1)
                nc.vector.scalar_tensor_tensor(picked[:, k, :], marked[:, k, :], MARK / 2, expd[:, k, :], ALU.is_lt, ALU.mult,
                                               accum_out=total[:, k]).then_inc(picked_done, 1)

            def invert(n, k):
                dve.wait_ge(picked_done, n + 1)
                nc.vector.reciprocal(total[:, k], total[:, k]).then_inc(recip_done, 1)

            walk(dve, TILES, B, B, [(0, statistics), (10, invert), (9, pick), (9, values), (8, mark), (7, eight_largest),
                                    (0, aggregate), (6, shift), (5, maximum), (1, normalise)])

        @block.scalar
        def _(act):
            def evacuate_x(n, k):
                act.wait_ge(x_turned, n + 1)
                wait(act, logits_ready, n - B + 1)
                nc.scalar.activation(xnT[:, k], ps_x[k % 2][:], ACT.Copy).then_inc(xnT_done, 1)
                nc.scalar.activation(x_turned_all[:, :, bass.ds(tile(n, k) * P, P)], ps_x[k % 2][:], ACT.Copy).then_inc(xnT_kept, 1)

            def gates(n, k):
                act.wait_ge(recip_done, n + 1)
                wait(act, gate_stored[k], 16 * turns(n, k, B))
                nc.scalar.activation(gate[:, k, :], picked[:, k, :], ACT.Copy, scale=total[:, k]).then_inc(gate_done, 1)

            def exponential(n, k):
                act.wait_ge(logit_done, n + 1)
                wait(act, picked_done, n - B + 1)
                nc.scalar.activation(expd[:, k, :], logit[:, k, :], ACT.Exp).then_inc(exp_done, 1)

            def put_order(n, k):
                act.wait_ge(value_turned, n + 1)
                half = slice(k % 2 * E, (k % 2 + 1) * E)
                nc.scalar.activation(order[half, bass.ds(turns(n, k % 2, 2) * P, P)], ps_v[k % 2][half, :], ACT.Copy).then_inc(order_done, 1)

            walk(act, TILES, B, B, [(3, evacuate_x), (7, exponential), (11, put_order), (11, gates)])
            act.wait_ge(order_done, TILES)
            act.wait_ge(xnT_kept, TILES)

        @block.tensor
        def _(pe):
            for c in range(2):
                last = nc.tensor.transpose(ps_x[0][:, c, 0:E], rw_rows[:, c * P:(c + 1) * P], ident[0:E, 0:E])
            last.then_inc(w_turned, 1)
            pe.wait_ge(w_copied, 1)

            def turn_x(n, k):
                pe.wait_ge(xn_done, n + 1)
                wait(pe, xnT_kept, n - 1)
                for c in range(2):
                    last = nc.tensor.transpose(ps_x[k % 2][:, c, :], xn[:, k, c * P:(c + 1) * P], ident[:])
                last.then_inc(x_turned, 1)

            def logits(n, k):
                pe.wait_ge(xnT_done, n + 1)
                wait(pe, logit_done, n - 1)
                for c in range(2):
                    last = nc.tensor.matmul(ps_l[k % 2][:], xnT[:, k, c, :], rwT[:, c, :], start=c == 0, stop=c == 1)
                last.then_inc(logits_ready, 1)

            def turn_values(n, k):
                pe.wait_ge(value_done, n + 1)
                wait(pe, order_done, n - 1)
                half = slice(k % 2 * E, (k % 2 + 1) * E)
                nc.tensor.matmul(ps_v[k % 2][half, :], value[:, k, :], ident[:], start=True, stop=True).then_inc(value_turned, 1)

            walk(pe, TILES, B, B, [(3, turn_x), (4, logits), (10, turn_values)])


def moe_shared(nc, tag, x_out, const):
    import concourse.bass as bass
    from concourse import mybir
    from contextlib import ExitStack
    fp32 = mybir.dt.float32
    ALU, ACT = mybir.AluOpType, mybir.ActivationFunctionType
    P, D, T, E, SF, CAP = 128, 256, 8192, 64, 192, 128
    SR = SF - P
    S = 512
    ROUNDS, B = CAP // 8, 4
    assert T // S == ROUNDS
    order, slots, x_rows, x_turned = const["order"], const["slots"], const["x_rows"], const["x_turned"]

    with ExitStack() as ctx:
        def sb(name, shape, dt=fp32):
            return ctx.enter_context(nc.sbuf_tensor(f"{tag}s_" + name, shape, dt))

        def pb(name, shape, dt=fp32):
            return ctx.enter_context(nc.psum_tensor(f"{tag}s_" + name, shape, dt))

        def sem(name):
            return nc.alloc_semaphore(f"{tag}s_" + name)

        w_gu = const["ws_gate_up_sb"]
        w_d = const["ws_down_sb"]
        ident, reverse = const["ident_sb"], const["reverse_sb"]
        spare_row = const["spare_row_sb"]
        act_g = sb("act_g", [P, 2, 2, S])
        up = sb("up", [P, 2, 2, S])
        hT = sb("hT", [P, 2, 2, S])
        xo = sb("xo", [P, 2, 4, D])
        top8 = sb("top8", [P, B, 8])
        first = sb("first", [P, CAP])
        halves = sb("halves", [P, 2 * E])
        more = sb("more", [P, E])
        taken = sb("taken", [P, E])
        empty = sb("empty", [P, E])
        number = sb("number", [P, E])
        ps_h = [[pb(f"ps_h{u}{i}", [P, S]) for i in range(3)] for u in range(2)]
        ps_d = [pb(f"ps_d{q}", [P, 2, D]) for q in range(2)]
        ps_t, ps_r = ps_d[0][:, 0, 0:2 * E], ps_d[1][:, 0, 0:E]

        stored = [sem(f"stored{u}") for u in range(2)]
        gated, silu_done, h_done, down_done, down_copied, added = (
            sem(n) for n in ("gated", "silu_done", "h_done", "down_done", "down_copied", "added"))
        (top_found, top_kept, top_removed, first_turned, halves_done, second_reversed, more_done, taken_done, empty_done, number_done,
         slots_done) = (sem(n) for n in (
             "top_found", "top_kept", "top_removed", "first_turned", "halves_done", "second_reversed", "more_done", "taken_done",
             "empty_done", "number_done", "slots_done"))
        dve_passed = sem("dve_passed")
        block = ctx.enter_context(nc.Block())

        @block.sync
        def _(sp):
            def store(r, k):
                sp.wait_ge(added, 2 * (r + 1))
                sp.dma_start(x_out[bass.ds(r * S, S), :].rearrange("(t p) d -> p t d", p=P), xo[:, k % 2]).then_inc(stored[k % 2], 16)

            walk(sp, ROUNDS, B, B, [(0, store)])
            for u in range(2):
                sp.wait_ge(stored[u], 16 * ROUNDS // 2)

        @block.tensor
        def _(pe):
            def gate_up(r, k):
                wait(pe, silu_done, 2 * (r - 1))
                for i in range(3):
                    for c in range(2):
                        last = nc.tensor.matmul(ps_h[k % 2][i][:], w_gu[:, c, i, :], x_turned[:, c, bass.ds(r * S, S)], start=c == 0, stop=c == 1)
                    last.then_inc(gated, 1)

            def down(r, k):
                pe.wait_ge(h_done, 2 * (r + 1))
                for q in range(2):
                    wait(pe, down_copied, 2 * r + q - 1)
                    for t in range(2):
                        at = (2 * q + t) * P
                        nc.tensor.matmul(ps_d[q][:, t, :], hT[:, k % 2, 0, at:at + P], w_d[:, 0, :], start=True, stop=False)
                        last = nc.tensor.matmul(ps_d[q][:, t, :], hT[0:SR, k % 2, 1, at:at + P], w_d[0:SR, 1, :], start=False, stop=True)
                    last.then_inc(down_done, 1)

            walk(pe, ROUNDS, B, B, [(0, gate_up), (1, down)])
            pe.wait_ge(down_copied, 2 * ROUNDS)
            pe.wait_ge(top_kept, ROUNDS)
            nc.tensor.transpose(ps_t, first[:], ident[:]).then_inc(first_turned, 1)
            pe.wait_ge(halves_done, 1)
            nc.tensor.matmul(ps_r, reverse[:], halves[:, E:2 * E], start=True, stop=True).then_inc(second_reversed, 1)

        @block.scalar
        def _(act):
            def silu(r, k):
                wait(act, h_done, 2 * (r - 1))
                act.wait_ge(gated, 3 * r + 1)
                nc.scalar.activation(act_g[:, k % 2, 0, :], ps_h[k % 2][0][:], ACT.Silu)
                act.wait_ge(gated, 3 * r + 2)
                nc.scalar.activation(up[:, k % 2, 0, :], ps_h[k % 2][1][:], ACT.Copy).then_inc(silu_done, 1)
                act.wait_ge(gated, 3 * r + 3)
                nc.scalar.activation(act_g[0:SR, k % 2, 1, :], ps_h[k % 2][2][0:SR, :], ACT.Silu)
                nc.scalar.activation(up[0:SR, k % 2, 1, :], ps_h[k % 2][2][SR:P, :], ACT.Copy).then_inc(silu_done, 1)

            def copy_down(r, k):
                wait(act, stored[k % 2], 16 * turns(r, k % 2, 2))
                for q in range(2):
                    act.wait_ge(down_done, 2 * r + q + 1)
                    nc.scalar.activation(xo[:, k % 2, 2 * q:2 * q + 2, :], ps_d[q][:], ACT.Copy).then_inc(down_copied, 1)

            def keep(r, k):
                act.wait_ge(top_found, r + 1)
                nc.scalar.activation(first[:, bass.ds(r * 8, 8)], top8[:, k, :], ACT.Copy).then_inc(top_kept, 1)

            walk(act, ROUNDS, B, B, [(0, silu), (1, keep), (1, copy_down)])

        @block.gpsimd
        def _(pool):
            def hidden(r, k):
                wait(pool, down_done, 2 * (r - 1))
                for i, n in enumerate((P, SR)):
                    pool.wait_ge(silu_done, 2 * r + i + 1)
                    nc.gpsimd.tensor_tensor(hT[0:n, k % 2, i, :], act_g[0:n, k % 2, i, :], up[0:n, k % 2, i, :], ALU.mult).then_inc(h_done, 1)

            def add(r, k):
                for q in range(2):
                    half = xo[:, k % 2, 2 * q:2 * q + 2, :]
                    pool.wait_ge(down_copied, 2 * r + q + 1)
                    nc.gpsimd.tensor_tensor(half, half, x_rows[:, bass.ds(r * 4 + 2 * q, 2), :], ALU.add).then_inc(added, 1)

            walk(pool, ROUNDS, B, B, [(0, hidden), (1, add)])

        @block.vector
        def _(dve):
            def find(r, k):
                wait(dve, top_removed, r)
                wait(dve, top_kept, r - B + 1)
                passed_by(dve, dve_passed)
                nc.vector.max(top8[:, k, :], order[:]).then_inc(top_found, 1)

            def remove(r, k):
                dve.wait_ge(top_found, r + 1)
                passed_by(dve, dve_passed)
                nc.vector.match_replace(order[:], top8[:, k, :], order[:], 0.0).then_inc(top_removed, 1)

            walk(dve, ROUNDS, B, B, [(0, find), (0, remove)])
            dve.wait_ge(first_turned, 1)
            nc.vector.tensor_copy(halves[:], ps_t).then_inc(halves_done, 1)
            dve.wait_ge(second_reversed, 1)
            dve.wait_ge(halves_done, 1)
            nc.vector.scalar_tensor_tensor(more[:], halves[:, 0:E], 0.5, ps_r, ALU.is_lt, ALU.mult).then_inc(more_done, 1)
            dve.wait_ge(more_done, 1)
            nc.vector.tensor_tensor(taken[:], halves[:, 0:E], more[:], ALU.add).then_inc(taken_done, 1)
            dve.wait_ge(taken_done, 1)
            nc.vector.tensor_scalar(empty[:], taken[:], 0.5, spare_row[:], ALU.is_lt, ALU.mult).then_inc(empty_done, 1)
            nc.vector.tensor_scalar(number[:], taken[:], -1.0, float(T), ALU.mult, ALU.add).then_inc(number_done, 1)
            dve.wait_ge(empty_done, 1)
            dve.wait_ge(number_done, 1)
            nc.vector.tensor_tensor(slots[:], number[:], empty[:], ALU.add).then_inc(slots_done, 1)
            dve.wait_ge(slots_done, 1)


def moe_experts(nc, tag, dram, x_out, w_gate, w_up, w_down, const):
    import concourse.bass as bass
    from concourse import mybir
    from contextlib import ExitStack
    fp32, u32 = mybir.dt.float32, mybir.dt.uint32
    ALU, ACT = mybir.AluOpType, mybir.ActivationFunctionType
    P, D, E, F, B = 128, 256, 64, 192, 8
    FR = F - P
    slots = const["slots"]

    with ExitStack() as ctx:
        def sb(name, shape, dt=fp32):
            return ctx.enter_context(nc.sbuf_tensor(f"{tag}e_" + name, shape, dt))

        def pb(name, shape, dt=fp32):
            return ctx.enter_context(nc.psum_tensor(f"{tag}e_" + name, shape, dt))

        def sem(name):
            return nc.alloc_semaphore(f"{tag}e_" + name)

        ident = const["ident_sb"]
        w_gu = sb("w_gu", [P, B, 2, 2 * F])
        w_d = sb("w_d", [P, B, 2, D])
        index = sb("index", [P, B, 1], u32)
        xg = sb("xg", [P, B, D + E])
        xgT = sb("xgT", [P, 2, 2, P])
        act_g = sb("act_g", [P, 2, 2, P])
        hT = sb("hT", [P, 2, 2, P])
        y = sb("y", [P, B, D])
        ps_x = [pb(f"ps_x{u}", [P, 2, P]) for u in range(2)]
        ps_h = [pb(f"ps_h{u}", [P, 3, P]) for u in range(2)]
        ps_y = [pb(f"ps_y{u}", [P, D]) for u in range(2)]

        w_loaded = [sem(f"w_loaded{k}") for k in range(B)]
        gathered = [sem(f"gathered{k}") for k in range(B)]
        index_done, x_turned, xT_done, h_ready, silu_done, h_done, y_ready, y_done, scattered = (sem(n) for n in (
            "index_done", "x_turned", "xT_done", "h_ready", "silu_done", "h_done", "y_ready", "y_done", "scattered"))
        pool_passed = sem("pool_passed")
        block = ctx.enter_context(nc.Block())

        @block.sync
        def _(sp):
            def load(e, k):
                wait(sp, y_ready, e - B + 1)
                for i, w in enumerate((w_gate, w_up)):
                    sp.dma_start(w_gu[:, k, :, i * F:(i + 1) * F], w[bass.ds(e, 1)].rearrange("o (c p) f -> p (o c) f", p=P)).then_inc(w_loaded[k], 16)
                sp.dma_start(w_d[:, k, 0:1, :], w_down[bass.ds(e, 1), 0:P].rearrange("o p d -> p o d")).then_inc(w_loaded[k], 16)
                sp.dma_start(w_d[0:FR, k, 1:2, :], w_down[bass.ds(e, 1), P:F].rearrange("o p d -> p o d")).then_inc(w_loaded[k], 16)

            walk(sp, E, B, B, [(0, load)])

        @block.gpsimd
        def _(pool):
            def gather(e, k):
                wait(pool, y_done, e - B + 1)
                nc.gpsimd.tensor_copy(index[:, k], slots[:, bass.ds(e, 1)]).then_inc(index_done, 1)
                pool.wait_ge(index_done, e + 1)
                passed_by(pool, pool_passed)
                pool.indirect_dma_start(xg[:, k, :], None, dram["rows"][:, :], bass.IndirectOffsetOnAxis(index[:, k], 0)).then_inc(gathered[k], 16)

            def scatter(e, k):
                pool.wait_ge(y_done, e + 1)
                wait(pool, scattered, 16 * e)
                passed_by(pool, pool_passed)
                pool.indirect_dma_start(x_out[:, :], bass.IndirectOffsetOnAxis(index[:, k], 0), y[:, k, :], None,
                                        compute_op=ALU.add).then_inc(scattered, 16)

            walk(pool, E, B, B, [(7, scatter), (0, gather)])
            pool.wait_ge(scattered, 16 * E)

        @block.tensor
        def _(pe):
            def turn(e, k):
                u = k % 2
                pe.wait_ge(gathered[k], 16 * (turns(e, k, B) + 1))
                wait(pe, xT_done, e - 1)
                for c in range(2):
                    last = nc.tensor.transpose(ps_x[u][:, c, :], xg[:, k, c * P:(c + 1) * P], ident[:])
                last.then_inc(x_turned, 1)

            def gate_up(e, k):
                u = k % 2
                pe.wait_ge(w_loaded[k], 64 * (turns(e, k, B) + 1))
                pe.wait_ge(xT_done, e + 1)
                wait(pe, h_done, e - 1)
                for i in range(3):
                    for c in range(2):
                        last = nc.tensor.matmul(ps_h[u][:, i, :], w_gu[:, k, c, i * P:(i + 1) * P], xgT[:, u, c, :], start=c == 0, stop=c == 1)
                last.then_inc(h_ready, 1)

            def down(e, k):
                u = k % 2
                pe.wait_ge(h_done, e + 1)
                wait(pe, y_done, e - 1)
                nc.tensor.matmul(ps_y[u][:], hT[:, u, 0, :], w_d[:, k, 0, :], start=True, stop=False)
                last = nc.tensor.matmul(ps_y[u][:], hT[0:FR, u, 1, :], w_d[0:FR, k, 1, :], start=False, stop=True)
                last.then_inc(y_ready, 1)

            walk(pe, E, B, B, [(2, turn), (3, gate_up), (4, down)])

        @block.scalar
        def _(act):
            def copy_x(e, k):
                u = k % 2
                act.wait_ge(x_turned, e + 1)
                wait(act, h_ready, e - 1)
                nc.scalar.activation(xgT[:, u], ps_x[u][:], ACT.Copy).then_inc(xT_done, 1)

            def silu(e, k):
                u = k % 2
                act.wait_ge(h_ready, e + 1)
                wait(act, h_done, e - 1)
                nc.scalar.activation(act_g[:, u, 0, :], ps_h[u][:, 0, :], ACT.Silu)
                nc.scalar.activation(act_g[0:FR, u, 1, :], ps_h[u][0:FR, 1, :], ACT.Silu).then_inc(silu_done, 1)

            walk(act, E, B, B, [(2, copy_x), (3, silu)])

        @block.vector
        def _(dve):
            def hidden(e, k):
                u = k % 2
                dve.wait_ge(silu_done, e + 1)
                wait(dve, y_ready, e - 1)
                nc.vector.tensor_tensor(hT[0:FR, u, 0, :], act_g[0:FR, u, 0, :], ps_h[u][FR:P, 1, :], ALU.mult)
                nc.vector.tensor_tensor(hT[FR:P, u, 0, :], act_g[FR:P, u, 0, :], ps_h[u][0:FR, 2, :], ALU.mult)
                nc.vector.tensor_tensor(hT[0:FR, u, 1, :], act_g[0:FR, u, 1, :], ps_h[u][FR:P, 2, :], ALU.mult).then_inc(h_done, 1)

            def weigh(e, k):
                u = k % 2
                dve.wait_ge(y_ready, e + 1)
                wait(dve, scattered, 16 * (e - B + 1))
                nc.vector.tensor_scalar(y[:, k, :], ps_y[u][:], xg[:, k, bass.ds(e + D, 1)], None, ALU.mult).then_inc(y_done, 1)

            walk(dve, E, B, B, [(3, hidden), (4, weigh)])


def forget_attention(nc, x_in, x_out, const):
    import concourse.bass as bass
    from concourse import mybir
    from contextlib import ExitStack
    fp32 = mybir.dt.float32
    ALU, ACT = mybir.AluOpType, mybir.ActivationFunctionType
    P, D, H, DK, B = 128, 256, 16, 16, 8
    STEPS, COLS, GROUPS = 16, 8, 64
    VW = 2 * DK
    VF = D + H
    L_NORM, L_TURN, L_PROJ, L_BIAS, L_NEG, L_EXP, L_PHI, L_LOG, L_QK = 1, 2, 3, 4, 5, 6, 7, 8, 8
    L_BD, L_LSUM, L_DECAY, L_EXPAND, L_S, L_PV, L_ROWS, L_ADD_ROWS, L_OUT = 9, 9, 9, 9, 10, 11, 10, 11, 12

    with ExitStack() as ctx:
        def sb(name, shape, dt=fp32):
            return ctx.enter_context(nc.sbuf_tensor("b_" + name, shape, dt))

        def pb(name, shape, dt=fp32):
            return ctx.enter_context(nc.psum_tensor("b_" + name, shape, dt))

        def sem(name):
            return nc.alloc_semaphore("b_" + name)

        w_qk = sb("w_qk", [P, 2, 2 * D])
        w_vf = sb("w_vf", [P, 2, VF])
        w_o = sb("w_o", [P, 2, D])
        w_rows, f_rows = const["b_w_rows"], const["b_f_rows"]
        b_qk, b_vf, b_o = const["b_qk"], const["b_vf"], const["b_o"]
        ident = const["ident_sb"]
        later = const["later_sb"]
        upto = const["upto_sb"]
        own = const["own_sb"]
        head_rows = const["head_rows_sb"]
        minus_half = sb("minus_half", [P, 1])
        eps = sb("eps", [P, 1])
        xt = sb("xt", [P, B, D])
        stats = sb("stats", [P, B, 6])
        mean_var = sb("mean_var", [P, B, 2])
        var_eps = sb("var_eps", [P, B, 1])
        rstd = sb("rstd", [P, B, 1])
        xn = sb("xn", [P, B, D])
        xnT = sb("xnT", [P, B, 2, P])
        z_qk = sb("z_qk", [P, B, 2 * D])
        e_qk = sb("e_qk", [P, 2, 2 * D])
        phi = sb("phi", [P, 2, 2 * D])
        v_aug = sb("v_aug", [P, B, H, VW])
        z_f = sb("z_f", [P, B, H])
        low_f = sb("low_f", [P, B, H])
        abs_f = sb("abs_f", [P, B, H])
        log_f = sb("log_f", [P, B, H])
        log_upto = sb("log_upto", [P, 2, H, STEPS])
        decay = sb("decay", [P, 2, H, STEPS])
        spread = sb("spread", [P, 2, H, STEPS, COLS])
        q_bd = sb("q_bd", [P, 2, 2, COLS, P])
        kT = sb("kT", [P, 4, 2, P])
        weight = sb("weight", [P, 2, H, P])
        o_sb = sb("o_sb", [P, 2, 4 * P])
        den = sb("den", [P, 2, H])
        att = sb("att", [P, 2, D])
        attT = sb("attT", [P, 2, 2, P])
        xr = sb("xr", [P, B, D])
        xo = sb("xo", [P, B, D])
        ps_xl = pb("ps_xl", [P, 2, 2 * P])
        ps_qk = pb("ps_qk", [P, 2 * D])
        ps_vf = pb("ps_vf", [P, VF])
        ps_t = pb("ps_t", [P, 4, P])
        ps_s = [pb(f"ps_s{u}", [P, 4, P]) for u in range(2)]
        ps_o = pb("ps_o", [P, 4, P])
        ps_w = pb("ps_w", [P, 4, P])

        setup, w_turned, w_copied = (sem(n) for n in ("setup", "w_turned", "w_copied"))
        x_loaded = [sem(f"x_loaded{k}") for k in range(B)]
        xr_loaded = [sem(f"xr_loaded{k}") for k in range(B)]
        stored = [sem(f"stored{k}") for k in range(B)]
        (stats_done, mv_done, ve_done, rstd_done, xn_done, x_turned, xnT_done, qk_ready, vf_ready, qk_biased, v_biased, f_biased,
         neg_done, low_done, abs_done, exp_done, f_exp_done, f_log_done, phi_done, log_done, qk_turned, bd_done, kT_done, upto_done,
         sums_ready, decay_done, spread_done, s_ready, weight_done, o_ready, o_copied, o_turned, den_done, att_done, att_turned,
         attT_done, out_ready, rows_ready, added) = (sem(n) for n in (
             "stats_done", "mv_done", "ve_done", "rstd_done", "xn_done", "x_turned", "xnT_done", "qk_ready", "vf_ready", "qk_biased",
             "v_biased", "f_biased", "neg_done", "low_done", "abs_done", "exp_done", "f_exp_done", "f_log_done", "phi_done", "log_done",
             "qk_turned", "bd_done", "kT_done", "upto_done", "sums_ready", "decay_done", "spread_done", "s_ready", "weight_done",
             "o_ready", "o_copied", "o_turned", "den_done", "att_done", "att_turned", "attT_done", "out_ready", "rows_ready", "added"))
        dve_passed = sem("dve_passed")
        block = ctx.enter_context(nc.Block())

        def group_rows(t, n):
            return t.rearrange("(s c) d -> s c d", s=STEPS)[:, bass.ds(n * COLS, COLS), :]

        @block.sync
        def _(sp):
            def load(n, k):
                wait(sp, xn_done, n - B + 1)
                sp.dma_start(xt[:, k, :], group_rows(x_in, n)).then_inc(x_loaded[k], 16)

            def load_rows(n, k):
                wait(sp, added, n - B + 1)
                sp.dma_start(xr[:, k, :], group_rows(x_in, n)).then_inc(xr_loaded[k], 16)

            def store(n, k):
                sp.wait_ge(added, n + 1)
                sp.dma_start(group_rows(x_out, n), xo[:, k, :]).then_inc(stored[k], 16)

            walk(sp, GROUPS, B, B, [(0, load), (L_ROWS, load_rows), (L_OUT + 3, store)])
            for k in range(B):
                sp.wait_ge(stored[k], 16 * GROUPS // B)

        @block.gpsimd
        def _(pool):
            nc.gpsimd.memset(minus_half[:], -0.5).then_inc(setup, 1)
            nc.gpsimd.memset(eps[:], 1e-5).then_inc(setup, 1)
            nc.gpsimd.memset(v_aug[:], 0.0).then_inc(setup, 1)
            pool.wait_ge(setup, 3)
            nc.gpsimd.memset(v_aug[:, :, :, DK:DK + 1], 1.0).then_inc(setup, 1)

            def inverse_deviation(n, k):
                pool.wait_ge(mv_done, n + 1)
                nc.gpsimd.tensor_tensor(var_eps[:, k], mean_var[:, k, 1:2], eps[:], ALU.add).then_inc(ve_done, 1)
                pool.wait_ge(ve_done, n + 1)
                wait(pool, xn_done, n - B + 1)
                nc.gpsimd.tensor_tensor(rstd[:, k], var_eps[:, k], minus_half[:], ALU.pow).then_inc(rstd_done, 1)

            def log_gates(n, k):
                pool.wait_ge(log_done, n + 1)
                wait(pool, sums_ready, n - 1)
                nc.gpsimd.tensor_tensor(log_upto[:, k % 2], log_f[:, k, :].rearrange("p (h o) -> p h o", o=1).to_broadcast([P, H, STEPS]),
                                        upto[:].rearrange("p (o t) -> p o t", o=1).to_broadcast([P, H, STEPS]), ALU.mult).then_inc(upto_done, 1)

            def expand(n, k):
                pool.wait_ge(decay_done, n + 1)
                wait(pool, weight_done, 4 * (n - 1))
                nc.gpsimd.tensor_tensor(spread[:, k % 2].rearrange("p h t c -> p (h t) c"),
                                        decay[:, k % 2].rearrange("p h (t o) -> p (h t) o", o=1).to_broadcast([P, H * STEPS, COLS]),
                                        own[:].rearrange("p (o t) -> p o t", o=1).to_broadcast([P, H, P]), ALU.mult).then_inc(spread_done, 1)

            def rows(n, k):
                pool.wait_ge(xr_loaded[k], 16 * (turns(n, k, B) + 1))
                nc.gpsimd.tensor_tensor(xr[:, k, :], xr[:, k, :], b_o[:], ALU.add).then_inc(rows_ready, 1)

            walk(pool, GROUPS, B, B, [(0, inverse_deviation), (L_LOG, log_gates), (L_ADD_ROWS, rows), (L_EXPAND, expand)])

        @block.vector
        def _(dve):
            for i in range(5):
                dve.wait_ge(w_turned, i + 1)
                bank = (ps_t, ps_w)[i % 2]
                if i < 4:
                    dst = (w_qk[:, :, 0:D], w_qk[:, :, D:2 * D], w_vf[:, :, 0:D], w_o[:])[i]
                    nc.vector.tensor_copy(dst, bank[:].rearrange("p (c r) a -> p c (r a)", c=2)).then_inc(w_copied, 1)
                else:
                    nc.vector.tensor_copy(w_vf[:, :, D:VF], bank[:, 0:2, 0:H]).then_inc(w_copied, 1)

            def statistics(n, k):
                dve.wait_ge(x_loaded[k], 16 * (turns(n, k, B) + 1))
                nc.vector.bn_stats(stats[:, k, :], xt[:, k, :]).then_inc(stats_done, 1)

            def aggregate(n, k):
                dve.wait_ge(stats_done, n + 1)
                passed_by(dve, dve_passed)
                nc.vector.bn_aggr(mean_var[:, k, :], stats[:, k, :]).then_inc(mv_done, 1)

            def normalise(n, k):
                dve.wait_ge(rstd_done, n + 1)
                wait(dve, x_turned, n - B + 1)
                nc.vector.tensor_scalar(xn[:, k, :], xt[:, k, :], mean_var[:, k, 0:1], rstd[:, k],
                                        ALU.subtract, ALU.mult).then_inc(xn_done, 1)

            def add_bias(n, k):
                dve.wait_ge(qk_ready, n + 1)
                nc.vector.tensor_tensor(z_qk[:, k, :], ps_qk[:], b_qk[:], ALU.add).then_inc(qk_biased, 1)
                dve.wait_ge(vf_ready, n + 1)
                if isinstance(n, int) and n == 0:
                    dve.wait_ge(setup, 4)
                wait(dve, o_ready, n - B + 1)
                nc.vector.tensor_tensor(v_aug[:, k, :, 0:DK], ps_vf[:, 0:D].rearrange("p (h d) -> p h d", d=DK),
                                        b_vf[:, 0:D].rearrange("p (h d) -> p h d", d=DK), ALU.add).then_inc(v_biased, 1)
                nc.vector.tensor_tensor(z_f[:, k, :], ps_vf[:, D:VF], b_vf[:, D:VF], ALU.add).then_inc(f_biased, 1)

            def negative_part(n, k):
                dve.wait_ge(qk_biased, n + 1)
                dve.wait_ge(f_biased, n + 1)
                wait(dve, phi_done, n - 1)
                nc.vector.tensor_scalar(e_qk[:, k % 2, :], z_qk[:, k, :], 0.0, None, ALU.min).then_inc(neg_done, 1)
                nc.vector.tensor_scalar(low_f[:, k, :], z_f[:, k, :], 0.0, None, ALU.min).then_inc(low_done, 1)
                dve.wait_ge(low_done, n + 1)
                nc.vector.scalar_tensor_tensor(abs_f[:, k, :], low_f[:, k, :], 2.0, z_f[:, k, :], ALU.mult, ALU.subtract).then_inc(abs_done, 1)

            def features(n, k):
                dve.wait_ge(exp_done, n + 1)
                wait(dve, qk_turned, n - 1)
                nc.vector.scalar_tensor_tensor(phi[:, k % 2, :], z_qk[:, k, :], 0.0, e_qk[:, k % 2, :], ALU.max, ALU.add).then_inc(phi_done, 1)
                dve.wait_ge(f_log_done, n + 1)
                nc.vector.tensor_tensor(log_f[:, k, :], low_f[:, k, :], abs_f[:, k, :], ALU.subtract).then_inc(log_done, 1)

            def block_queries(n, k):
                dve.wait_ge(kT_done, n + 1)
                wait(dve, s_ready, 4 * (n - 1))
                for half in range(2):
                    last = nc.vector.tensor_tensor(q_bd[:, k % 2, half], ps_t[:, half, :].rearrange("p (o t) -> p o t", o=1).to_broadcast([P, COLS, P]),
                                                   head_rows[:].rearrange("p (j o) -> p j o", o=1).to_broadcast([P, COLS, P]), ALU.mult)
                last.then_inc(bd_done, 1)

            def weigh(i):
                def stage(n, k):
                    dve.wait_ge(s_ready, 4 * n + i + 1)
                    if i == 0:
                        dve.wait_ge(spread_done, n + 1)
                        wait(dve, o_ready, n - 1)
                    heads = slice(4 * i, 4 * i + 4)
                    nc.vector.tensor_tensor(weight[:, k % 2, heads, :], ps_s[i % 2][:], spread[:, k % 2, heads].rearrange("p h t c -> p h (t c)"),
                                            ALU.mult).then_inc(weight_done, 1)
                return stage

            def divide(n, k):
                dve.wait_ge(o_turned, n + 1)
                heads = ps_w[:].rearrange("p i (j w) -> p (i j) w", w=VW)
                nc.vector.tensor_scalar(den[:, k % 2, :], heads[:, :, DK], 1e-6, None, ALU.add).then_inc(den_done, 1)
                dve.wait_ge(den_done, 2 * n + 1)
                nc.vector.reciprocal(den[:, k % 2, :], den[:, k % 2, :]).then_inc(den_done, 1)
                dve.wait_ge(den_done, 2 * n + 2)
                wait(dve, att_turned, n - 1)
                nc.vector.tensor_tensor(att[:, k % 2, :].rearrange("p (h d) -> p h d", d=DK), heads[:, :, 0:DK],
                                        den[:, k % 2, :].rearrange("p (h o) -> p h o", o=1).to_broadcast([P, H, DK]), ALU.mult).then_inc(att_done, 1)

            def add(n, k):
                dve.wait_ge(out_ready, n + 1)
                dve.wait_ge(rows_ready, n + 1)
                wait(dve, stored[k], 16 * turns(n, k, B))
                nc.vector.tensor_tensor(xo[:, k, :], ps_w[:].rearrange("p i a -> p (i a)")[:, D:2 * D], xr[:, k, :], ALU.add).then_inc(added, 1)

            walk(dve, GROUPS, B, B, [(0, statistics), (0, aggregate), (L_OUT, divide), (L_S, weigh(0)), (L_S, weigh(1)), (L_BIAS, add_bias),
                                     (L_NORM, normalise), (L_S, weigh(2)), (L_PHI, features), (L_BD, block_queries), (L_S, weigh(3)),
                                     (L_OUT, add), (L_NEG, negative_part)])

        @block.scalar
        def _(act):
            def evacuate_x(n, k):
                act.wait_ge(x_turned, n + 1)
                wait(act, vf_ready, n - B + 1)
                nc.scalar.activation(xnT[:, k], ps_xl[:, 0, :].rearrange("p (c t) -> p c t", c=2), ACT.Copy).then_inc(xnT_done, 1)

            def exponentials(n, k):
                act.wait_ge(neg_done, n + 1)
                nc.scalar.activation(e_qk[:, k % 2, :], e_qk[:, k % 2, :], ACT.Exp).then_inc(exp_done, 1)
                act.wait_ge(abs_done, n + 1)
                nc.scalar.activation(abs_f[:, k, :], abs_f[:, k, :], ACT.Exp).then_inc(f_exp_done, 1)
                act.wait_ge(f_exp_done, n + 1)
                nc.scalar.activation(abs_f[:, k, :], abs_f[:, k, :], ACT.Ln, bias=1.0).then_inc(f_log_done, 1)

            def copy_keys(n, k):
                act.wait_ge(qk_turned, n + 1)
                wait(act, s_ready, 4 * (n - 3))
                nc.scalar.activation(kT[:, k % 4], ps_t[:, 2:4, :], ACT.Copy).then_inc(kT_done, 1)

            def decays(n, k):
                act.wait_ge(sums_ready, n + 1)
                wait(act, spread_done, n - 1)
                nc.scalar.activation(decay[:, k % 2].rearrange("p h t -> p (h t)"), ps_xl[:, 1, :], ACT.Exp).then_inc(decay_done, 1)

            def copy_output(n, k):
                act.wait_ge(o_ready, n + 1)
                wait(act, o_turned, n - 1)
                nc.scalar.activation(o_sb[:, k % 2, :], ps_o[:].rearrange("p i a -> p (i a)"), ACT.Copy).then_inc(o_copied, 1)

            def copy_att(n, k):
                act.wait_ge(att_turned, n + 1)
                wait(act, out_ready, n - 1)
                nc.scalar.activation(attT[:, k % 2], ps_w[:, 0:2, :], ACT.Copy).then_inc(attT_done, 1)

            walk(act, GROUPS, B, B, [(L_BD, copy_keys), (L_EXP, exponentials), (L_TURN, evacuate_x), (L_OUT, copy_att), (L_PV, copy_output),
                                     (L_DECAY, decays)])

        @block.tensor
        def _(pe):
            for i in range(5):
                wait(pe, w_copied, i - 1)
                bank = (ps_t, ps_w)[i % 2]
                for c in range(2):
                    if i < 4:
                        for r in range(2):
                            last = nc.tensor.transpose(bank[:, 2 * c + r, :], w_rows[:, 2 * i + r, c * P:(c + 1) * P], ident[:])
                    else:
                        last = nc.tensor.transpose(bank[:, c, 0:H], f_rows[:, c * P:(c + 1) * P], ident[0:H, 0:H])
                last.then_inc(w_turned, 1)
            pe.wait_ge(w_copied, 5)

            def turn_x(n, k):
                pe.wait_ge(xn_done, n + 1)
                wait(pe, xnT_done, n)
                wait(pe, decay_done, n + L_TURN - L_LSUM)
                for c in range(2):
                    last = nc.tensor.transpose(ps_xl[:, 0, c * P:(c + 1) * P], xn[:, k, c * P:(c + 1) * P], ident[:])
                last.then_inc(x_turned, 1)

            def project(n, k):
                pe.wait_ge(xnT_done, n + 1)
                wait(pe, qk_biased, n)
                for c in range(2):
                    last = nc.tensor.matmul(ps_qk[:], xnT[:, k, c, :], w_qk[:, c, :], start=c == 0, stop=c == 1)
                last.then_inc(qk_ready, 1)
                wait(pe, f_biased, n)
                wait(pe, v_biased, n)
                for c in range(2):
                    last = nc.tensor.matmul(ps_vf[:], xnT[:, k, c, :], w_vf[:, c, :], start=c == 0, stop=c == 1)
                last.then_inc(vf_ready, 1)

            def turn_qk(n, k):
                pe.wait_ge(phi_done, n + 1)
                wait(pe, bd_done, n)
                wait(pe, kT_done, n)
                for g in range(4):
                    last = nc.tensor.transpose(ps_t[:, g, :], phi[:, k % 2, g * P:(g + 1) * P], ident[:])
                last.then_inc(qk_turned, 1)

            def sum_logs(n, k):
                pe.wait_ge(upto_done, n + 1)
                seen = n + L_LSUM - L_TURN + 1
                pe.wait_ge(xnT_done, min(seen, GROUPS) if isinstance(seen, int) else seen)
                nc.tensor.matmul(ps_xl[:, 1, :], later[:], log_upto[:, k % 2].rearrange("p h t -> p (h t)"), start=True, stop=True).then_inc(sums_ready, 1)

            def scores(i):
                def stage(n, k):
                    if i == 0:
                        pe.wait_ge(bd_done, n + 1)
                        pe.wait_ge(kT_done, n + 1)
                    wait(pe, weight_done, 4 * n + i - 1)
                    half, quarter = i // 2, i % 2
                    nc.tensor.matmul(ps_s[i % 2][:], kT[:, k % 4, half, :], q_bd[:, k % 2, half, 4 * quarter:4 * quarter + 4, :],
                                     start=True, stop=True).then_inc(s_ready, 1)
                return stage

            def mix_values(n, k):
                pe.wait_ge(weight_done, 4 * n + 4)
                wait(pe, o_copied, n)
                for i in range(4):
                    for j in range(4):
                        h = 4 * i + j
                        last = nc.tensor.matmul(ps_o[VW * j:VW * (j + 1), i, :], v_aug[:, k, h, :], weight[:, k % 2, h, :], start=True, stop=True)
                last.then_inc(o_ready, 1)

            def turn_output(n, k):
                pe.wait_ge(o_copied, n + 1)
                wait(pe, added, n)
                for i in range(4):
                    last = nc.tensor.transpose(ps_w[:, i, :], o_sb[:, k % 2, i * P:(i + 1) * P], ident[:])
                last.then_inc(o_turned, 1)

            def turn_att(n, k):
                pe.wait_ge(att_done, n + 1)
                for c in range(2):
                    last = nc.tensor.transpose(ps_w[:, c, :], att[:, k % 2, c * P:(c + 1) * P], ident[:])
                last.then_inc(att_turned, 1)

            def project_out(n, k):
                pe.wait_ge(attT_done, n + 1)
                out = ps_w[:].rearrange("p i a -> p (i a)")[:, D:2 * D]
                for c in range(2):
                    last = nc.tensor.matmul(out, attT[:, k % 2, c, :], w_o[:, c, :], start=c == 0, stop=c == 1)
                last.then_inc(out_ready, 1)

            walk(pe, GROUPS, B, B, [(L_OUT, turn_output), (L_S, scores(0)), (L_S, scores(1)), (L_TURN, turn_x), (L_OUT, turn_att),
                                    (L_S, scores(2)), (L_PV, mix_values), (L_LSUM, sum_logs), (L_OUT, project_out), (L_S, scores(3)),
                                    (L_PROJ, project), (L_QK, turn_qk)])


def held_constants(nc, ctx, a):
    from concourse import mybir
    fp32 = mybir.dt.float32
    P, D, E, SF, STEPS = 128, 256, 64, 192, 16
    held, ahead = {}, []

    def hold(name, shape):
        held[name] = ctx.enter_context(nc.sbuf_tensor("held_" + name, shape, fp32))
        return held[name]

    def rows(w):
        return w.rearrange("(c p) d -> p c d", p=P)

    hold("ident_sb", [P, P])
    ahead.append((hold("wo_rows", [P, 2, D])[:], rows(a["L0_attn_a_Wo"])))
    ahead.append((hold("rw_rows", [E, D])[:], a["L0_ffn_router_w"]))
    gate_up = hold("ws_gate_up_sb", [P, 2, 3, P])
    source = a["L0_ffn_ws_gate_up"].rearrange("(c p) (h f) -> p c h f", p=P, h=2)
    for h in range(2):
        rest = SF - P
        ahead.append((gate_up[:, :, h, :], source[:, :, h, 0:P]))
        ahead.append((gate_up[:, :, 2, h * rest:(h + 1) * rest], source[:, :, h, P:SF]))
    down = hold("ws_down_sb", [P, 2, D])
    ahead.append((down[:, 0, :], a["L0_ffn_ws_down"][0:P, :]))
    ahead.append((down[0:SF - P, 1, :], a["L0_ffn_ws_down"][P:SF, :]))
    w_rows = hold("b_w_rows", [P, 8, D])
    for i, m in enumerate("qkvo"):
        ahead.append((w_rows[:, 2 * i:2 * i + 2, :], rows(a["L0_attn_b_W" + m])))
    ahead.append((hold("b_f_rows", [STEPS, D])[:], a["L0_attn_b_Wf"]))
    for name, parts in (("b_qk", "qk"), ("b_vf", "vf"), ("b_o", "o")):
        tile, at = hold(name, [P, sum(a["L0_attn_b_b" + m].shape[0] for m in parts)]), 0
        for m in parts:
            bias = a["L0_attn_b_b" + m]
            n = bias.shape[0]
            ahead.append((tile[:, at:at + n], bias.rearrange("(o n) -> o n", o=1).to_broadcast([P, n])))
            at += n
    for name in ("rank_value", "spare_row", "reverse", "later", "upto", "own", "head_rows"):
        ahead.append((hold(name + "_sb", list(a[name].shape))[:], a[name]))
    return held, ahead


def program(nc, a):
    from concourse import mybir
    from contextlib import ExitStack
    fp32, bf16, u32 = mybir.dt.float32, mybir.dt.bfloat16, mybir.dt.uint32
    P, D, T, E, SEQS, S = 128, 256, 8192, 64, 16, 512
    SPARE = P

    def scratch(name, shape, dt=fp32):
        return nc.dram_tensor(name, shape, dt).ap()

    split = {"parts": scratch("parts", (SEQS, 12, P, S), bf16), "v": scratch("v", (T, D))}
    routed = {"rows": scratch("rows", (T + SPARE, D + E))}
    x0 = a["L0_attn_a_x"].rearrange("b s d -> (b s) d")
    x1, x3 = scratch("x1", (T, D)), scratch("x3", (T, D))
    x2 = scratch("x2", (T + SPARE, D))

    def mixture(tag, x_in, x_out):
        with nc.sbuf_tensor(tag + "_slots", [P, E], u32) as slots:
            with (nc.sbuf_tensor(tag + "_order", [P, T // 2], fp32) as order,
                  nc.sbuf_tensor(tag + "_x_rows", [P, T // P, D], fp32) as x_rows,
                  nc.sbuf_tensor(tag + "_x_turned", [P, D // P, T], fp32) as x_turned):
                const = dict(held, order=order, x_rows=x_rows, x_turned=x_turned, slots=slots)
                with nc.cleanup_on_exit():
                    moe_route(nc, tag, routed, x_in, const)
                with nc.cleanup_on_exit():
                    moe_shared(nc, tag, x_out, const)
            with nc.cleanup_on_exit():
                moe_experts(nc, tag, routed, x_out, a["L0_ffn_w_gate"], a["L0_ffn_w_up"], a["L0_ffn_w_down"], dict(held, slots=slots))

    with ExitStack() as ctx:
        held, ahead = held_constants(nc, ctx, a)
        with nc.cleanup_on_exit():
            attention_project(nc, split, x0, a["L0_attn_a_Wq"], a["L0_attn_a_Wk"], a["L0_attn_a_Wv"], dict(a, **held), ahead)
        with nc.cleanup_on_exit():
            attention_mix(nc, split, x0, x1, held)
        mixture("m1", x1, x2)
        with nc.cleanup_on_exit():
            forget_attention(nc, x2[0:T, :], x3, held)
        mixture("m2", x3, a["out"])


_INS = ["L0_attn_a_x", "L0_attn_a_Wq", "L0_attn_a_Wk", "L0_attn_a_Wv", "L0_attn_a_Wo", "L0_attn_b_Wq", "L0_attn_b_bq", "L0_attn_b_Wk",
        "L0_attn_b_bk", "L0_attn_b_Wv", "L0_attn_b_bv", "L0_attn_b_Wf", "L0_attn_b_bf", "L0_attn_b_Wo", "L0_attn_b_bo",
        "L0_ffn_router_w", "L0_ffn_w_gate", "L0_ffn_w_up", "L0_ffn_w_down", "L0_ffn_ws_gate_up", "L0_ffn_ws_down"]


def constants():
    P, S, DK, T = 128, 512, 16, 8192
    p = np.arange(P)
    angle = np.arange(S, dtype=np.float32)[:, None] * (1.0 / 10000.0 ** (np.arange(0, DK, 2, dtype=np.float32) / DK)).astype(np.float32)
    by_tile = lambda t: t.reshape(S // P, P, DK).transpose(1, 0, 2)
    item = np.arange(T // P)
    tile = item % 2 * (T // P // 2) + item // 2
    step, col = p // 8, p % 8
    tables = {
        "ident": np.eye(P),
        "reverse": np.eye(P)[::-1],
        "cos": by_tile(np.concatenate([np.cos(angle), np.cos(angle)], 1)),
        "sin": by_tile(np.concatenate([-np.sin(angle), np.sin(angle)], 1)),
        "rank_value": T - (tile[None, :] * P + p[:, None]),
        "spare_row": p[:, None],
        "later": (col[:, None] == col) & (step[:, None] > step),
        "upto": step[:, None] <= np.arange(16),
        "own": (col[:, None] == col) & (step[:, None] <= step),
        "head_rows": p[:, None] // DK == np.arange(P // DK),
    }
    return {name: np.ascontiguousarray(t, dtype=np.float32) for name, t in tables.items()}


def kernel(**inputs):
    import concourse.bacc as _bacc
    from concourse import mybir as _mybir
    from concourse.bass_utils import run_bass_kernel_spmd as _run

    nc = _bacc.Bacc("TRN2", target_bir_lowering=False, num_devices=1)
    data = {name: np.ascontiguousarray(inputs[name]) for name in _INS}
    data.update(constants())
    arrays, a = {}, {}
    for name, t in data.items():
        arrays[f"in_{name}_dram"] = t
        a[name] = nc.dram_tensor(f"in_{name}_dram", t.shape, _mybir.dt.from_np(t.dtype), kind="ExternalInput").ap()
    tokens, features = 16 * 512, 256
    a["out"] = nc.dram_tensor("out_0_dram", (tokens + 128, features), _mybir.dt.float32, kind="ExternalOutput").ap()
    program(nc, a)
    r = _run(nc, [arrays], core_ids=[0])
    return r.results[0]["out_0_dram"][:tokens].reshape(16, 512, features)
```
